# Optimizing a Trainium2 kernel written in Bass

```python
import numpy as np
import jax
import jax.numpy as jnp

def _softmax(x, axis=-1):
    return jax.nn.softmax(x, axis=axis)

def _gelu(x):
    return jax.nn.gelu(x, approximate=True)

def _silu(x):
    return jax.nn.silu(x)

def _sigmoid(x):
    return jax.nn.sigmoid(x)

def _layernorm(x, axis=-1, eps=1e-05):
    m = jnp.mean(x, axis=axis, keepdims=True)
    v = jnp.var(x, axis=axis, keepdims=True)
    return (x - m) / jnp.sqrt(v + eps)

def _scatter_add(tgt, idx, src, axis=0):
    return tgt.at[idx].add(src)

def _segment_sum(src, seg, n):
    return jax.ops.segment_sum(src, seg, n)
kernel_name = 'mk_prb_d2_jaxref_r8_061927'

def setup_inputs(seed: int=0):
    np.random.seed(seed)
    _w = jnp.asarray

    def _L0_attn_setup():
        import jax, jax.numpy as jnp
        import numpy as np
        B, S, D = (4, 256, 128)
        H = 16
        HS = D // H
        SCALE = HS ** 0.5
        key = jax.random.key(seed)
        ks = jax.random.split(key, 9)
        std = 1.0 / np.sqrt(D)

        def lin(kw, kb, fan_in, fan_out):
            w = jax.random.uniform(kw, (fan_in, fan_out), minval=-std, maxval=std, dtype=jnp.float32)
            b = jax.random.uniform(kb, (fan_out,), minval=-std, maxval=std, dtype=jnp.float32)
            return (w, b)
        Wq, bq = lin(ks[0], ks[1], D, D)
        Wk, bk = lin(ks[2], ks[3], D, D)
        Wv, bv = lin(ks[4], ks[5], D, D)
        Wm, bm = lin(ks[6], ks[7], D, D)
        x = jax.random.normal(ks[8], (B, S, D), dtype=jnp.float32)
        return {'x': x, 'Wq': Wq, 'bq': bq, 'Wk': Wk, 'bk': bk, 'Wv': Wv, 'bv': bv, 'Wm': Wm, 'bm': bm}
    _L0_attn_in = _L0_attn_setup()

    def _L0_ffn_setup():
        import jax, jax.numpy as jnp
        import numpy as np
        B, S, D = (2, 256, 128)
        E, K, F = (16, 2, 64)
        FS = 128
        key = jax.random.key(seed)
        ks = jax.random.split(key, 8)

        def w(k, shape, fan_in):
            return jax.random.normal(k, shape, jnp.float32) / np.sqrt(fan_in).astype(np.float32)
        return {'x': jax.random.normal(ks[0], (B, S, D), jnp.float32), 'Wr': w(ks[1], (D, E), D), 'Wg': w(ks[2], (E, D, F), D), 'Wu': w(ks[3], (E, D, F), D), 'Wd': w(ks[4], (E, F, D), F), 'Sg': w(ks[5], (D, FS), D), 'Su': w(ks[6], (D, FS), D), 'Sd': w(ks[7], (FS, D), FS)}
    _L0_ffn_in = _L0_ffn_setup()

    def _L1_attn_setup():
        import jax, jax.numpy as jnp
        import numpy as np
        B, S, HID, NH = (8, 512, 128, 16)
        D = HID // NH
        LN_EPS = 1e-05

        def _l2norm(a):
            n = jnp.sqrt(jnp.sum(a * a, axis=-1, keepdims=True))
            return a / jnp.maximum(n, 1e-12)
        key = jax.random.key(seed)
        ks = jax.random.split(key, 8)
        s = 0.02
        x = jax.random.normal(ks[0], (B, S, HID), jnp.float32)
        Wq = jax.random.normal(ks[1], (HID, NH * D), jnp.float32) * s
        Wk = jax.random.normal(ks[2], (HID, NH * D), jnp.float32) * s
        Wv = jax.random.normal(ks[3], (HID, NH * D), jnp.float32) * s
        Wbeta = jax.random.normal(ks[4], (HID, NH), jnp.float32) * s
        Wg = jax.random.normal(ks[5], (HID, NH * D), jnp.float32) * s
        Wout = jax.random.normal(ks[6], (NH * D, HID), jnp.float32) * s
        ln_g = jnp.ones((NH * D,), jnp.float32)
        ln_b = jnp.zeros((NH * D,), jnp.float32)
        return {'x': x, 'Wq': Wq, 'Wk': Wk, 'Wv': Wv, 'Wbeta': Wbeta, 'Wg': Wg, 'Wout': Wout, 'ln_g': ln_g, 'ln_b': ln_b}
    _L1_attn_in = _L1_attn_setup()

    def _L1_ffn_setup():
        import jax, jax.numpy as jnp
        import numpy as np
        B, S, D = (2, 256, 128)
        E, H, K = (8, 704, 2)
        N_RESERVED = 4
        key = jax.random.key(seed)
        ks = jax.random.split(key, 5)
        scale = 0.02
        x = jax.random.normal(ks[0], (B, S, D), dtype=jnp.float32)
        gate_w = jax.random.normal(ks[1], (E, D), dtype=jnp.float32) * scale
        w1 = jax.random.normal(ks[2], (E, D, H), dtype=jnp.float32) * scale
        w3 = jax.random.normal(ks[3], (E, D, H), dtype=jnp.float32) * scale
        w2 = jax.random.normal(ks[4], (E, H, D), dtype=jnp.float32) * scale
        return {'x': x, 'gate_w': gate_w, 'w1': w1, 'w2': w2, 'w3': w3}
    _L1_ffn_in = _L1_ffn_setup()
    _d = {'L0_attn_x': _L0_attn_in['x'], 'L0_attn_Wq': _L0_attn_in['Wq'], 'L0_attn_bq': _L0_attn_in['bq'], 'L0_attn_Wk': _L0_attn_in['Wk'], 'L0_attn_bk': _L0_attn_in['bk'], 'L0_attn_Wv': _L0_attn_in['Wv'], 'L0_attn_bv': _L0_attn_in['bv'], 'L0_attn_Wm': _L0_attn_in['Wm'], 'L0_attn_bm': _L0_attn_in['bm'], 'L0_ffn_Wr': _L0_ffn_in['Wr'], 'L0_ffn_Wg': _L0_ffn_in['Wg'], 'L0_ffn_Wu': _L0_ffn_in['Wu'], 'L0_ffn_Wd': _L0_ffn_in['Wd'], 'L0_ffn_Sg': _L0_ffn_in['Sg'], 'L0_ffn_Su': _L0_ffn_in['Su'], 'L0_ffn_Sd': _L0_ffn_in['Sd'], 'L1_attn_Wq': _L1_attn_in['Wq'], 'L1_attn_Wk': _L1_attn_in['Wk'], 'L1_attn_Wv': _L1_attn_in['Wv'], 'L1_attn_Wbeta': _L1_attn_in['Wbeta'], 'L1_attn_Wg': _L1_attn_in['Wg'], 'L1_attn_Wout': _L1_attn_in['Wout'], 'L1_attn_ln_g': _L1_attn_in['ln_g'], 'L1_attn_ln_b': _L1_attn_in['ln_b'], 'L1_ffn_gate_w': _L1_ffn_in['gate_w'], 'L1_ffn_w1': _L1_ffn_in['w1'], 'L1_ffn_w2': _L1_ffn_in['w2'], 'L1_ffn_w3': _L1_ffn_in['w3']}
    _x0 = _d['L0_attn_x']
    _d['L0_attn_x'] = jax.random.normal(jax.random.fold_in(jax.random.key(seed), 1), (32, 256, 128), dtype=_x0.dtype)
    del _x0
    return _d

def reference(L0_attn_x, L0_attn_Wq, L0_attn_bq, L0_attn_Wk, L0_attn_bk, L0_attn_Wv, L0_attn_bv, L0_attn_Wm, L0_attn_bm, L0_ffn_Wr, L0_ffn_Wg, L0_ffn_Wu, L0_ffn_Wd, L0_ffn_Sg, L0_ffn_Su, L0_ffn_Sd, L1_attn_Wq, L1_attn_Wk, L1_attn_Wv, L1_attn_Wbeta, L1_attn_Wg, L1_attn_Wout, L1_attn_ln_g, L1_attn_ln_b, L1_ffn_gate_w, L1_ffn_w1, L1_ffn_w2, L1_ffn_w3):

    def _L0_attn_ref(x, Wq, bq, Wk, bk, Wv, bv, Wm, bm):
        import jax, jax.numpy as jnp
        import numpy as np
        B, S, D = (4, 256, 128)
        H = 16
        HS = D // H
        SCALE = HS ** 0.5
        bs, seq, _ = x.shape

        def heads(w, b):
            return (x @ w + b).reshape(bs, seq, H, HS).transpose(0, 2, 1, 3)
        q = heads(Wq, bq)
        k = heads(Wk, bk)
        v = heads(Wv, bv)
        scores = jnp.einsum('bhqd,bhkd->bhqk', q, k) / SCALE
        causal_mask = jnp.arange(seq)[None, :] > jnp.arange(seq)[:, None]
        scores = jnp.where(causal_mask, jnp.float32(-1000000000000.0), scores)
        probs = jax.nn.softmax(scores, axis=-1)
        attn = jnp.einsum('bhqk,bhkd->bhqd', probs, v)
        attn = attn.transpose(0, 2, 1, 3).reshape(bs, seq, H * HS)
        return attn @ Wm + bm

    def _L0_ffn_ref(x, Wr, Wg, Wu, Wd, Sg, Su, Sd):
        import jax, jax.numpy as jnp
        import numpy as np
        B, S, D = (2, 256, 128)
        E, K, F = (16, 2, 64)
        FS = 128
        b, s, d = x.shape
        T = b * s
        xf = x.reshape(T, d)
        shared = jax.nn.silu(xf @ Sg) * (xf @ Su) @ Sd
        probs = jax.nn.softmax(xf @ Wr, axis=-1)
        topk_p, topk_i = jax.lax.top_k(probs, K)
        n_exp = Wr.shape[1]
        cw = jnp.zeros((T, n_exp), x.dtype).at[jnp.arange(T)[:, None], topk_i].add(topk_p)

        def step(acc, ew):
            wg, wu, wd, c = ew
            y = jax.nn.silu(xf @ wg) * (xf @ wu) @ wd
            return (acc + y * c[:, None], None)
        routed, _ = jax.lax.scan(step, jnp.zeros_like(xf), (Wg, Wu, Wd, cw.T))
        return (routed + shared).reshape(b, s, d)

    def _L1_attn_ref(x, Wq, Wk, Wv, Wbeta, Wg, Wout, ln_g, ln_b):
        import jax, jax.numpy as jnp
        import numpy as np
        B, S, HID, NH = (8, 512, 128, 16)
        D = HID // NH
        LN_EPS = 1e-05

        def _l2norm(a):
            n = jnp.sqrt(jnp.sum(a * a, axis=-1, keepdims=True))
            return a / jnp.maximum(n, 1e-12)
        b, s, _ = x.shape
        nh = Wbeta.shape[1]
        d = Wq.shape[1] // nh
        q = _l2norm((x @ Wq).reshape(b, s, nh, d))
        k = _l2norm((x @ Wk).reshape(b, s, nh, d))
        v = (x @ Wv).reshape(b, s, nh, d)
        beta = jax.nn.sigmoid(x @ Wbeta)
        qT = jnp.moveaxis(q, 1, 0)
        kT = jnp.moveaxis(k, 1, 0)
        vT = jnp.moveaxis(v, 1, 0)
        bT = jnp.moveaxis(beta, 1, 0)
        state0 = jnp.zeros((b, nh, d, d), x.dtype)

        def step(state, inp):
            qt, kt, vt, bt = inp
            kk = kt[..., :, None] * kt[..., None, :]
            bb = bt[..., None, None]
            state = state * (1.0 - bb * kk) + bb * (vt[..., :, None] * kt[..., None, :])
            out_t = jnp.einsum('bhij,bhj->bhi', state, qt)
            return (state, out_t)
        _, outs = jax.lax.scan(step, state0, (qT, kT, vT, bT))
        out = jnp.moveaxis(outs, 0, 1).reshape(b, s, nh * d)
        mu = jnp.mean(out, axis=-1, keepdims=True)
        var = jnp.mean((out - mu) ** 2, axis=-1, keepdims=True)
        out = (out - mu) / jnp.sqrt(var + LN_EPS) * ln_g + ln_b
        out = out * jax.nn.silu(x @ Wg)
        return out @ Wout

    def _L1_ffn_ref(x, gate_w, w1, w2, w3):
        import jax, jax.numpy as jnp
        import numpy as np
        B, S, D = (2, 256, 128)
        E, H, K = (8, 704, 2)
        N_RESERVED = 4
        b, s, d = x.shape
        T = b * s
        xf = x.reshape(T, d)
        logits = xf @ gate_w.T
        expert_ids = jnp.arange(E)
        logits = jnp.where(expert_ids[None, :] >= E - N_RESERVED, -jnp.inf, logits)
        weights = jax.nn.softmax(logits, axis=-1)
        top_w, top_idx = jax.lax.top_k(weights, K)
        top_w = top_w / jnp.sum(top_w, axis=-1, keepdims=True)
        cw = jnp.zeros((T, E), dtype=x.dtype).at[jnp.arange(T)[:, None], top_idx].add(top_w)
        h = jax.nn.silu(jnp.einsum('td,edh->teh', xf, w1)) * jnp.einsum('td,edh->teh', xf, w3)
        y = jnp.einsum('teh,ehd->ted', h, w2)
        out = jnp.einsum('te,ted->td', cw, y)
        return out.reshape(b, s, d)
    x = L0_attn_x
    xn = _layernorm(x, axis=-1)
    x = x + _L0_attn_ref(xn, L0_attn_Wq, L0_attn_bq, L0_attn_Wk, L0_attn_bk, L0_attn_Wv, L0_attn_bv, L0_attn_Wm, L0_attn_bm) + _L0_ffn_ref(xn, L0_ffn_Wr, L0_ffn_Wg, L0_ffn_Wu, L0_ffn_Wd, L0_ffn_Sg, L0_ffn_Su, L0_ffn_Sd)
    xn = _layernorm(x, axis=-1)
    x = x + _L1_attn_ref(xn, L1_attn_Wq, L1_attn_Wk, L1_attn_Wv, L1_attn_Wbeta, L1_attn_Wg, L1_attn_Wout, L1_attn_ln_g, L1_attn_ln_b) + _L1_ffn_ref(xn, L1_ffn_gate_w, L1_ffn_w1, L1_ffn_w2, L1_ffn_w3)
    return x

_drawn_inputs = setup_inputs


def setup_inputs(seed=0):
    import zlib

    import numpy as np

    out = dict(_drawn_inputs(seed))
    spreads = {'L1_attn_ln_g': (1.0, 0.6), 'L1_attn_ln_b': (0.0, 2.0)}
    factors = {'L0_attn_Wq': 3.735,
     'L0_attn_bq': 8.0,
     'L0_attn_Wk': 3.713,
     'L0_attn_bk': 64.0,
     'L1_attn_Wbeta': 64.0,
     'L1_ffn_gate_w': 8.0,
     'L1_ffn_w1': 6.863,
     'L1_ffn_w2': 6.835,
     'L1_ffn_w3': 6.832,
     'L1_attn_Wq': 8.0,
     'L1_attn_Wk': 8.0,
     'L1_attn_Wv': 8.0,
     'L1_attn_Wg': 7.223,
     'L1_attn_Wout': 7.135}
    for name, (base, spread) in spreads.items():
        noise = np.random.default_rng([zlib.crc32(name.encode()), seed]).standard_normal(out[name].shape)
        drawn = base * np.exp(spread * noise) if base else spread * noise
        out[name] = jnp.asarray(drawn.astype(out[name].dtype))
    for name, factor in factors.items():
        out[name] = (out[name] * factor).astype(out[name].dtype)
    return out
```

```python
from contextlib import ExitStack

import concourse.bass as bass
from concourse import mybir

ALU = mybir.AluOpType
ACT = mybir.ActivationFunctionType
AX = mybir.AxisListType
F32 = mybir.dt.float32
F32R = mybir.dt.float32r
BF16 = mybir.dt.bfloat16

P = 128
C = 512
S = 256
TILES = C // P
H = 16
HD = 8
H2 = H // 2
E0, F0 = 16, 64
E1, F1 = 4, 704
LN_EPS = 1e-5
SCORE_SCALE = float(HD) ** -0.5
MASKED = -1e30

NF0 = E0 * F0 // P + 1
NF1 = E1 * F1 // P
NPAIR = 2 * H2

W0_Q, W0_K, W0_V, W0_M, W0_SG, W0_SU, W0_G = (P * n for n in range(7))
W0_U = W0_G + E0 * F0
W0_R = W0_U + E0 * F0
W0_COLS = W0_R + E0
W1_Q, W1_K, W1_V, W1_G, W1_O, W1_1 = (P * n for n in range(6))
W1_3 = W1_1 + E1 * F1
W1_R = W1_3 + E1 * F1
R1 = H + E1
W1_COLS = W1_R + R1
STAGE = 1024

SLOTS = [(0, 0), (1, 0), (2, 0), (0, 1), (1, 1), (0, 2)]
QK_ROWS = HD * len(SLOTS)
ST_ROWS = QK_ROWS + 3

OWNERS = []
for _c in range(NF1):
    _lo, _hi = _c * P, (_c + 1) * P
    OWNERS.append([(e, max(_lo, e * F1) - _lo, min(_hi, (e + 1) * F1) - _lo)
                   for e in range(E1) if max(_lo, e * F1) < min(_hi, (e + 1) * F1)])
LAST_OF = [max(c for c in range(NF1) if any(o[0] == e for o in OWNERS[c])) for e in range(E1)]
FIRST_OF = [min(c for c in range(NF1) if any(o[0] == e for o in OWNERS[c])) for e in range(E1)]

MAX_AT = {2: (0, 3), 3: (3, 6), 4: (6, 9), 5: (9, 12), 6: (12, 14), 7: (14, 16)}
J_AT = {3 + 2 * j: j for j in range(HD)}


class Signal:

    def __init__(self, sem, per, unit=1, ahead=0):
        self.sem, self.per, self.unit, self.ahead = sem, per, unit, ahead

    def __call__(self, i, k=None):
        k = self.per if k is None else k
        return self.sem, i * (self.per * self.unit) + (k + self.ahead) * self.unit


class Banks:

    def __init__(self, tile, full, free, uses):
        self.tile, self.full, self.free = tile, full, free
        self.order, self.parts, n = {}, {}, 0
        for k, (name, parts) in enumerate(uses):
            self.order[name], self.parts[name] = k, (n, parts)
            n += parts
        self.uses, self.fills = len(uses), n

    def empty(self, i, name):
        return self.free, i * self.uses + self.order[name] + 1

    def filled(self, i, name, part=None):
        first, parts = self.parts[name]
        return self.full, i * self.fills + first + (parts if part is None else part)

    def released(self, i, name):
        return self.free, i * self.uses + self.order[name] + 2


def two_layer_kernel(nc, x, Wq0, bq0, Wk0, bk0, Wv0, bv0, Wm0, bm0, Wr0, Wg0, Wu0, Wd0, Sg0, Su0, Sd0,
                     Wq1, Wk1, Wv1, Wbeta1, Wgate1, Wout1, ln_g1, ln_b1, gate_w1, w1, w2, w3, out):
    tokens = x.shape[0] * x.shape[1]
    NCH = tokens // C
    x_chunks = x.rearrange("b s d -> (b s) d").rearrange("(n t p) d -> n p t d", t=TILES, p=P)
    out_chunks = out.rearrange("b s d -> (b s) d").rearrange("(n t p) d -> n p t d", t=TILES, p=P)
    max_dram = nc.dram_tensor("max_dram", (6 * H2, C), BF16).ap()
    qk_dram = nc.dram_tensor("qk_dram", (2, 3, P, C), BF16).ap()

    ctx = ExitStack()
    with ctx:
        def sb(name, shape, dt=F32):
            return ctx.enter_context(nc.sbuf_tensor(name, shape, dt))

        def sem(name):
            return ctx.enter_context(nc.semaphore(name))

        def signal(name, per, unit=1, ahead=0):
            return Signal(sem(name), per, unit, ahead)

        w0h, w0l = sb("w0h", [P, W0_COLS], F32R), sb("w0l", [P, W0_COLS], F32R)
        w1h, w1l = sb("w1h", [P, W1_COLS], F32R), sb("w1l", [P, W1_COLS], F32R)
        wd0 = sb("wd0", [P, NF0, P])
        wd1 = sb("wd1", [P, NF1, P])
        bias0 = sb("bias0", [P, 3])
        bm_rows = sb("bm_rows", [P, P])
        ln1 = sb("ln1", [P, 2])
        ident = sb("ident", [P, P])
        ident_b = sb("ident_b", [P, P], BF16)
        causal = sb("causal", [P, 2, P], BF16)
        same_head = sb("same_head", [P, P])
        pick = sb("pick", [P, HD, P], F32R)
        head_of = sb("head_of", [P, H])
        part_row = sb("part_row", [2 * H, H])
        pick_e = sb("pick_e", [2 * H + 2 * E1, NF0 - 1, P], F32R)
        pick_e0, pick_e1 = pick_e[0:2 * H, :, :], pick_e[2 * H:, 0:E1, :]
        pick_h = sb("pick_h", [2 * H, P], F32R)
        mhalf = sb("mhalf", [P, TILES])

        xin = sb("xin", [P, TILES, P])
        xb = sb("xb", [P, TILES, P])
        x1 = sb("x1", [P, TILES, P])
        x2 = xb
        xn = sb("xn", [P, TILES, P])
        xh, xl = sb("xh", [P, C], F32R), sb("xl", [P, C], F32R)
        stat = sb("stat", [P, TILES, 6])
        mv = sb("mv", [P, TILES, 2])
        veps = sb("veps", [P, TILES])
        rstd = sb("rstd", [P, TILES])
        qk_parts = sb("qk_parts_sb", [P, 2, 3, C], BF16)
        sq = sb("sq", [P, 2, C])
        qk_rest = sq
        Q = sb("Q", [P, H2, C], BF16)
        K = sb("K", [P, H2, C], BF16)
        V = sb("V", [P, TILES, H, HD + 1])
        row_max = sb("row_max", [P, 2, H2, 2, 3])
        neg_max = sb("neg_max", [P, TILES, 2, H2])
        max_rest = sb("max_rest", [P, TILES, 2, H2])
        max_parts = sb("max_parts", [P, TILES, 2, 3, H2], BF16)
        max_rows = sb("max_rows", [6 * H2, C], BF16)
        probs = sb("probs", [P, 3, 2, 3 * P])
        rden = sb("rden", [P, 2, 2, H])
        attn = sb("attn", [P, TILES, P])
        ah, al = sb("ah", [P, C], F32R), sb("al", [P, C], F32R)
        top_max = sb("top_max", [P, TILES])
        shifted = sb("shifted", [P, TILES, E0])
        ex0 = sb("ex0", [P, TILES, E0 + 8])
        ex1 = sb("ex1", [P, TILES, E1 + 8])
        rest0 = sb("rest0", [P, TILES, E0 + 6])
        rest1 = sb("rest1", [P, TILES, E1 + 6])
        top8 = sb("top8", [P, TILES, 8])
        ex_sum = sb("ex_sum", [P, TILES])
        cw = sb("cw", [P, TILES, E0])
        narrow = sb("narrow", [P, TILES, 2 * H + 2 * E1], F32R)
        rows = sb("rows", [2 * H + 2 * E1, C], F32R)
        eb = sb("eb", [P, TILES, H])
        beta = sb("beta", [P, TILES, H])
        gated = sb("gated", [P, 3, C])
        ug = sq
        hid = sb("hid", [P, 3, C])
        y0 = sb("y0", [P, C])
        kq = sb("kq", [P, 2, C])
        rs = kq
        kqh, kql = sb("kqh", [P, 2, C], F32R), sb("kql", [P, 2, C], F32R)
        nbk = sb("nbk", [P, C])
        bv = sb("bv", [P, C])
        beta_f = bv
        gate = sb("gate", [P, C])
        cw1 = sb("cw1", [P, E1, C])
        stage = cw1[:, :, :].rearrange("p (n a) c -> p n (a c)", n=2)
        scratch = probs[:, :, :, :].rearrange("p a g c -> p (a g c)")
        decay_in = scratch[:, 0:2 * C].rearrange("p (n c) -> p n c", n=2)
        decay = sb("decay", [P, 2, 2, S])
        write_in = scratch[:, 2 * C:4 * C].rearrange("p (n c) -> p n c", n=2)
        used = Q[:, :, :].rearrange("p h t -> p (h t)").bitcast(F32)
        state = used[:, 0:2 * C].rearrange("p (n c) -> p n c", n=2)
        read = used[:, 2 * C:4 * C].rearrange("p (n c) -> p n c", n=2)
        o_acc = attn[:, :, :].rearrange("p t c -> p (t c)")
        og = nbk
        oh, ol = ah, al
        ye = sq
        y_acc = y0

        def banks(name, n, uses):
            tile = ctx.enter_context(nc.psum_tensor(name, [P, n, C], F32))
            return Banks(tile, sem(name + "_full"), sem(name + "_free"), uses)

        G = [banks("g0", 2, [("xT0", 1), ("qk0", 2)] + [(("f0", c), 2) for c in range(0, NF0, 2)]
                   + [(("st", s), 1) for s in range(0, NPAIR, 2)] + [("xT1", 1), ("kq1", 2)]
                   + [(("f1", c), 2) for c in range(0, NF1, 2)] + [("out1", 1)]),
             banks("g1", 2, [("r0", 1), ("v0", 1)] + [(("f0", c), 2) for c in range(1, NF0, 2)]
                   + [(("st", s), 1) for s in range(1, NPAIR, 2)] + [("r1", 1), ("vb1", 2)]
                   + [(("f1", c), 2) for c in range(1, NF1, 2)])]
        B = [banks("b0", 1, [("cwT0", 1)] + [(("cw0", c), 1) for c in range(NF0 - 1)] + [("mT", 1), ("pv0", 0), ("gate1", 1),
                   ("cwT1", 1), ("cw1_0", 1), ("cw1_2", 1), ("y1_0", 0), ("y1_2", 0), ("nT", 1)]),
             banks("b1", 1, [("y0", 0), ("aT", 1), ("cw1_1", 1), ("cw1_3", 1), ("y1_1", 0), ("y1_3", 0)])]
        R = banks("r", 2, [(("max", m), 1) for m in range(NPAIR)] + [("pv1", 0), ("out0", 1), ("ss1", 2)]
                  + [(("j", j), 2) for j in range(HD)] + [("oT", 1)])

        def pv_banks(b):
            return (B[0], "pv0") if b == 0 else (R, "pv1")

        staged = [sem(f"staged{n}") for n in range(2)]
        hi_made, lo_made = sem("hi_made"), sem("lo_made")
        loaded, consts, consts_v = sem("loaded"), sem("consts"), sem("consts_v")
        x_loaded = signal("x_loaded", 1, 16)
        x_stored = signal("x_stored", 1, 16, ahead=1)
        qk_saved = signal("qk_saved", 1, 16)
        qk_packed = signal("qk_packed", 24, 16)
        max_saved = signal("max_saved", 1, 16)
        max_packed = signal("max_packed", 2, 16)
        var_made = [signal(f"var_made{n}", 1) for n in range(3)]
        rstd_made = [signal(f"rstd_made{n}", 1) for n in range(3)]
        normed = [signal(f"normed{n}", 1) for n in range(2)]
        x_hi = [signal(f"x_hi{n}", 1) for n in range(2)]
        x_plus_bm = signal("x_plus_bm", 1)
        exp_made = [signal(f"exp_made{n}", 1) for n in range(2)]
        cw_made = [signal(f"cw_made{n}", 1) for n in range(2)]
        beta_exp = signal("beta_exp", 1)
        rows_made = [signal(f"rows_made{n}", 1) for n in range(2)]
        part1 = signal("part1", 2)
        part2 = signal("part2", 1)
        part3 = signal("part3", 1)
        silu_made = [signal(f"silu_made{n}", n_) for n, n_ in ((0, NF0), (1, NF1))]
        down_done = [signal("down_done0", NF0), signal("down_done1", NF1)]
        max_parts_made = signal("max_parts_made", 1)
        probs_masked = signal("probs_masked", NPAIR)
        pv_done = signal("pv_done", NPAIR)
        a_hi = signal("a_hi", 1)
        squares = signal("squares", 1)
        ln_made = signal("ln_made", 1)
        rs_made = signal("rs_made", 1)
        kq_hi = signal("kq_hi", 1)
        kq_lo = signal("kq_lo", 1)
        beta_spread = signal("beta_spread", 1)
        gate_made = signal("gate_made", 1)
        decay_in_made = signal("decay_in_made", HD)
        decay_made = signal("decay_made", HD)
        read_added = signal("read_added", HD - 1)
        ye_added = signal("ye_added", E1 - 1)
        of_made = signal("of_made", 1)
        o_hi = signal("o_hi", 1)
        o_lo = signal("o_lo", 1)
        CHAIN = 51
        dve_chain = sem("dve_chain")
        dve_held, pool_held, sp_held = sem("dve_held"), sem("pool_held"), sem("sp_held")

        pieces = []
        for W, col in ((Wq0, W0_Q), (Wk0, W0_K), (Wv0, W0_V), (Wm0, W0_M), (Sg0, W0_SG), (Su0, W0_SU)):
            pieces.append((W, P, 0, col))
        pieces.append((Wr0, E0, 0, W0_R))
        pieces.append((Wg0.rearrange("e d f -> d e f"), E0 * F0, 0, W0_G))
        pieces.append((Wu0.rearrange("e d f -> d e f"), E0 * F0, 0, W0_U))
        for W, col in ((Wq1, W1_Q), (Wk1, W1_K), (Wv1, W1_V), (Wgate1, W1_G), (Wout1, W1_O)):
            pieces.append((W, P, 1, col))
        pieces.append((Wbeta1, H, 1, W1_R))
        pieces.append((gate_w1[0:E1, :].rearrange("e d -> d e"), E1, 1, W1_R + H))
        for e in range(E1):
            pieces.append((w1[e], F1, 1, W1_1 + e * F1))
            pieces.append((w3[e], F1, 1, W1_3 + e * F1))

        block = ctx.enter_context(nc.Block())

        @block.sync
        def _(sp):
            for n, (src, width, _, _) in enumerate(pieces):
                if n >= 2:
                    sp.wait_ge(lo_made, n - 1)
                dst = stage[:, n % 2, 0:width]
                if len(src.shape) == 3:
                    dst = dst.rearrange("p (e f) -> p e f", f=F0)
                sp.dma_start(dst, src, allow_slow_non_contiguous=width == E1).then_inc(staged[n % 2], 16)

            sp.sem_inc(x_stored.sem, 16)
            sp.dma_start(xin[:, :, :], x_chunks[0]).then_inc(x_loaded.sem, 16)

            def chunk(i, last=False):
                sp.wait_ge(*part3(i))
                sp.dma_start(qk_dram.rearrange("a p c t -> c (a p) t"),
                             qk_parts[:, :, :, :].rearrange("c a p t -> c (a p) t")).then_inc(qk_saved.sem, 16)
                sp.wait_ge(*qk_saved(i))
                for g in range(2):
                    for n, parts in enumerate(SLOTS):
                        for a, dst in enumerate((Q, K)):
                            src = qk_dram[a, parts[a]].rearrange("(h g d) t -> g d h t", g=2, d=HD)[g]
                            row = 64 * g + HD * n
                            sp.dma_start(dst[row:row + HD, :, :], src).then_inc(qk_packed.sem, 16)
                sp.wait_ge(*B[0].released(i, "mT"))
                sp.dma_start(max_dram, max_rows[:, :]).then_inc(max_saved.sem, 16)
                sp.wait_ge(*max_saved(i))
                for g in range(2):
                    sp.dma_start(Q[64 * g + QK_ROWS:64 * g + ST_ROWS, :, :],
                                 max_dram.rearrange("(g p h) t -> g p h t", g=2, h=H2)[g])\
                      .then_inc(max_packed.sem, 16)
                if not last:
                    sp.wait_ge(*R.released(i, "out0"))
                    sp.wait_ge(*x_plus_bm(i))
                    sp.sem_inc(sp_held, 1)
                    sp.dma_start(xin[:, :, :], x_chunks[i + 1]).then_inc(x_loaded.sem, 16)
                sp.wait_ge(*G[0].released(i, "out1"))
                sp.sem_inc(sp_held, 1)
                sp.dma_start(out_chunks[i], x2[:, :, :]).then_inc(x_stored.sem, 16)

            with sp.Fori(0, NCH - 1) as i:
                chunk(i)
            chunk(NCH - 1, last=True)
            sp.wait_ge(*x_stored(NCH - 1))

        @block.gpsimd
        def _(pool):
            pool.memset(ident[:, :], 0.0).then_inc(consts, 1)
            pool.memset(causal[:, :, :], 0.0).then_inc(consts, 1)
            pool.memset(mhalf[:, :], -0.5).then_inc(consts, 1)
            pool.memset(decay[:, :, :, :], 0.0).then_inc(consts, 1)
            pool.memset(V[:, :, :, :], 1.0).then_inc(consts, 1)
            pool.memset(K[:, :, :], 1.0).then_inc(consts, 1)
            pool.memset(ex0[:, :, :], -1.0).then_inc(consts, 1)
            pool.memset(ex1[:, :, :], -1.0).then_inc(consts, 1)
            pool.wait_ge(consts, 8)
            pool.affine_select(out=ident[:, :], in_=ident[:, :], compare_op=ALU.not_equal, fill=1.0,
                               base=0, pattern=[[-1, P]], channel_multiplier=1).then_inc(consts, 1)
            pool.affine_select(out=causal[:, :, :], in_=causal[:, :, :], compare_op=ALU.is_ge, fill=MASKED,
                               base=0, pattern=[[0, 2], [-1, P]], channel_multiplier=1).then_inc(consts, 1)
            for dst, src in ((bias0[:, 0:1], bq0), (bias0[:, 1:2], bk0), (bias0[:, 2:3], bv0),
                             (ln1[:, 0:1], ln_g1), (ln1[:, 1:2], ln_b1)):
                pool.dma_start(dst, src.rearrange("(p a) -> p a", a=1)).then_inc(loaded, 16)
            pool.dma_start(bm_rows[:, :], bm0.partition_broadcast(P)).then_inc(loaded, 16)
            pool.dma_start(wd0[:, 0:NF0 - 1, :], Wd0.rearrange("e f d -> (e f) d")
                           .rearrange("(c p) d -> p c d", p=P)).then_inc(loaded, 16)
            pool.dma_start(wd0[:, NF0 - 1, :], Sd0).then_inc(loaded, 16)
            pool.dma_start(wd1[:, :, :], w2[0:E1].rearrange("e f d -> (e f) d")
                           .rearrange("(c p) d -> p c d", p=P)).then_inc(loaded, 16)

            pool.wait_ge(loaded, 16 * 9)

            def rsqrt(n, i):
                pool.wait_ge(*var_made[n](i))
                pool.tensor_tensor(rstd[:, :], veps[:, :], mhalf[:, :], ALU.pow).then_inc(rstd_made[n].sem, 1)

            with pool.Fori(0, NCH) as i:
                rsqrt(0, i)
                pool.wait_ge(*x_loaded(i))
                pool.wait_ge(*x_stored(i, 0))
                pool.tensor_tensor(xb[:, :, :], xin[:, :, :],
                                   bm_rows[:, :].unsqueeze(1).to_broadcast([P, TILES, P]), ALU.add)\
                    .then_inc(x_plus_bm.sem, 1)
                for s in range(NPAIR):
                    pool.wait_ge(*G[s % 2].released(i, ("st", s)))
                    pool.sem_inc(pool_held, 1)
                    diag = probs[:, s % 3, :, 0:2 * P]
                    pool.affine_select(out=diag, in_=diag, compare_op=ALU.is_ge, fill=0.0, base=0,
                                       pattern=[[0, 2], [0, 2], [1, P]], channel_multiplier=-1)\
                        .then_inc(probs_masked.sem, 1)
                rsqrt(1, i)

                def add_read(j):
                    pool.wait_ge(*R.released(i, ("j", j)))
                    so_far = read[:, 0, :] if j == 1 else o_acc[:, :]
                    if j > 1:
                        pool.wait_ge(*read_added(i, j - 1))
                    pool.tensor_tensor(o_acc[:, :], so_far, read[:, j % 2, :], ALU.add)\
                        .then_inc(read_added.sem, 1)

                def add_expert(e):
                    pool.wait_ge(*B[e % 2].released(i, f"y1_{e}"))
                    so_far = ye[:, 0, :] if e == 1 else y_acc[:, :]
                    if e > 1:
                        pool.wait_ge(*ye_added(i, e - 1))
                    pool.tensor_tensor(y_acc[:, :], so_far, ye[:, e % 2, :], ALU.add)\
                        .then_inc(ye_added.sem, 1)

                for c in range(NF1 + 1):
                    if J_AT.get(c - 1, 0) > 0:
                        add_read(J_AT[c - 1])
                    for e in range(1, E1):
                        if c == LAST_OF[e] + 1:
                            add_expert(e)
                rsqrt(2, i)

        @block.scalar
        def _(act):
            for n, (_, width, layer, col) in enumerate(pieces):
                act.wait_ge(staged[n % 2], 16 * (n // 2 + 1))
                act.activation((w0h, w1h)[layer][:, col:col + width], stage[:, n % 2, 0:width], ACT.Copy)\
                   .then_inc(hi_made, 1)
            act.wait_ge(loaded, 16 * 9)
            act.wait_ge(consts, 10)

            def hi_of_x(n, i):
                act.wait_ge(*G[0].filled(i, f"xT{n}"))
                act.activation(xh[:, :], G[0].tile[:, 0, :], ACT.Copy).then_inc(x_hi[n].sem, 1)

            with act.Fori(0, NCH) as i:
                hi_of_x(0, i)
                for a, w in ((0, 1), (1, 2)):
                    act.wait_ge(*G[0].filled(i, "qk0", w))
                    act.activation(qk_parts[:, a, 0, :], G[0].tile[:, a, :], ACT.Identity,
                                   bias=bias0[:, a:a + 1]).then_inc(part1.sem, 1)
                act.wait_ge(*G[1].filled(i, "v0"))
                act.activation(V[:, :, :, 0:HD], G[1].tile[:, 0, :].rearrange("p (t h d) -> p t h d", t=TILES, d=HD),
                               ACT.Copy).then_inc(G[1].free, 1)
                act.wait_ge(*G[0].released(i, "qk0"))
                act.activation(qk_parts[:, :, 1, :], qk_rest[:, :, :], ACT.Copy).then_inc(part2.sem, 1)
                act.wait_ge(*G[1].released(i, "r0"))
                act.activation(ex0[:, :, 0:E0], shifted[:, :, :], ACT.Exp).then_inc(exp_made[0].sem, 1)
                act.wait_ge(*B[0].filled(i, "cwT0"))
                act.activation(rows[0:2 * H, :], B[0].tile[0:2 * H, 0, :], ACT.Copy).then_inc(B[0].free, 1)

                for c in range(NF0):
                    act.wait_ge(*G[c % 2].filled(i, ("f0", c), 1))
                    if c >= 3:
                        act.wait_ge(*G[(c - 3) % 2].released(i, ("f0", c - 3)))
                    act.activation(gated[:, c % 3, :], G[c % 2].tile[:, 0, :], ACT.Silu).then_inc(silu_made[0].sem, 1)
                act.wait_ge(*down_done[0](i))
                act.activation(y0[:, :], B[1].tile[:, 0, :], ACT.Copy).then_inc(B[1].free, 1)
                act.wait_ge(*B[0].filled(i, "mT"))
                act.activation(max_rows[:, :], B[0].tile[0:6 * H2, 0, :], ACT.Copy).then_inc(B[0].free, 1)

                for s in range(NPAIR):
                    act.wait_ge(*G[s % 2].filled(i, ("st", s)))
                    if s >= 3:
                        act.wait_ge(*pv_done(i, s - 2))
                    act.activation(probs[:, s % 3, :, :], G[s % 2].tile[:, :, 0:3 * P], ACT.Exp,
                                   scale=SCORE_SCALE).then_inc(G[s % 2].free, 1)
                act.wait_ge(*B[1].filled(i, "aT"))
                act.activation(ah[:, :], B[1].tile[:, 0, :], ACT.Identity, bias=bias0[:, 2:3]).then_inc(a_hi.sem, 1)

                hi_of_x(1, i)
                act.wait_ge(*G[1].filled(i, "r1"))
                act.activation(eb[:, :, :], G[1].tile[:, 0, 0:TILES * R1].rearrange("p (t r) -> p t r", r=R1)[:, :, 0:H],
                               ACT.Exp, scale=-1.0).then_inc(beta_exp.sem, 1)
                act.wait_ge(*G[1].released(i, "r1"))
                act.activation(ex1[:, :, 0:E1], shifted[:, :, 0:E1], ACT.Exp).then_inc(exp_made[1].sem, 1)
                act.wait_ge(*B[0].filled(i, "gate1"))
                act.activation(gate[:, :], B[0].tile[:, 0, :], ACT.Copy).then_inc(B[0].free, 1)
                act.wait_ge(*G[0].filled(i, "kq1"))
                act.activation(sq[:, :, :], G[0].tile[:, :, :], ACT.Square).then_inc(squares.sem, 1)
                act.wait_ge(*R.released(i, "ss1"))
                act.activation(rs[:, :, :], sq[:, :, :], ACT.Ln).then_inc(ln_made.sem, 1)
                act.wait_ge(*ln_made(i))
                act.activation(rs[:, :, :], rs[:, :, :], ACT.Exp, scale=-0.5).then_inc(rs_made.sem, 1)
                act.wait_ge(*B[0].filled(i, "cwT1"))
                act.activation(rows[:, :], B[0].tile[0:2 * H + 2 * E1, 0, :], ACT.Copy).then_inc(B[0].free, 1)
                act.wait_ge(*G[1].filled(i, "vb1"))
                act.activation(beta_f[:, :], G[1].tile[:, 1, :], ACT.Copy).then_inc(beta_spread.sem, 1)
                act.wait_ge(*G[0].released(i, "kq1"))
                act.activation(kqh[:, :, :], kq[:, :, :], ACT.Copy).then_inc(kq_hi.sem, 1)
                act.activation(gate[:, :], gate[:, :], ACT.Silu).then_inc(gate_made.sem, 1)
                for e in range(E1):
                    act.wait_ge(*B[e % 2].filled(i, f"cw1_{e}"))
                    act.activation(cw1[:, e, :], B[e % 2].tile[:, 0, :], ACT.Copy).then_inc(B[e % 2].free, 1)

                for c in range(NF1):
                    act.wait_ge(*G[c % 2].filled(i, ("f1", c), 1))
                    if c >= 3:
                        act.wait_ge(*G[(c - 3) % 2].released(i, ("f1", c - 3)))
                    act.activation(gated[:, c % 3, :], G[c % 2].tile[:, 0, :], ACT.Silu).then_inc(silu_made[1].sem, 1)
                    if c in J_AT:
                        j = J_AT[c]
                        act.wait_ge(*decay_in_made(i, j + 1))
                        act.activation(decay[:, j % 2, :, 1:S],
                                       decay_in[:, j % 2, :].rearrange("p (b s) -> p b s", s=S)[:, :, 1:S],
                                       ACT.Identity, bias=1.0).then_inc(decay_made.sem, 1)
                act.wait_ge(*B[0].filled(i, "nT"))
                act.activation(og[:, :], B[0].tile[:, 0, :], ACT.Identity, scale=ln1[:, 0:1], bias=ln1[:, 1:2])\
                   .then_inc(B[0].free, 1)
                act.wait_ge(*of_made(i))
                act.activation(oh[:, :], og[:, :], ACT.Copy).then_inc(o_hi.sem, 1)

        @block.vector
        def _(dve):
            for n, (_, width, layer, col) in enumerate(pieces):
                dve.wait_ge(hi_made, n + 1)
                dve.tensor_tensor((w0l, w1l)[layer][:, col:col + width], stage[:, n % 2, 0:width],
                                  (w0h, w1h)[layer][:, col:col + width], ALU.subtract).then_inc(lo_made, 1)
            dve.wait_ge(consts, 10)
            dve.tensor_copy(ident_b[:, :], ident[:, :]).then_inc(consts_v, 1)
            by_d = ident[:, :].rearrange("p (h d) -> p d h", d=HD)
            for j in range(HD):
                dve.tensor_copy(pick[:, j, :].rearrange("p (h i) -> p h i", i=HD),
                                by_d[:, j, :].unsqueeze(2).to_broadcast([P, H, HD])).then_inc(consts_v, 1)
            dve.reduce_sum(head_of[:, :], ident[:, :].rearrange("p (h d) -> p h d", d=HD), AX.X).then_inc(consts_v, 1)
            dve.wait_ge(consts_v, 2 + HD)
            dve.tensor_copy(same_head[:, :].rearrange("p (h i) -> p h i", i=HD),
                            head_of[:, :].unsqueeze(2).to_broadcast([P, H, HD])).then_inc(consts_v, 1)
            dve.tensor_tensor(part_row[:, :], ident[0:2 * H, 0:H], ident[0:2 * H, H:2 * H], ALU.add).then_inc(consts_v, 1)
            dve.wait_ge(consts_v, 4 + HD)
            dve.tensor_copy(pick_e0.rearrange("r c (k m) -> r c k m", k=2),
                            part_row[:, :].rearrange("r (c k) -> r c k", k=2).unsqueeze(3)
                            .to_broadcast([2 * H, NF0 - 1, 2, P // 2])).then_inc(consts_v, 1)
            dve.tensor_copy(pick_h[:, :].rearrange("r (h i) -> r h i", i=HD),
                            part_row[:, :].unsqueeze(2).to_broadcast([2 * H, H, HD])).then_inc(consts_v, 1)
            at = slice(2 * H, 2 * H + 2 * E1)
            dve.tensor_tensor(pick_e1,
                              ident[at, 2 * H:2 * H + E1].unsqueeze(2).to_broadcast([2 * E1, E1, P]),
                              ident[at, 2 * H + E1:2 * H + 2 * E1].unsqueeze(2).to_broadcast([2 * E1, E1, P]),
                              ALU.add).then_inc(consts_v, 1)
            dve.wait_ge(loaded, 16 * 9)
            chain = [0]

            with dve.Fori(0, NCH) as i:
                def link(ins):
                    chain[0] += 1
                    ins.then_inc(dve_chain, 1)
                    dve.wait_ge(dve_chain, i * CHAIN + chain[0])

                def stand_alone():
                    dve.sem_inc(dve_held, 1)

                def layer_norm(n, src):
                    for t in range(TILES):
                        ins = dve.bn_stats(stat[:, t, :], src[:, t, :])
                    link(ins)
                    stand_alone()
                    for t in range(TILES):
                        ins = dve.bn_aggr(mv[:, t, :], stat[:, t, :])
                    link(ins)
                    dve.tensor_scalar(veps[:, :], mv[:, :, 1], LN_EPS, None, ALU.add).then_inc(var_made[n].sem, 1)
                    dve.wait_ge(*rstd_made[n](i))
                    for t in range(TILES):
                        ins = dve.tensor_scalar(xn[:, t, :], src[:, t, :], mv[:, t, 0:1], rstd[:, t:t + 1],
                                                ALU.subtract, ALU.mult)
                    return ins

                def lo_of_x(n):
                    dve.wait_ge(*x_hi[n](i))
                    dve.tensor_tensor(xl[:, :], G[0].tile[:, 0, :], xh[:, :], ALU.subtract).then_inc(G[0].free, 1)

                def shift_logits(n, logits, experts):
                    link(dve.reduce_max(top_max[:, :], logits, AX.X))
                    return dve.tensor_tensor(shifted[:, :, 0:experts], logits,
                                             top_max[:, :].unsqueeze(2).to_broadcast([P, TILES, experts]),
                                             ALU.subtract)

                def top_two(n, ex, rest, experts):
                    stand_alone()
                    for t in range(TILES):
                        ins = dve.max(top8[:, t, :], ex[:, t, 0:experts + 6])
                    link(ins)
                    link(dve.memset(top8[:, :, 2:8], -1.0))
                    stand_alone()
                    for t in range(TILES):
                        ins = dve.match_replace(out=rest[:, t, :], in_to_replace=top8[:, t, :],
                                                in_values=ex[:, t, 0:experts + 6], imm_value=0.0)
                    link(ins)
                    link(dve.tensor_tensor(cw[:, :, 0:experts], ex[:, :, 0:experts], rest[:, :, 0:experts],
                                           ALU.subtract))

                def parts_of(values, at, width):
                    link(dve.tensor_copy(narrow[:, :, at:at + width], values))
                    return dve.tensor_tensor(narrow[:, :, at + width:at + 2 * width], values,
                                             narrow[:, :, at:at + width], ALU.subtract)

                def weigh(n, total_of, experts):
                    link(dve.reduce_sum(ex_sum[:, :], total_of, AX.X))
                    link(dve.reciprocal(ex_sum[:, :], ex_sum[:, :]))
                    link(dve.tensor_tensor(cw[:, :, 0:experts], cw[:, :, 0:experts],
                                           ex_sum[:, :].unsqueeze(2).to_broadcast([P, TILES, experts]), ALU.mult))
                    parts_of(cw[:, :, 0:experts], (0, 2 * H)[n], experts).then_inc(cw_made[n].sem, 1)

                dve.wait_ge(*x_loaded(i))
                layer_norm(0, xin).then_inc(normed[0].sem, 1)
                lo_of_x(0)
                dve.wait_ge(*G[1].filled(i, "r0"))
                ins = shift_logits(0, G[1].tile[:, 0, 0:TILES * E0].rearrange("p (t e) -> p t e", e=E0), E0)
                ins.then_inc(G[1].free, 1)
                for a in range(2):
                    dve.wait_ge(*part1(i, a + 1))
                    ins = dve.scalar_tensor_tensor(out=qk_rest[:, a, :], in0=G[0].tile[:, a, :],
                                                   scalar=bias0[:, a:a + 1], in1=qk_parts[:, a, 0, :],
                                                   op0=ALU.add, op1=ALU.subtract)
                ins.then_inc(G[0].free, 1)
                dve.wait_ge(*part2(i))
                dve.tensor_tensor(qk_parts[:, :, 2, :], qk_rest[:, :, :], qk_parts[:, :, 1, :], ALU.subtract)\
                   .then_inc(part3.sem, 1)
                dve.wait_ge(*exp_made[0](i))
                top_two(0, ex0, rest0, E0)
                weigh(0, ex0[:, :, 0:E0], E0)

                def row_maxima(m):
                    b, h2 = divmod(m, H2)
                    dve.wait_ge(*R.filled(i, ("max", m)))
                    dve.tensor_reduce(row_max[:, b, h2, :, :],
                                      R.tile[:, :, 0:3 * P].rearrange("p g (c t) -> p g c t", t=P),
                                      AX.X, ALU.max).then_inc(R.free, 1)

                def hidden0(c):
                    dve.wait_ge(*silu_made[0](i, c + 1))
                    dve.wait_ge(*G[c % 2].filled(i, ("f0", c)))
                    if c >= 3:
                        dve.wait_ge(*down_done[0](i, c - 2))
                    dst = ug[:, c % 2, :] if c < NF0 - 1 else hid[:, c % 3, :]
                    dve.tensor_tensor(dst, G[c % 2].tile[:, 1, :], gated[:, c % 3, :], ALU.mult)\
                       .then_inc(G[c % 2].free, 1)

                def weighted0(c):
                    dve.wait_ge(*G[c % 2].released(i, ("f0", c)))
                    dve.wait_ge(*B[0].filled(i, ("cw0", c)))
                    dve.tensor_tensor(hid[:, c % 3, :], B[0].tile[:, 0, :], ug[:, c % 2, :], ALU.mult)\
                       .then_inc(B[0].free, 1)

                for c in range(NF0):
                    hidden0(c)
                    if c < NF0 - 1:
                        weighted0(c)
                    for m in range(*MAX_AT.get(c, (0, 0))):
                        row_maxima(m)

                dve.wait_ge(*R.released(i, ("max", NPAIR - 1)))
                tiles = neg_max[:, :, :, :].rearrange("p (b q) g h -> p b q g h", q=2)
                by_head = row_max[:, :, :, :, :].rearrange("p b h g c -> p b g h c")
                link(dve.tensor_tensor(max_rest[:, 0:2, :, :], by_head[:, :, :, :, 1], by_head[:, :, :, :, 2], ALU.max))
                for b in range(2):
                    dve.tensor_scalar(tiles[:, b, 0, :, :], by_head[:, b, :, :, 0], -1.0, None, ALU.mult)
                    ins = dve.tensor_scalar(tiles[:, b, 1, :, :], max_rest[:, b, :, :], -1.0, None, ALU.mult)
                link(ins)
                link(dve.tensor_copy(max_parts[:, :, :, 0, :], neg_max[:, :, :, :]))
                link(dve.tensor_tensor(max_rest[:, :, :, :], neg_max[:, :, :, :], max_parts[:, :, :, 0, :], ALU.subtract))
                link(dve.tensor_copy(max_parts[:, :, :, 1, :], max_rest[:, :, :, :]))
                dve.tensor_tensor(max_parts[:, :, :, 2, :], max_rest[:, :, :, :], max_parts[:, :, :, 1, :],
                                  ALU.subtract).then_inc(max_parts_made.sem, 1)

                for b in range(2):
                    pv, name = pv_banks(b)
                    dve.wait_ge(*pv_done(i, H2 * (b + 1)))
                    got = pv.tile[:, 0, 0:2 * H * (HD + 1)].rearrange("p (q h c) -> p q h c", q=2, c=HD + 1)
                    link(dve.reciprocal(rden[:, b, :, :], got[:, :, :, HD]))
                    dve.tensor_tensor(attn[:, 2 * b:2 * b + 2, :].rearrange("p q (h d) -> p q h d", d=HD),
                                      got[:, :, :, 0:HD], rden[:, b, :, :].unsqueeze(3).to_broadcast([P, 2, H, HD]),
                                      ALU.mult).then_inc(pv.free, 1)
                dve.wait_ge(*a_hi(i))
                dve.scalar_tensor_tensor(out=al[:, :], in0=B[1].tile[:, 0, :], scalar=bias0[:, 2:3], in1=ah[:, :],
                                         op0=ALU.add, op1=ALU.subtract).then_inc(B[1].free, 1)
                dve.wait_ge(*x_plus_bm(i))
                dve.wait_ge(*R.filled(i, "out0"))
                dve.tensor_tensor(x1[:, :, :], R.tile[:, 0, :].rearrange("p (t d) -> p t d", t=TILES), xb[:, :, :],
                                  ALU.add).then_inc(R.free, 1)
                dve.wait_ge(*R.released(i, "out0"))

                layer_norm(1, x1).then_inc(normed[1].sem, 1)
                lo_of_x(1)
                dve.wait_ge(*G[1].filled(i, "r1"))
                dve.wait_ge(*beta_exp(i))
                ins = shift_logits(1, G[1].tile[:, 0, 0:TILES * R1].rearrange("p (t r) -> p t r", r=R1)[:, :, H:R1], E1)
                ins.then_inc(G[1].free, 1)
                link(dve.tensor_scalar(eb[:, :, :], eb[:, :, :], 1.0, None, ALU.add))
                link(dve.reciprocal(beta[:, :, :], eb[:, :, :]))
                link(parts_of(beta[:, :, :], 0, H))
                dve.wait_ge(*exp_made[1](i))
                top_two(1, ex1, rest1, E1)
                weigh(1, cw[:, :, 0:E1], E1)
                dve.wait_ge(*R.filled(i, "ss1"))
                dve.tensor_scalar(sq[:, :, :], R.tile[:, :, :], 1e-24, None, ALU.max).then_inc(R.free, 1)
                dve.wait_ge(*rs_made(i))
                dve.tensor_tensor(kq[:, :, :], G[0].tile[:, :, :], rs[:, :, :], ALU.mult).then_inc(G[0].free, 1)
                dve.wait_ge(*G[0].released(i, "kq1"))
                dve.wait_ge(*beta_spread(i))
                dve.scalar_tensor_tensor(out=nbk[:, :], in0=kq[:, 0, :], scalar=-1.0, in1=beta_f[:, :],
                                         op0=ALU.mult, op1=ALU.mult)
                dve.tensor_tensor(bv[:, :], G[1].tile[:, 0, :], beta_f[:, :], ALU.mult).then_inc(G[1].free, 1)
                dve.wait_ge(*kq_hi(i))
                dve.tensor_tensor(kql[:, :, :], kq[:, :, :], kqh[:, :, :], ALU.subtract).then_inc(kq_lo.sem, 1)

                def hidden1(c):
                    dve.wait_ge(*silu_made[1](i, c + 1))
                    dve.wait_ge(*G[c % 2].filled(i, ("f1", c)))
                    if c >= 3:
                        dve.wait_ge(*down_done[1](i, c - 2))
                    dve.tensor_tensor(hid[:, c % 3, :], G[c % 2].tile[:, 1, :], gated[:, c % 3, :], ALU.mult)\
                       .then_inc(G[c % 2].free, 1)

                def delta_in(j):
                    dve.wait_ge(*R.filled(i, ("j", j)))
                    dve.tensor_tensor(decay_in[:, j % 2, :], R.tile[:, 0, :], nbk[:, :], ALU.mult)\
                       .then_inc(decay_in_made.sem, 1)
                    link(dve.tensor_tensor(write_in[:, j % 2, :], R.tile[:, 0, :], bv[:, :], ALU.mult))

                def delta_scan(j):
                    dve.wait_ge(*decay_made(i, j + 1))
                    link(dve.tensor_tensor_scan(state[:, j % 2, :],
                                                decay[:, j % 2, :, :].rearrange("p b s -> p (b s)"),
                                                write_in[:, j % 2, :], 0.0, ALU.mult, ALU.add))
                    if j >= 2:
                        dve.wait_ge(*read_added(i, max(1, j - 2)))
                    dve.tensor_tensor(read[:, j % 2, :], R.tile[:, 1, :], state[:, j % 2, :], ALU.mult)\
                       .then_inc(R.free, 1)

                def weighted1(e):
                    dve.wait_ge(*down_done[1](i, LAST_OF[e] + 1))
                    if e >= 2:
                        dve.wait_ge(*ye_added(i, max(1, e - 2)))
                    dve.tensor_tensor(ye[:, e % 2, :], B[e % 2].tile[:, 0, :], cw1[:, e, :], ALU.mult)\
                       .then_inc(B[e % 2].free, 1)

                for c in range(NF1 + 1):
                    if c < NF1:
                        hidden1(c)
                    if c in J_AT:
                        delta_in(J_AT[c])
                    if c - 1 in J_AT:
                        delta_scan(J_AT[c - 1])
                    for e in range(E1):
                        if c == LAST_OF[e] + 1:
                            weighted1(e)

                dve.wait_ge(*R.filled(i, "oT"))
                layer_norm(2, R.tile[:, 0, :].rearrange("p (t d) -> p t d", t=TILES)).then_inc(R.free, 1)
                dve.wait_ge(*gate_made(i))
                dve.wait_ge(*B[0].released(i, "nT"))
                dve.tensor_tensor(og[:, :], og[:, :], gate[:, :], ALU.mult).then_inc(of_made.sem, 1)
                dve.wait_ge(*o_hi(i))
                dve.tensor_tensor(ol[:, :], og[:, :], oh[:, :], ALU.subtract).then_inc(o_lo.sem, 1)
                dve.wait_ge(*G[0].filled(i, "out1"))
                dve.wait_ge(*x_stored(i, 0))
                dve.tensor_tensor(x2[:, :, :], G[0].tile[:, 0, :].rearrange("p (t d) -> p t d", t=TILES), x1[:, :, :],
                                  ALU.add).then_inc(G[0].free, 1)
            assert chain[0] == CHAIN, chain[0]

        @block.tensor
        def _(pe):
            pe.wait_ge(lo_made, len(pieces))
            pe.wait_ge(consts, 10)
            pe.wait_ge(consts_v, 7 + HD)
            pe.wait_ge(loaded, 16 * 9)

            def three(dst, left, right, start=True, stop=True):
                pe.matmul(dst, left[0], right[0], start=start, stop=False)
                pe.matmul(dst, left[1], right[0], start=False, stop=False)
                return pe.matmul(dst, left[0], right[1], start=False, stop=stop)

            def w(layer, col, width=P):
                hi, lo = ((w0h, w0l), (w1h, w1l))[layer]
                return hi[:, col:col + width], lo[:, col:col + width]

            def cols(pair, t):
                return pair[0][:, t * P:(t + 1) * P], pair[1][:, t * P:(t + 1) * P]

            X = (xh[:, :], xl[:, :])
            for banks in (*G, *B, R):
                pe.sem_inc(banks.free, 1)

            with pe.Fori(0, NCH) as i:
                def fill(banks, name, ins):
                    ins.then_inc(banks.full, 1)

                def turn_x(n):
                    pe.wait_ge(*normed[n](i))
                    pe.wait_ge(*G[0].empty(i, f"xT{n}"))
                    for t in range(TILES):
                        ins = pe.transpose(G[0].tile[:, 0, t * P:(t + 1) * P], xn[:, t, :], ident[:, :])
                    ins.then_inc(G[0].full, 1)
                    pe.wait_ge(*G[0].released(i, f"xT{n}"))

                def by_token(dst, layer, col, width):
                    for t in range(TILES):
                        ins = three(dst[:, t * width:(t + 1) * width], cols((xh, xl), t), w(layer, col, width))
                    return ins

                turn_x(0)
                pe.wait_ge(*G[1].empty(i, "r0"))
                by_token(G[1].tile[:, 0, :], 0, W0_R, E0).then_inc(G[1].full, 1)
                pe.wait_ge(*G[0].empty(i, "qk0"))
                three(G[0].tile[:, 0, :], w(0, W0_Q), X).then_inc(G[0].full, 1)
                three(G[0].tile[:, 1, :], w(0, W0_K), X).then_inc(G[0].full, 1)
                pe.wait_ge(*G[1].empty(i, "v0"))
                by_token(G[1].tile[:, 0, :], 0, W0_V, P).then_inc(G[1].full, 1)

                def up0(c):
                    g, u = (W0_G + c * P, W0_U + c * P) if c < NF0 - 1 else (W0_SG, W0_SU)
                    pe.wait_ge(*G[c % 2].empty(i, ("f0", c)))
                    three(G[c % 2].tile[:, 0, :], w(0, g), X).then_inc(G[c % 2].full, 1)
                    three(G[c % 2].tile[:, 1, :], w(0, u), X).then_inc(G[c % 2].full, 1)

                def turn_narrow(n, width):
                    pe.wait_ge(*cw_made[n](i))
                    pe.wait_ge(*B[0].empty(i, f"cwT{n}"))
                    for t in range(TILES):
                        ins = pe.matmul(B[0].tile[0:width, 0, t * P:(t + 1) * P], narrow[:, t, 0:width].bitcast(F32),
                                        ident[:, :], start=True, stop=True)
                    ins.then_inc(B[0].full, 1)
                    pe.wait_ge(*B[0].released(i, f"cwT{n}"))

                def spread(banks, name, pick_rows, from_rows):
                    pe.wait_ge(*banks.empty(i, name))
                    pe.matmul(banks.tile[:, 0, :], pick_rows, from_rows, start=True, stop=True).then_inc(banks.full, 1)

                def down0(c):
                    if c < NF0 - 1:
                        pe.wait_ge(*B[0].released(i, ("cw0", c)))
                    else:
                        pe.wait_ge(*G[c % 2].released(i, ("f0", c)))
                    if c == 0:
                        pe.wait_ge(*B[1].empty(i, "y0"))
                    ins = pe.matmul(B[1].tile[:, 0, :], wd0[:, c, :], hid[:, c % 3, :], start=c == 0, stop=c == NF0 - 1)
                    ins.then_inc(down_done[0].sem, 1)

                def score_rows(m):
                    b, h2 = divmod(m, H2)
                    pe.wait_ge(*R.empty(i, ("max", m)))
                    for g in range(2):
                        q, k = Q[64 * g:64 * g + QK_ROWS, h2, :], K[64 * g:64 * g + QK_ROWS, h2, :]
                        q0, dst = b * S, R.tile[:, g, :]
                        pe.matmul(dst[:, 0:P], q[:, q0:q0 + P], k[:, q0:q0 + P], start=True, stop=False,
                                  skip_group_check=True)
                        pe.matmul(dst[:, P:3 * P], q[:, q0 + P:q0 + S], k[:, q0:q0 + S], start=False, stop=False,
                                  skip_group_check=True)
                        ins = pe.matmul(dst[:, 0:3 * P].rearrange("p (c t) -> p c t", t=P)[:, 0:3:2, :], ident_b[:, :],
                                        causal[:, :, :], start=False, stop=True, skip_group_check=True)
                    ins.then_inc(R.full, 1)

                for c in range(NF0 + 1):
                    if c < NF0:
                        up0(c)
                    if c == 1:
                        turn_narrow(0, 2 * H)
                    for n in ((0, 1) if c == 1 else (c,) if 1 < c < NF0 - 1 else ()):
                        if n >= 1:
                            down0(n - 1)
                        spread(B[0], ("cw0", n), pick_e0[:, n, :], rows[0:2 * H, :])
                    if c == NF0 - 1:
                        down0(c - 1)
                    if c == NF0:
                        down0(c - 1)
                    if c == min(MAX_AT):
                        pe.wait_ge(*qk_packed(i))
                    for m in range(*MAX_AT.get(c, (0, 0))):
                        score_rows(m)

                pe.wait_ge(*max_parts_made(i))
                pe.wait_ge(*B[0].empty(i, "mT"))
                for t in range(TILES):
                    ins = pe.matmul(B[0].tile[0:6 * H2, 0, t * P:(t + 1) * P],
                                    max_parts[:, t, :, :, :].rearrange("p g c h -> p (g c h)"), ident_b[:, :],
                                    start=True, stop=True)
                ins.then_inc(B[0].full, 1)

                def score_cols(s):
                    b, h2 = divmod(s, H2)
                    pe.wait_ge(*G[s % 2].empty(i, ("st", s)))
                    for g in range(2):
                        q, k = Q[64 * g:64 * g + ST_ROWS, h2, :], K[64 * g:64 * g + ST_ROWS, h2, :]
                        q0, dst = b * S, G[s % 2].tile[:, g, :]
                        pe.matmul(dst[:, 0:3 * P].rearrange("p (c t) -> p c t", t=P)[:, 0:3:2, :], k[:, q0:q0 + P],
                                  q[:, q0:q0 + S], start=True, stop=True)
                        ins = pe.matmul(dst[:, P:2 * P], k[:, q0 + P:q0 + S], q[:, q0 + P:q0 + S], start=True, stop=True)
                    ins.then_inc(G[s % 2].full, 1)

                def weigh_values(s):
                    b, h2 = divmod(s, H2)
                    pv, name = pv_banks(b)
                    if h2 == 0:
                        pe.wait_ge(*pv.empty(i, name))
                    pe.wait_ge(*probs_masked(i, s + 1))
                    out_of = pv.tile[:, 0, 0:2 * H * (HD + 1)].rearrange("p (q h c) -> p q h c", q=2, c=HD + 1)
                    for g in range(2):
                        h = 2 * h2 + g
                        pr = probs[:, s % 3, g, :]
                        pe.matmul(out_of[:, 0, h, :], pr[:, 0:P], V[:, 2 * b, h, :], start=True, stop=True)
                        pe.matmul(out_of[:, 1, h, :], pr[:, 2 * P:3 * P], V[:, 2 * b, h, :], start=True, stop=False)
                        ins = pe.matmul(out_of[:, 1, h, :], pr[:, P:2 * P], V[:, 2 * b + 1, h, :], start=False, stop=True)
                    ins.then_inc(pv_done.sem, 1)

                pe.wait_ge(*max_packed(i))
                for s in range(NPAIR + 2):
                    if s < NPAIR:
                        score_cols(s)
                    if s >= 2:
                        weigh_values(s - 2)

                pe.wait_ge(*pv_banks(0)[0].released(i, "pv0"))
                pe.wait_ge(*pv_banks(1)[0].released(i, "pv1"))
                pe.wait_ge(*B[1].empty(i, "aT"))
                for t in range(TILES):
                    ins = pe.transpose(B[1].tile[:, 0, t * P:(t + 1) * P], attn[:, t, :], ident[:, :])
                ins.then_inc(B[1].full, 1)
                pe.wait_ge(*R.empty(i, "out0"))
                pe.wait_ge(*B[1].released(i, "aT"))
                for t in range(TILES):
                    dst = R.tile[:, 0, t * P:(t + 1) * P]
                    pe.matmul(dst, y0[:, t * P:(t + 1) * P], ident[:, :], start=True, stop=False)
                    ins = three(dst, cols((ah, al), t), w(0, W0_M), start=False)
                ins.then_inc(R.full, 1)

                turn_x(1)
                pe.wait_ge(*G[1].empty(i, "r1"))
                by_token(G[1].tile[:, 0, :], 1, W1_R, R1).then_inc(G[1].full, 1)
                pe.wait_ge(*G[0].empty(i, "kq1"))
                three(G[0].tile[:, 0, :], w(1, W1_K), X).then_inc(G[0].full, 1)
                three(G[0].tile[:, 1, :], w(1, W1_Q), X).then_inc(G[0].full, 1)
                pe.wait_ge(*B[0].empty(i, "gate1"))
                three(B[0].tile[:, 0, :], w(1, W1_G), X).then_inc(B[0].full, 1)
                pe.wait_ge(*G[1].empty(i, "vb1"))
                three(G[1].tile[:, 0, :], w(1, W1_V), X).then_inc(G[1].full, 1)
                pe.wait_ge(*squares(i))
                pe.wait_ge(*R.empty(i, "ss1"))
                for a in range(2):
                    pe.matmul(R.tile[:, a, :], same_head[:, :], sq[:, a, :], start=True, stop=True).then_inc(R.full, 1)
                turn_narrow(1, 2 * H + 2 * E1)
                pe.matmul(G[1].tile[:, 1, :], pick_h[:, :], rows[0:2 * H, :], start=True, stop=True).then_inc(G[1].full, 1)
                for e in range(E1):
                    spread(B[e % 2], f"cw1_{e}", pick_e1[:, e, :], rows[2 * H:, :])

                def up1(c):
                    pe.wait_ge(*G[c % 2].empty(i, ("f1", c)))
                    three(G[c % 2].tile[:, 0, :], w(1, W1_1 + c * P), X).then_inc(G[c % 2].full, 1)
                    three(G[c % 2].tile[:, 1, :], w(1, W1_3 + c * P), X).then_inc(G[c % 2].full, 1)

                def down1(c):
                    pe.wait_ge(*G[c % 2].released(i, ("f1", c)))
                    for n, (e, lo, hi) in enumerate(OWNERS[c]):
                        if c == FIRST_OF[e]:
                            pe.wait_ge(*B[e % 2].empty(i, f"y1_{e}"))
                        ins = pe.matmul(B[e % 2].tile[:, 0, :], wd1[lo:hi, c, :], hid[lo:hi, c % 3, :],
                                        start=c == FIRST_OF[e], stop=c == LAST_OF[e])
                    ins.then_inc(down_done[1].sem, 1)

                def spread_kq(j):
                    pe.wait_ge(*R.empty(i, ("j", j)))
                    for a in range(2):
                        pe.matmul(R.tile[:, a, :], pick[:, j, :], kqh[:, a, :], start=True, stop=False)
                        pe.matmul(R.tile[:, a, :], pick[:, j, :], kql[:, a, :], start=False, stop=True)\
                          .then_inc(R.full, 1)

                for c in range(NF1 + 1):
                    if c in J_AT:
                        if J_AT[c] == 0:
                            pe.wait_ge(*kq_lo(i))
                        spread_kq(J_AT[c])
                    if c < NF1:
                        up1(c)
                    if c >= 1:
                        down1(c - 1)

                pe.wait_ge(*read_added(i))
                pe.wait_ge(*R.empty(i, "oT"))
                for t in range(TILES):
                    ins = pe.transpose(R.tile[:, 0, t * P:(t + 1) * P], o_acc[:, t * P:(t + 1) * P], ident[:, :])
                ins.then_inc(R.full, 1)
                pe.wait_ge(*R.released(i, "oT"))
                pe.wait_ge(*B[0].empty(i, "nT"))
                for t in range(TILES):
                    ins = pe.transpose(B[0].tile[:, 0, t * P:(t + 1) * P], xn[:, t, :], ident[:, :])
                ins.then_inc(B[0].full, 1)
                pe.wait_ge(*G[0].empty(i, "out1"))
                pe.wait_ge(*ye_added(i))
                pe.wait_ge(*o_lo(i))
                for t in range(TILES):
                    dst = G[0].tile[:, 0, t * P:(t + 1) * P]
                    pe.matmul(dst, y_acc[:, t * P:(t + 1) * P], ident[:, :], start=True, stop=False)
                    ins = three(dst, cols((oh, ol), t), w(1, W1_O), start=False)
                ins.then_inc(G[0].full, 1)


_INS = ['L0_attn_x', 'L0_attn_Wq', 'L0_attn_bq', 'L0_attn_Wk', 'L0_attn_bk', 'L0_attn_Wv', 'L0_attn_bv',
        'L0_attn_Wm', 'L0_attn_bm', 'L0_ffn_Wr', 'L0_ffn_Wg', 'L0_ffn_Wu', 'L0_ffn_Wd', 'L0_ffn_Sg', 'L0_ffn_Su',
        'L0_ffn_Sd', 'L1_attn_Wq', 'L1_attn_Wk', 'L1_attn_Wv', 'L1_attn_Wbeta', 'L1_attn_Wg', 'L1_attn_Wout',
        'L1_attn_ln_g', 'L1_attn_ln_b', 'L1_ffn_gate_w', 'L1_ffn_w1', 'L1_ffn_w2', 'L1_ffn_w3']


def kernel(**inputs):
    import numpy as _np
    import concourse.bacc as _bacc
    from concourse import mybir as _mybir
    from concourse.bass_utils import run_bass_kernel_spmd as _run

    nc = _bacc.Bacc("TRN2", target_bir_lowering=False, num_devices=1)
    arrays, args = {}, []
    for name in _INS:
        a = _np.ascontiguousarray(inputs[name])
        arrays[f"in_{name}_dram"] = a
        args.append(nc.dram_tensor(f"in_{name}_dram", a.shape, _mybir.dt.from_np(a.dtype), kind="ExternalInput").ap())
    shape = inputs['L0_attn_x'].shape
    args.append(nc.dram_tensor("out_0_dram", shape, _mybir.dt.from_np(_np.dtype("float32")),
                               kind="ExternalOutput").ap())
    two_layer_kernel(nc, *args)
    r = _run(nc, [arrays], core_ids=[0])
    return r.results[0]["out_0_dram"]
```

```python
from contextlib import ExitStack

import concourse.bass as bass
from concourse import mybir

ALU = mybir.AluOpType
ACT = mybir.ActivationFunctionType
AX = mybir.AxisListType
F32 = mybir.dt.float32
F32R = mybir.dt.float32r
BF16 = mybir.dt.bfloat16

P = 128
C = 512
S = 256
TILES = C // P
H = 16
HD = 8
H2 = H // 2
E0, F0 = 16, 64
E1, F1 = 4, 704
LN_EPS = 1e-5
SCORE_SCALE = float(HD) ** -0.5
MASKED = -1e30

NF0 = E0 * F0 // P + 1
NF1 = E1 * F1 // P
NPAIR = 2 * H2

W0_Q, W0_K, W0_V, W0_M, W0_SG, W0_SU, W0_G = (P * n for n in range(7))
W0_U = W0_G + E0 * F0
W0_R = W0_U + E0 * F0
W0_COLS = W0_R + E0
W1_Q, W1_K, W1_V, W1_G, W1_O, W1_1 = (P * n for n in range(6))
W1_3 = W1_1 + E1 * F1
W1_R = W1_3 + E1 * F1
R1 = H + E1
W1_COLS = W1_R + R1
STAGE = 1024

SLOTS = [(0, 0), (1, 0), (2, 0), (0, 1), (1, 1), (0, 2)]
QK_ROWS = HD * len(SLOTS)
ST_ROWS = QK_ROWS + 3

OWNERS = []
for _c in range(NF1):
    _lo, _hi = _c * P, (_c + 1) * P
    OWNERS.append([(e, max(_lo, e * F1) - _lo, min(_hi, (e + 1) * F1) - _lo)
                   for e in range(E1) if max(_lo, e * F1) < min(_hi, (e + 1) * F1)])
LAST_OF = [max(c for c in range(NF1) if any(o[0] == e for o in OWNERS[c])) for e in range(E1)]
FIRST_OF = [min(c for c in range(NF1) if any(o[0] == e for o in OWNERS[c])) for e in range(E1)]

LAG = 2
X1_AT, PROJ_AT, V1_AT, SS_AT, LOG_AT, CWT1_AT, BETA_AT = 0, 1, 2, 3, 4, 6, 8
MAX_AT = {c: (2 * c, 2 * c + 2) for c in range(NPAIR // 2)}
MT_AT = 10
GROUPS = 4
ST_AT = {13 + 2 * n: n for n in range(GROUPS)}
PV_AT = {14 + 2 * n: n for n in range(GROUPS)}
ON_AT = {15 + 2 * n: n for n in range(GROUPS)}
K_AT = {2 + 2 * j: j for j in range(HD)}
S_AT = {3 + 2 * j: j for j in range(HD)}
OT_AT, NT_AT, OG_AT, AT_AT = 20, 22, 23, 23


def bank_uses():
    yield from (("F", n, 0, 1) for n in ("xT0", "r0", "q0", "k0", "v0"))
    for c in range(NF0 + LAG):
        if c < NF0:
            yield from (("F", (n, c), 0, 1) for n in ("g0", "u0"))
        if c == 1:
            yield "F", "cwT0", 0, 1
        if 1 <= c < NF0:
            yield "F", ("cw0", c - 1), 0, 1
        if c == LAG:
            yield "Y1", "y0", 0, 0
        names = {X1_AT: ("xT1",), PROJ_AT: ("r1", "k1", "q1"), V1_AT: ("v1", "gate1"), SS_AT: ("ss0", "ss1"),
                 CWT1_AT: ("cwT1",), BETA_AT: ("beta",)}.get(c, ())
        yield from (("F", n, 1, 1) for n in names)
    for c in range(NF1 + LAG):
        if c < NF1:
            yield from (("F", (n, c), 1, 1) for n in ("g1", "u1"))
        for m in range(*MAX_AT.get(c, (0, 0))):
            yield from (("X", ("max", m, g), 0, 1) for g in range(2))
        if c in K_AT:
            yield "X", ("kb", K_AT[c]), 1, 1
        if c in S_AT:
            yield "X", ("qb", S_AT[c]), 1, 1
        for e in range(E1):
            if c == LAST_OF[e] + 1:
                yield "F", ("cw1", e), 1, 1
            if c - LAG == FIRST_OF[e]:
                yield f"Y{e % 2}", ("y1", e), 1, 0
        if c == MT_AT:
            yield "F", "mT", 0, 1
        if c in PV_AT:
            yield "F", ("pv", PV_AT[c]), 0, 1
        if c in ON_AT:
            yield "F", ("on", ON_AT[c]), 0, 1
        if c in ST_AT:
            yield from (("X", ("st", ST_AT[c], h), 0, 1) for h in range(8))
        if c == OT_AT:
            yield "Y0", "oT", 1, 1
        if c == NT_AT:
            yield "F", "nT", 1, 1
        if c == AT_AT:
            yield "F", "aT", 0, 1
    yield "F", "out1", 1, 1
    yield "F", "out0", 0, 1


class Step:

    def __init__(self, kind, m, chunks):
        self.kind = kind
        self.layers = {"first": (0,), "both": (0, 1), "last": (1,)}[kind]
        self.i0 = m + 1 if kind == "both" else 0
        self.i1 = m if kind == "both" else chunks - 1
        self.m = m

    def before(self, first, both):
        return 0 if self.kind == "first" else self.m * both + first


class Signal:

    def __init__(self, sem, per, unit=1, ahead=0):
        self.sem, self.per, self.unit, self.ahead = sem, per, unit, ahead

    def __call__(self, i, k=None):
        k = self.per if k is None else k
        return self.sem, i * (self.per * self.unit) + (k + self.ahead) * self.unit


class Bank:

    def __init__(self, tile, full, free):
        self.tile, self.full, self.free = tile, full, free
        self.uses = []

    def at(self, step, name):
        uses = [u for u in self.uses if u[1] in step.layers]
        k = [u[0] for u in uses].index(name)
        first = [u for u in self.uses if u[1] == 0]
        return (step.before(len(first), len(self.uses)) + k,
                step.before(sum(u[2] for u in first), sum(u[2] for u in self.uses)) + sum(u[2] for u in uses[:k]))


class Use:

    def __init__(self, bank, name):
        self.bank, self.name = bank, name
        self.full, self.free = bank.full, bank.free

    def __getitem__(self, key):
        return self.bank.tile[key]

    def empty(self, step):
        return self.free, self.bank.at(step, self.name)[0] + 1

    def filled(self, step):
        return self.full, self.bank.at(step, self.name)[1] + 1

    def released(self, step):
        return self.free, self.bank.at(step, self.name)[0] + 2


def two_layer_kernel(nc, x, Wq0, bq0, Wk0, bk0, Wv0, bv0, Wm0, bm0, Wr0, Wg0, Wu0, Wd0, Sg0, Su0, Sd0,
                     Wq1, Wk1, Wv1, Wbeta1, Wgate1, Wout1, ln_g1, ln_b1, gate_w1, w1, w2, w3, out):
    tokens = x.shape[0] * x.shape[1]
    NCH = tokens // C
    x_chunks = x.rearrange("b s d -> (b s) d").rearrange("(n t p) d -> n p t d", t=TILES, p=P)
    out_chunks = out.rearrange("b s d -> (b s) d").rearrange("(n t p) d -> n p t d", t=TILES, p=P)
    max_dram = nc.dram_tensor("max_dram", (6 * H2, C), BF16).ap()
    qk_dram = nc.dram_tensor("qk_dram", (2, 3, P, C), BF16).ap()

    ctx = ExitStack()
    with ctx:
        def sb(name, shape, dt=F32):
            return ctx.enter_context(nc.sbuf_tensor(name, shape, dt))

        def sem(name):
            return ctx.enter_context(nc.semaphore(name))

        def signal(name, per, unit=1, ahead=0):
            return Signal(sem(name), per, unit, ahead)

        w0h, w0l = sb("w0h", [P, W0_COLS], F32R), sb("w0l", [P, W0_COLS], F32R)
        w1h, w1l = sb("w1h", [P, W1_COLS], F32R), sb("w1l", [P, W1_COLS], F32R)
        wd0 = sb("wd0", [P, NF0, P])
        wd1 = sb("wd1", [P, NF1, P])
        bias0 = sb("bias0", [P, 3])
        bm_rows = sb("bm_rows", [P, P])
        ln1 = sb("ln1", [P, 2])
        ident = sb("ident", [P, P])
        ident_b = sb("ident_b", [P, P], BF16)
        causal = sb("causal", [P, 2, P], BF16)
        same_head = sb("same_head", [P, P])
        pick = sb("pick", [P, HD, P], F32R)
        head_of = sb("head_of", [P, H])
        part_row = sb("part_row", [2 * H, H])
        pick_e = sb("pick_e", [2 * H + 2 * E1, NF0 - 1, P], F32R)
        pick_e0, pick_e1 = pick_e[0:2 * H, :, :], pick_e[2 * H:, 0:E1, :]
        pick_h = sb("pick_h", [2 * H, P], F32R)
        mhalf = sb("mhalf", [P, TILES])

        xin = sb("xin", [P, TILES, P])
        xres = sb("xres", [P, TILES, P])
        xh0, xl0 = sb("xh0", [P, C], F32R), sb("xl0", [P, C], F32R)
        qk_parts = sb("qk_parts_sb", [P, 2, 3, C], BF16)
        qk_rest = sb("qk_rest", [P, 2, C])
        Q = sb("Q", [P, H2, C], BF16)
        K = sb("K", [P, H2, C], BF16)
        V = sb("V", [P, TILES, H, HD + 1])
        row_max = sb("row_max", [P, 2, H2, 2, 3])
        neg_max = sb("neg_max", [P, TILES, 2, H2])
        max_rest = sb("max_rest", [P, TILES, 2, H2])
        max_parts = sb("max_parts", [P, TILES, 2, 3, H2], BF16)
        probs = sb("probs", [P, 2, 4, 3 * P])
        stage = probs[:, :, :, :].rearrange("p b h t -> p (b h t)")[:, 0:2 * STAGE]\
            .rearrange("p (n c) -> p n c", n=2)
        rden = sb("rden", [P, TILES, 4])
        attn = sb("attn", [P, TILES, P])
        ah, al = xh0, xl0
        rows0 = sb("rows0", [2 * H, C], F32R)
        max_rows = sb("max_rows", [6 * H2, C], BF16)
        ug = qk_rest
        heads_out = qk_rest
        y0 = sb("y0", [P, C])

        stat = [sb(f"stat{n}", [P, TILES, 6]) for n in range(2)]
        mv = [sb(f"mv{n}", [P, TILES, 2]) for n in range(2)]
        veps = [sb(f"veps{n}", [P, TILES]) for n in range(2)]
        rstd = [sb(f"rstd{n}", [P, TILES]) for n in range(2)]
        top_max = sb("top_max", [P, TILES])
        shifted = sb("shifted", [P, TILES, E0])
        ex0 = sb("ex0", [P, TILES, E0 + 8])
        ex1 = sb("ex1", [P, TILES, E1 + 8])
        rest0 = sb("rest0", [P, TILES, E0 + 6])
        rest1 = sb("rest1", [P, TILES, E1 + 6])
        top8 = sb("top8", [P, TILES, 8])
        ex_sum = sb("ex_sum", [P, TILES])
        cw = sb("cw", [P, TILES, E0])
        narrow = sb("narrow", [P, TILES, 2 * H + 2 * E1], F32R)
        gated = sb("gated", [P, 2, C])
        hid = sb("hid", [P, 3, C])

        x1 = sb("x1", [P, TILES, P])
        x1n = sb("x1n", [P, TILES, P])
        xh1, xl1 = sb("xh1", [P, C], F32R), sb("xl1", [P, C], F32R)
        rows1 = sb("rows1", [2 * H + 2 * E1, C], F32R)
        eb = sb("eb", [P, TILES, H])
        beta = sb("beta", [P, TILES, H])
        sq = sb("sq", [P, 2, C])
        kq = sb("kq", [P, 2, C])
        kqh, kql = sb("kqh", [P, 2, C], F32R), sb("kql", [P, 2, C], F32R)
        nbk = sb("nbk", [P, C])
        bv = sb("bv", [P, C])
        gate = sb("gate", [P, C])
        decay = sb("decay", [P, 2, 2, S])
        write_in = sb("write_in", [P, C])
        state = sb("state", [P, C])
        read, o_acc = kq[:, 0, :], kq[:, 1, :]
        x2 = state[:, :].rearrange("p (t d) -> p t d", t=TILES)
        on1 = x1n
        og = nbk
        oh, ol = kqh[:, 0, :], kql[:, 0, :]
        ye, y_acc = sq[:, 0, :], sq[:, 1, :]
        cw1 = qk_parts[:, :, :, :].rearrange("p a n t -> p (a n t)").bitcast(F32)[:, 0:2 * C]\
            .rearrange("p (n c) -> p n c", n=2)

        size = {"F": 4, "X": 2, "Y0": 1, "Y1": 1}
        ring_banks = {}
        for ring, n in size.items():
            for b in range(n):
                name = f"{ring}{b}"
                tile = ctx.enter_context(nc.psum_tensor(name, [P, C], F32))
                ring_banks[ring, b] = Bank(tile, sem(name + "_full"), sem(name + "_free"))
        use, seen = {}, dict.fromkeys(size, 0)
        for ring, name, layer, parts in bank_uses():
            bank = ring_banks[ring, seen[ring] % size[ring]]
            seen[ring] += 1
            bank.uses.append((name, layer, parts))
            use[name] = Use(bank, name)

        staged = [sem(f"staged{n}") for n in range(2)]
        hi_made, lo_made = sem("hi_made"), sem("lo_made")
        loaded, consts, consts_v = sem("loaded"), sem("consts"), sem("consts_v")
        x_loaded = signal("x_loaded", 1, 16)
        res_loaded = signal("res_loaded", 1, 16)
        qk_saved = signal("qk_saved", 1, 16)
        qk_packed = signal("qk_packed", 24, 16)
        max_saved = signal("max_saved", 1, 16)
        max_packed = signal("max_packed", 2, 16)
        x_plus_bm = signal("x_plus_bm", 1)
        part1 = signal("part1", 2)
        part2 = signal("part2", 1)
        part3 = signal("part3", 1)
        max_parts_made = signal("max_parts_made", 1)
        probs_masked = signal("probs_masked", 4 * GROUPS)
        a_hi = signal("a_hi", 1)
        var_made = [signal(f"var_made{n}", 1) for n in range(3)]
        rstd_made = [signal(f"rstd_made{n}", 1) for n in range(3)]
        normed = [signal(f"normed{n}", 1) for n in range(2)]
        x_hi = [signal(f"x_hi{n}", 1) for n in range(2)]
        exp_made = [signal(f"exp_made{n}", 1) for n in range(2)]
        cw_made = [signal(f"cw_made{n}", 1) for n in range(2)]
        silu_made = [signal("silu_made0", NF0), signal("silu_made1", NF1)]
        down_done = [signal("down_done0", NF0), signal("down_done1", NF1)]
        x_stored = signal("x_stored", 1, 16, ahead=1)
        beta_in = signal("beta_in", 1)
        beta_exp = signal("beta_exp", 1)
        ln_made = signal("ln_made", 1)
        rs_made = signal("rs_made", 1)
        kq_made = signal("kq_made", 1)
        kq_hi = signal("kq_hi", 1)
        kq_lo = signal("kq_lo", 1)
        gate_made = signal("gate_made", 1)
        decay_in_made = signal("decay_in_made", HD)
        decay_made = signal("decay_made", HD)
        read_added = signal("read_added", HD - 1)
        ye_added = signal("ye_added", E1 - 1)
        of_made = signal("of_made", 1)
        o_hi = signal("o_hi", 1)
        o_lo = signal("o_lo", 1)
        CH_FIRST, CH_BOTH = 20, 45
        dve_chain = sem("dve_chain")
        dve_held, pool_held, sp_held = sem("dve_held"), sem("pool_held"), sem("sp_held")

        def run_steps(engine, step):
            step(Step("first", 0, NCH))
            with engine.Fori(0, NCH - 1) as m:
                step(Step("both", m, NCH))
            step(Step("last", NCH - 1, NCH))

        pieces = []
        for W, col in ((Wq0, W0_Q), (Wk0, W0_K), (Wv0, W0_V), (Wm0, W0_M), (Sg0, W0_SG), (Su0, W0_SU)):
            pieces.append((W, P, 0, col))
        pieces.append((Wr0, E0, 0, W0_R))
        pieces.append((Wg0.rearrange("e d f -> d e f"), E0 * F0, 0, W0_G))
        pieces.append((Wu0.rearrange("e d f -> d e f"), E0 * F0, 0, W0_U))
        for W, col in ((Wq1, W1_Q), (Wk1, W1_K), (Wv1, W1_V), (Wgate1, W1_G), (Wout1, W1_O)):
            pieces.append((W, P, 1, col))
        pieces.append((Wbeta1, H, 1, W1_R))
        pieces.append((gate_w1[0:E1, :].rearrange("e d -> d e"), E1, 1, W1_R + H))
        for e in range(E1):
            pieces.append((w1[e], F1, 1, W1_1 + e * F1))
            pieces.append((w3[e], F1, 1, W1_3 + e * F1))

        block = ctx.enter_context(nc.Block())

        @block.sync
        def _(sp):
            for n, (src, width, _, _) in enumerate(pieces):
                if n >= 2:
                    sp.wait_ge(lo_made, n - 1)
                dst = stage[:, n % 2, 0:width]
                if len(src.shape) == 3:
                    dst = dst.rearrange("p (e f) -> p e f", f=F0)
                sp.dma_start(dst, src, allow_slow_non_contiguous=width == E1).then_inc(staged[n % 2], 16)

            sp.sem_inc(x_stored.sem, 16)
            sp.dma_start(xin[:, :, :], x_chunks[0]).then_inc(x_loaded.sem, 16)

            def step(st, next_x=True):
                i0, i1 = st.i0, st.i1
                if 0 in st.layers:
                    sp.wait_ge(*part3(i0))
                    sp.dma_start(qk_dram.rearrange("a p c t -> c (a p) t"),
                                 qk_parts[:, :, :, :].rearrange("c a p t -> c (a p) t")).then_inc(qk_saved.sem, 16)
                    sp.wait_ge(*qk_saved(i0))
                    for g in range(2):
                        for n, parts in enumerate(SLOTS):
                            for a, dst in enumerate((Q, K)):
                                src = qk_dram[a, parts[a]].rearrange("(h g d) t -> g d h t", g=2, d=HD)[g]
                                row = 64 * g + HD * n
                                sp.dma_start(dst[row:row + HD, :, :], src).then_inc(qk_packed.sem, 16)
                    sp.wait_ge(*use["xT0"].released(st))
                    sp.sem_inc(sp_held, 1)
                    sp.dma_start(xres[:, :, :], x_chunks[i0]).then_inc(res_loaded.sem, 16)
                    if next_x:
                        sp.dma_start(xin[:, :, :], x_chunks[i0 + 1]).then_inc(x_loaded.sem, 16)
                    sp.wait_ge(*use["mT"].released(st))
                    sp.dma_start(max_dram, max_rows[:, :]).then_inc(max_saved.sem, 16)
                    sp.wait_ge(*max_saved(i0))
                    for g in range(2):
                        sp.dma_start(Q[64 * g + QK_ROWS:64 * g + ST_ROWS, :, :],
                                     max_dram.rearrange("(g p h) t -> g p h t", g=2, h=H2)[g])\
                          .then_inc(max_packed.sem, 16)
                if 1 in st.layers:
                    sp.wait_ge(*use["out1"].released(st))
                    sp.sem_inc(sp_held, 1)
                    sp.dma_start(out_chunks[i1], x2).then_inc(x_stored.sem, 16)

            step(Step("first", 0, NCH))
            if NCH > 2:
                with sp.Fori(0, NCH - 2) as m:
                    step(Step("both", m, NCH))
            step(Step("both", NCH - 2, NCH), next_x=False)
            step(Step("last", NCH - 1, NCH))
            sp.wait_ge(*x_stored(NCH - 1))

        @block.gpsimd
        def _(pool):
            pool.memset(ident[:, :], 0.0).then_inc(consts, 1)
            pool.memset(causal[:, :, :], 0.0).then_inc(consts, 1)
            pool.memset(mhalf[:, :], -0.5).then_inc(consts, 1)
            pool.memset(decay[:, :, :, :], 0.0).then_inc(consts, 1)
            pool.memset(V[:, :, :, :], 1.0).then_inc(consts, 1)
            pool.memset(K[:, :, :], 1.0).then_inc(consts, 1)
            pool.memset(ex0[:, :, :], -1.0).then_inc(consts, 1)
            pool.memset(ex1[:, :, :], -1.0).then_inc(consts, 1)
            pool.wait_ge(consts, 8)
            pool.affine_select(out=ident[:, :], in_=ident[:, :], compare_op=ALU.not_equal, fill=1.0,
                               base=0, pattern=[[-1, P]], channel_multiplier=1).then_inc(consts, 1)
            pool.affine_select(out=causal[:, :, :], in_=causal[:, :, :], compare_op=ALU.is_ge, fill=MASKED,
                               base=0, pattern=[[0, 2], [-1, P]], channel_multiplier=1).then_inc(consts, 1)
            for dst, src in ((bias0[:, 0:1], bq0), (bias0[:, 1:2], bk0), (bias0[:, 2:3], bv0),
                             (ln1[:, 0:1], ln_g1), (ln1[:, 1:2], ln_b1)):
                pool.dma_start(dst, src.rearrange("(p a) -> p a", a=1)).then_inc(loaded, 16)
            pool.dma_start(bm_rows[:, :], bm0.partition_broadcast(P)).then_inc(loaded, 16)
            pool.dma_start(wd0[:, 0:NF0 - 1, :], Wd0.rearrange("e f d -> (e f) d")
                           .rearrange("(c p) d -> p c d", p=P)).then_inc(loaded, 16)
            pool.dma_start(wd0[:, NF0 - 1, :], Sd0).then_inc(loaded, 16)
            pool.dma_start(wd1[:, :, :], w2[0:E1].rearrange("e f d -> (e f) d")
                           .rearrange("(c p) d -> p c d", p=P)).then_inc(loaded, 16)

            pool.wait_ge(loaded, 16 * 9)

            def rsqrt(n, i):
                pool.wait_ge(*var_made[n](i))
                pool.tensor_tensor(rstd[min(n, 1)][:, :], veps[min(n, 1)][:, :], mhalf[:, :], ALU.pow)\
                    .then_inc(rstd_made[n].sem, 1)

            def step(st):
                i0, i1 = st.i0, st.i1
                if 0 in st.layers:
                    rsqrt(0, i0)
                if 1 in st.layers:
                    rsqrt(1, i1)
                if 0 in st.layers:
                    pool.wait_ge(*res_loaded(i0))
                    pool.tensor_tensor(xres[:, :, :], xres[:, :, :],
                                       bm_rows[:, :].unsqueeze(1).to_broadcast([P, TILES, P]), ALU.add)\
                        .then_inc(x_plus_bm.sem, 1)

                def mask_group(n):
                    for k in range(0, 8, 2):
                        pool.wait_ge(*use["st", n, k + 1].released(st))
                        pool.sem_inc(pool_held, 1)
                        diag = probs[:, k // 4, k % 4:k % 4 + 2, 0:2 * P]
                        pool.affine_select(out=diag, in_=diag, compare_op=ALU.is_ge, fill=0.0, base=0,
                                           pattern=[[0, 2], [0, 2], [1, P]], channel_multiplier=-1)\
                            .then_inc(probs_masked.sem, 1)

                def add_read(j):
                    pool.wait_ge(*use["qb", j].released(st))
                    if j > 1:
                        pool.wait_ge(*read_added(i1, j - 1))
                    pool.tensor_tensor(o_acc, o_acc, read, ALU.add).then_inc(read_added.sem, 1)

                def add_expert(e):
                    pool.wait_ge(*use["y1", e].released(st))
                    if e > 1:
                        pool.wait_ge(*ye_added(i1, e - 1))
                    pool.tensor_tensor(y_acc, y_acc, ye, ALU.add).then_inc(ye_added.sem, 1)

                for c in range(NF1 + LAG):
                    if 1 in st.layers:
                        if S_AT.get(c, 0) > 0:
                            add_read(S_AT[c])
                        for e in range(1, E1):
                            if c == LAST_OF[e] + LAG:
                                add_expert(e)
                    if c in ST_AT and 0 in st.layers:
                        mask_group(ST_AT[c])
                    if c == OT_AT and 1 in st.layers:
                        rsqrt(2, i1)

            run_steps(pool, step)

        @block.scalar
        def _(act):
            for n, (_, width, layer, col) in enumerate(pieces):
                act.wait_ge(staged[n % 2], 16 * (n // 2 + 1))
                act.activation((w0h, w1h)[layer][:, col:col + width], stage[:, n % 2, 0:width], ACT.Copy)\
                   .then_inc(hi_made, 1)
            act.wait_ge(loaded, 16 * 9)
            act.wait_ge(consts, 10)

            def step(st):
                i0, i1 = st.i0, st.i1

                def hi_of_x(n):
                    act.wait_ge(*use[f"xT{n}"].filled(st))
                    act.activation((xh0, xh1)[n][:, :], use[f"xT{n}"][:, :], ACT.Copy).then_inc(x_hi[n].sem, 1)

                def layer0_start():
                    hi_of_x(0)
                    for a, name in ((0, "q0"), (1, "k0")):
                        act.wait_ge(*use[name].filled(st))
                        act.activation(qk_parts[:, a, 0, :], use[name][:, :], ACT.Identity,
                                       bias=bias0[:, a:a + 1]).then_inc(part1.sem, 1)
                    act.wait_ge(*use["r0"].released(st))
                    act.activation(ex0[:, :, 0:E0], shifted[:, :, :], ACT.Exp).then_inc(exp_made[0].sem, 1)
                    act.wait_ge(*use["v0"].filled(st))
                    act.activation(V[:, :, :, 0:HD], use["v0"][:, :].rearrange("p (t h d) -> p t h d", t=TILES, d=HD),
                                   ACT.Copy).then_inc(use["v0"].free, 1)
                    act.wait_ge(*use["k0"].released(st))
                    act.activation(qk_parts[:, :, 1, :], qk_rest[:, :, :], ACT.Copy).then_inc(part2.sem, 1)

                def silu(layer, c):
                    g = use[f"g{layer}", c]
                    act.wait_ge(*g.filled(st))
                    if c >= 2:
                        act.wait_ge(*use[f"u{layer}", c - 2].released(st))
                    elif layer == 1 and 0 in st.layers:
                        act.wait_ge(*use["u0", NF0 - 1].released(st))
                    act.activation(gated[:, c % 2, :], g[:, :], ACT.Silu).then_inc(g.free, 1)

                def layer1_projections(c):
                    if c == X1_AT:
                        hi_of_x(1)
                    if c == PROJ_AT:
                        r = use["r1"]
                        act.wait_ge(*r.filled(st))
                        act.activation(eb[:, :, :], r[:, 0:TILES * R1].rearrange("p (t r) -> p t r", r=R1)[:, :, 0:H],
                                       ACT.Copy).then_inc(beta_in.sem, 1)
                        for a, name in enumerate(("k1", "q1")):
                            act.wait_ge(*use[name].filled(st))
                            act.activation(kq[:, a, :], use[name][:, :], ACT.Copy)
                            act.activation(sq[:, a, :], use[name][:, :], ACT.Square).then_inc(use[name].free, 1)
                    if c == V1_AT:
                        act.wait_ge(*use["v1"].filled(st))
                        act.activation(bv[:, :], use["v1"][:, :], ACT.Copy).then_inc(use["v1"].free, 1)
                        act.wait_ge(*use["gate1"].filled(st))
                        act.activation(gate[:, :], use["gate1"][:, :], ACT.Silu).then_inc(use["gate1"].free, 1)
                    if c == SS_AT:
                        act.wait_ge(*use["ss1"].released(st))
                        act.activation(sq[:, :, :], sq[:, :, :], ACT.Ln).then_inc(ln_made.sem, 1)
                        act.wait_ge(*beta_in(i1))
                        act.activation(eb[:, :, :], eb[:, :, :], ACT.Exp, scale=-1.0).then_inc(beta_exp.sem, 1)
                        act.wait_ge(*use["r1"].released(st))
                        act.activation(ex1[:, :, 0:E1], shifted[:, :, 0:E1], ACT.Exp).then_inc(exp_made[1].sem, 1)
                        act.wait_ge(*ln_made(i1))
                        act.activation(sq[:, :, :], sq[:, :, :], ACT.Exp, scale=-0.5).then_inc(rs_made.sem, 1)
                    if c == LOG_AT + 1:
                        act.wait_ge(*kq_made(i1))
                        act.activation(kqh[:, :, :], kq[:, :, :], ACT.Copy).then_inc(kq_hi.sem, 1)
                    if c == CWT1_AT:
                        act.wait_ge(*use["cwT1"].filled(st))
                        act.activation(rows1[:, :], use["cwT1"][0:2 * H + 2 * E1, :], ACT.Copy)\
                           .then_inc(use["cwT1"].free, 1)

                if 0 in st.layers:
                    layer0_start()
                for c in range(NF0 + LAG):
                    if 0 in st.layers:
                        if c < NF0:
                            silu(0, c)
                        if c == 1:
                            act.wait_ge(*use["cwT0"].filled(st))
                            act.activation(rows0[:, :], use["cwT0"][0:2 * H, :], ACT.Copy).then_inc(use["cwT0"].free, 1)
                    if 1 in st.layers:
                        layer1_projections(c)
                if 0 in st.layers:
                    act.wait_ge(*down_done[0](i0))
                    act.activation(y0[:, :], use["y0"][:, :], ACT.Copy).then_inc(use["y0"].free, 1)

                def grow_decay(j):
                    act.wait_ge(*decay_in_made(i1, j + 1))
                    d = decay[:, j % 2, :, 1:S]
                    act.activation(d, d, ACT.Identity, bias=1.0).then_inc(decay_made.sem, 1)

                def exp_group(n):
                    if n >= 1:
                        act.wait_ge(*use["pv", n - 1].filled(st))
                    for k in range(8):
                        bank = use["st", n, k]
                        act.wait_ge(*bank.filled(st))
                        act.activation(probs[:, k // 4, k % 4, :], bank[:, 0:3 * P], ACT.Exp,
                                       scale=SCORE_SCALE).then_inc(bank.free, 1)

                for c in range(NF1 + LAG):
                    if c < NF1 and 1 in st.layers:
                        silu(1, c)
                        if c in K_AT:
                            grow_decay(K_AT[c])
                        for e in range(E1):
                            if c == LAST_OF[e] + 1:
                                if e >= 2:
                                    act.wait_ge(*use["y1", e - 2].released(st))
                                act.wait_ge(*use["cw1", e].filled(st))
                                act.activation(cw1[:, e % 2, :], use["cw1", e][:, :], ACT.Copy)\
                                   .then_inc(use["cw1", e].free, 1)
                    if 0 in st.layers:
                        if c == MT_AT:
                            act.wait_ge(*use["mT"].filled(st))
                            act.activation(max_rows[:, :], use["mT"][0:6 * H2, :], ACT.Copy).then_inc(use["mT"].free, 1)
                        if c in PV_AT:
                            n = PV_AT[c]
                            act.wait_ge(*use["pv", n].filled(st))
                            if n >= 2:
                                act.wait_ge(*use["on", n - 2].filled(st))
                            act.activation(heads_out[:, n % 2, :], use["pv", n][:, :], ACT.Copy)\
                               .then_inc(use["pv", n].free, 1)
                        if c in ST_AT:
                            exp_group(ST_AT[c])
                    if c == LAST_OF[E1 - 1] + 1 and 1 in st.layers and c >= NF1:
                        act.wait_ge(*use["y1", E1 - 3].released(st))
                        act.wait_ge(*use["cw1", E1 - 1].filled(st))
                        act.activation(cw1[:, (E1 - 1) % 2, :], use["cw1", E1 - 1][:, :], ACT.Copy)\
                           .then_inc(use["cw1", E1 - 1].free, 1)
                    if c == NT_AT and 1 in st.layers:
                        act.wait_ge(*use["nT"].filled(st))
                        act.activation(og[:, :], use["nT"][:, :], ACT.Identity, scale=ln1[:, 0:1], bias=ln1[:, 1:2])\
                           .then_inc(use["nT"].free, 1)
                if 0 in st.layers:
                    act.wait_ge(*use["aT"].filled(st))
                    act.activation(ah[:, :], use["aT"][:, :], ACT.Identity, bias=bias0[:, 2:3]).then_inc(a_hi.sem, 1)
                if 1 in st.layers:
                    act.wait_ge(*of_made(i1))
                    act.activation(oh, og[:, :], ACT.Copy).then_inc(o_hi.sem, 1)

            run_steps(act, step)

        @block.vector
        def _(dve):
            for n, (_, width, layer, col) in enumerate(pieces):
                dve.wait_ge(hi_made, n + 1)
                dve.tensor_tensor((w0l, w1l)[layer][:, col:col + width], stage[:, n % 2, 0:width],
                                  (w0h, w1h)[layer][:, col:col + width], ALU.subtract).then_inc(lo_made, 1)
            dve.wait_ge(consts, 10)
            dve.tensor_copy(ident_b[:, :], ident[:, :]).then_inc(consts_v, 1)
            by_d = ident[:, :].rearrange("p (h d) -> p d h", d=HD)
            for j in range(HD):
                dve.tensor_copy(pick[:, j, :].rearrange("p (h i) -> p h i", i=HD),
                                by_d[:, j, :].unsqueeze(2).to_broadcast([P, H, HD])).then_inc(consts_v, 1)
            dve.reduce_sum(head_of[:, :], ident[:, :].rearrange("p (h d) -> p h d", d=HD), AX.X).then_inc(consts_v, 1)
            dve.wait_ge(consts_v, 2 + HD)
            dve.tensor_copy(same_head[:, :].rearrange("p (h i) -> p h i", i=HD),
                            head_of[:, :].unsqueeze(2).to_broadcast([P, H, HD])).then_inc(consts_v, 1)
            dve.tensor_tensor(part_row[:, :], ident[0:2 * H, 0:H], ident[0:2 * H, H:2 * H], ALU.add).then_inc(consts_v, 1)
            dve.wait_ge(consts_v, 4 + HD)
            dve.tensor_copy(pick_e0.rearrange("r c (k m) -> r c k m", k=2),
                            part_row[:, :].rearrange("r (c k) -> r c k", k=2).unsqueeze(3)
                            .to_broadcast([2 * H, NF0 - 1, 2, P // 2])).then_inc(consts_v, 1)
            dve.tensor_copy(pick_h[:, :].rearrange("r (h i) -> r h i", i=HD),
                            part_row[:, :].unsqueeze(2).to_broadcast([2 * H, H, HD])).then_inc(consts_v, 1)
            at = slice(2 * H, 2 * H + 2 * E1)
            dve.tensor_tensor(pick_e1,
                              ident[at, 2 * H:2 * H + E1].unsqueeze(2).to_broadcast([2 * E1, E1, P]),
                              ident[at, 2 * H + E1:2 * H + 2 * E1].unsqueeze(2).to_broadcast([2 * E1, E1, P]),
                              ALU.add).then_inc(consts_v, 1)
            dve.wait_ge(loaded, 16 * 9)

            def step(st):
                i0, i1 = st.i0, st.i1
                chain = [0]

                def link(ins):
                    chain[0] += 1
                    ins.then_inc(dve_chain, 1)
                    dve.wait_ge(dve_chain, st.before(CH_FIRST, CH_BOTH) + chain[0])

                def stand_alone():
                    dve.sem_inc(dve_held, 1)

                def variance(n, src):
                    w = min(n, 1)
                    for t in range(TILES):
                        ins = dve.bn_stats(stat[w][:, t, :], src[:, t, :])
                    link(ins)
                    stand_alone()
                    for t in range(TILES):
                        ins = dve.bn_aggr(mv[w][:, t, :], stat[w][:, t, :])
                    link(ins)
                    dve.tensor_scalar(veps[w][:, :], mv[w][:, :, 1], LN_EPS, None, ALU.add).then_inc(var_made[n].sem, 1)

                def normalise(n, i, dst, src):
                    w = min(n, 1)
                    dve.wait_ge(*rstd_made[n](i))
                    for t in range(TILES):
                        ins = dve.tensor_scalar(dst[:, t, :], src[:, t, :], mv[w][:, t, 0:1], rstd[w][:, t:t + 1],
                                                ALU.subtract, ALU.mult)
                    return ins

                def lo_of_x(n, i):
                    dve.wait_ge(*x_hi[n](i))
                    dve.tensor_tensor((xl0, xl1)[n][:, :], use[f"xT{n}"][:, :], (xh0, xh1)[n][:, :], ALU.subtract)\
                       .then_inc(use[f"xT{n}"].free, 1)

                def shift_logits(logits, experts):
                    link(dve.reduce_max(top_max[:, :], logits, AX.X))
                    return dve.tensor_tensor(shifted[:, :, 0:experts], logits,
                                             top_max[:, :].unsqueeze(2).to_broadcast([P, TILES, experts]),
                                             ALU.subtract)

                def top_two(ex, rest, experts):
                    stand_alone()
                    for t in range(TILES):
                        ins = dve.max(top8[:, t, :], ex[:, t, 0:experts + 6])
                    link(ins)
                    link(dve.memset(top8[:, :, 2:8], -1.0))
                    stand_alone()
                    for t in range(TILES):
                        ins = dve.match_replace(out=rest[:, t, :], in_to_replace=top8[:, t, :],
                                                in_values=ex[:, t, 0:experts + 6], imm_value=0.0)
                    link(ins)
                    link(dve.tensor_tensor(cw[:, :, 0:experts], ex[:, :, 0:experts], rest[:, :, 0:experts],
                                           ALU.subtract))

                def parts_of(values, at, width):
                    link(dve.tensor_copy(narrow[:, :, at:at + width], values))
                    return dve.tensor_tensor(narrow[:, :, at + width:at + 2 * width], values,
                                             narrow[:, :, at:at + width], ALU.subtract)

                def weigh(n, total_of, experts):
                    link(dve.reduce_sum(ex_sum[:, :], total_of, AX.X))
                    link(dve.reciprocal(ex_sum[:, :], ex_sum[:, :]))
                    link(dve.tensor_tensor(cw[:, :, 0:experts], cw[:, :, 0:experts],
                                           ex_sum[:, :].unsqueeze(2).to_broadcast([P, TILES, experts]), ALU.mult))
                    parts_of(cw[:, :, 0:experts], (0, 2 * H)[n], experts).then_inc(cw_made[n].sem, 1)

                if 0 in st.layers:
                    dve.wait_ge(*x_loaded(i0))
                    variance(0, xin)
                if 1 in st.layers:
                    variance(1, x1)
                if 0 in st.layers:
                    normalise(0, i0, xin, xin).then_inc(normed[0].sem, 1)
                if 1 in st.layers:
                    normalise(1, i1, x1n, x1).then_inc(normed[1].sem, 1)
                if 0 in st.layers:
                    lo_of_x(0, i0)
                    dve.wait_ge(*use["r0"].filled(st))
                    shift_logits(use["r0"][:, 0:TILES * E0].rearrange("p (t e) -> p t e", e=E0), E0)\
                        .then_inc(use["r0"].free, 1)
                    for a, name in enumerate(("q0", "k0")):
                        dve.wait_ge(*part1(i0, a + 1))
                        dve.scalar_tensor_tensor(out=qk_rest[:, a, :], in0=use[name][:, :],
                                                 scalar=bias0[:, a:a + 1], in1=qk_parts[:, a, 0, :],
                                                 op0=ALU.add, op1=ALU.subtract).then_inc(use[name].free, 1)
                    dve.wait_ge(*exp_made[0](i0))
                    top_two(ex0, rest0, E0)
                    weigh(0, ex0[:, :, 0:E0], E0)
                    dve.wait_ge(*part2(i0))
                    dve.tensor_tensor(qk_parts[:, :, 2, :], qk_rest[:, :, :], qk_parts[:, :, 1, :], ALU.subtract)\
                       .then_inc(part3.sem, 1)

                def hidden0(c):
                    g, u = use["g0", c], use["u0", c]
                    dve.wait_ge(*g.released(st))
                    dve.wait_ge(*u.filled(st))
                    if c == NF0 - 1:
                        dve.wait_ge(*down_done[0](i0, c - 2))
                    elif c >= 2:
                        dve.wait_ge(*use["cw0", c - 2].released(st))
                    else:
                        dve.wait_ge(*part3(i0))
                    dst = ug[:, c % 2, :] if c < NF0 - 1 else hid[:, c % 3, :]
                    dve.tensor_tensor(dst, u[:, :], gated[:, c % 2, :], ALU.mult).then_inc(u.free, 1)

                def weighted0(c):
                    dve.wait_ge(*use["u0", c].released(st))
                    dve.wait_ge(*use["cw0", c].filled(st))
                    if c >= 3:
                        dve.wait_ge(*down_done[0](i0, c - 2))
                    dve.tensor_tensor(hid[:, c % 3, :], use["cw0", c][:, :], ug[:, c % 2, :], ALU.mult)\
                       .then_inc(use["cw0", c].free, 1)

                def layer1_projections(c):
                    if c == X1_AT:
                        lo_of_x(1, i1)
                    if c == PROJ_AT:
                        r = use["r1"]
                        dve.wait_ge(*r.filled(st))
                        dve.wait_ge(*beta_in(i1))
                        shift_logits(r[:, 0:TILES * R1].rearrange("p (t r) -> p t r", r=R1)[:, :, H:R1], E1)\
                            .then_inc(r.free, 1)
                    if c == SS_AT:
                        for a in range(2):
                            ss = use[f"ss{a}"]
                            dve.wait_ge(*ss.filled(st))
                            dve.tensor_scalar(sq[:, a, :], ss[:, :], 1e-24, None, ALU.max).then_inc(ss.free, 1)
                    if c == LOG_AT:
                        dve.wait_ge(*rs_made(i1))
                        dve.tensor_tensor(kq[:, :, :], kq[:, :, :], sq[:, :, :], ALU.mult).then_inc(kq_made.sem, 1)
                        dve.wait_ge(*beta_exp(i1))
                        link(dve.tensor_scalar(eb[:, :, :], eb[:, :, :], 1.0, None, ALU.add))
                        link(dve.reciprocal(beta[:, :, :], eb[:, :, :]))
                        link(parts_of(beta[:, :, :], 0, H))
                    if c == LOG_AT + 1:
                        dve.wait_ge(*exp_made[1](i1))
                        top_two(ex1, rest1, E1)
                        weigh(1, cw[:, :, 0:E1], E1)
                        dve.wait_ge(*kq_hi(i1))
                        dve.tensor_tensor(kql[:, :, :], kq[:, :, :], kqh[:, :, :], ALU.subtract).then_inc(kq_lo.sem, 1)
                    if c == BETA_AT:
                        b = use["beta"]
                        dve.wait_ge(*b.filled(st))
                        dve.wait_ge(*kq_made(i1))
                        dve.scalar_tensor_tensor(out=nbk[:, :], in0=kq[:, 0, :], scalar=-1.0, in1=b[:, :],
                                                 op0=ALU.mult, op1=ALU.mult)
                        dve.wait_ge(*use["v1"].released(st))
                        dve.tensor_tensor(bv[:, :], bv[:, :], b[:, :], ALU.mult).then_inc(b.free, 1)

                for c in range(NF0 + LAG):
                    if 0 in st.layers:
                        if c < NF0:
                            hidden0(c)
                        if 1 <= c < NF0:
                            weighted0(c - 1)
                    if 1 in st.layers:
                        layer1_projections(c)

                def hidden1(c):
                    g, u = use["g1", c], use["u1", c]
                    dve.wait_ge(*g.released(st))
                    dve.wait_ge(*u.filled(st))
                    if c >= 3:
                        dve.wait_ge(*down_done[1](i1, c - 2))
                    elif 0 in st.layers:
                        dve.wait_ge(*down_done[0](i0))
                    dve.tensor_tensor(hid[:, c % 3, :], u[:, :], gated[:, c % 2, :], ALU.mult).then_inc(u.free, 1)

                def row_maxima(m):
                    b, h2 = divmod(m, H2)
                    for g in range(2):
                        bank = use["max", m, g]
                        dve.wait_ge(*bank.filled(st))
                        dve.tensor_reduce(row_max[:, b, h2, g, :], bank[:, 0:3 * P].rearrange("p (c t) -> p c t", t=P),
                                          AX.X, ALU.max).then_inc(bank.free, 1)

                def split_maxima():
                    dve.wait_ge(*use["max", NPAIR - 1, 1].released(st))
                    tiles = neg_max[:, :, :, :].rearrange("p (b q) g h -> p b q g h", q=2)
                    by_head = row_max[:, :, :, :, :].rearrange("p b h g c -> p b g h c")
                    link(dve.tensor_tensor(max_rest[:, 0:2, :, :], by_head[:, :, :, :, 1], by_head[:, :, :, :, 2],
                                           ALU.max))
                    for b in range(2):
                        dve.tensor_scalar(tiles[:, b, 0, :, :], by_head[:, b, :, :, 0], -1.0, None, ALU.mult)
                        ins = dve.tensor_scalar(tiles[:, b, 1, :, :], max_rest[:, b, :, :], -1.0, None, ALU.mult)
                    link(ins)
                    link(dve.tensor_copy(max_parts[:, :, :, 0, :], neg_max[:, :, :, :]))
                    link(dve.tensor_tensor(max_rest[:, :, :, :], neg_max[:, :, :, :], max_parts[:, :, :, 0, :],
                                           ALU.subtract))
                    link(dve.tensor_copy(max_parts[:, :, :, 1, :], max_rest[:, :, :, :]))
                    dve.tensor_tensor(max_parts[:, :, :, 2, :], max_rest[:, :, :, :], max_parts[:, :, :, 1, :],
                                      ALU.subtract).then_inc(max_parts_made.sem, 1)

                def delta_in(j):
                    kb = use["kb", j]
                    dve.wait_ge(*kb.filled(st))
                    if j == 0:
                        dve.wait_ge(*use["beta"].released(st))
                    halves = kb[:, :].rearrange("p (b s) -> p b s", s=S)
                    dve.tensor_tensor(decay[:, j % 2, :, 1:S], halves[:, :, 1:S],
                                      nbk[:, :].rearrange("p (b s) -> p b s", s=S)[:, :, 1:S], ALU.mult)\
                       .then_inc(decay_in_made.sem, 1)
                    dve.tensor_tensor(write_in[:, :], kb[:, :], bv[:, :], ALU.mult).then_inc(kb.free, 1)

                def delta_scan(j):
                    dve.wait_ge(*decay_made(i1, j + 1))
                    dve.wait_ge(*use["kb", j].released(st))
                    if j == 0:
                        dve.wait_ge(*x_stored(i1, 0))
                    link(dve.tensor_tensor_scan(state[:, :], decay[:, j % 2, :, :].rearrange("p b s -> p (b s)"),
                                                write_in[:, :], 0.0, ALU.mult, ALU.add))
                    qb = use["qb", j]
                    dve.wait_ge(*qb.filled(st))
                    if j >= 2:
                        dve.wait_ge(*read_added(i1, j - 1))
                    dve.tensor_tensor(o_acc if j == 0 else read, qb[:, :], state[:, :], ALU.mult)\
                       .then_inc(qb.free, 1)

                def weighted1(e):
                    dve.wait_ge(*down_done[1](i1, LAST_OF[e] + 1))
                    dve.wait_ge(*use["cw1", e].released(st))
                    if e >= 2:
                        dve.wait_ge(*ye_added(i1, e - 1))
                    dve.tensor_tensor(y_acc if e == 0 else ye, use["y1", e][:, :], cw1[:, e % 2, :], ALU.mult)\
                       .then_inc(use["y1", e].free, 1)

                def normalise_heads(n):
                    on = use["on", n]
                    dve.wait_ge(*on.filled(st))
                    if n >= 1:
                        dve.wait_ge(*use["on", n - 1].released(st))
                    got = on[:, :].rearrange("p (t h c) -> p t h c", t=TILES, h=4)
                    link(dve.reciprocal(rden[:, :, :], got[:, :, :, HD]))
                    dve.tensor_tensor(attn[:, :, :].rearrange("p t (h d) -> p t h d", d=HD)[:, :, 4 * n:4 * n + 4, :],
                                      got[:, :, :, 0:HD], rden[:, :, :].unsqueeze(3).to_broadcast([P, TILES, 4, HD]),
                                      ALU.mult).then_inc(on.free, 1)

                for c in range(NF1 + LAG):
                    if c < NF1 and 1 in st.layers:
                        hidden1(c)
                    if 0 in st.layers:
                        for m in range(*MAX_AT.get(c, (0, 0))):
                            row_maxima(m)
                        if c == MT_AT - 2:
                            split_maxima()
                        if c in ON_AT:
                            normalise_heads(ON_AT[c])
                    if 1 in st.layers:
                        if c in K_AT:
                            delta_in(K_AT[c])
                        if c in S_AT:
                            delta_scan(S_AT[c])
                        for e in range(E1):
                            if c == LAST_OF[e] + LAG:
                                weighted1(e)
                        if c == OT_AT:
                            oT = use["oT"]
                            dve.wait_ge(*oT.filled(st))
                            turned = oT[:, :].rearrange("p (t d) -> p t d", t=TILES)
                            variance(2, turned)
                            normalise(2, i1, on1, turned).then_inc(oT.free, 1)
                if 1 in st.layers:
                    dve.wait_ge(*gate_done(st))
                    dve.wait_ge(*use["nT"].released(st))
                    dve.tensor_tensor(og[:, :], og[:, :], gate[:, :], ALU.mult).then_inc(of_made.sem, 1)
                if 0 in st.layers:
                    dve.wait_ge(*a_hi(i0))
                    dve.scalar_tensor_tensor(out=al[:, :], in0=use["aT"][:, :], scalar=bias0[:, 2:3], in1=ah[:, :],
                                             op0=ALU.add, op1=ALU.subtract).then_inc(use["aT"].free, 1)
                if 1 in st.layers:
                    dve.wait_ge(*o_hi(i1))
                    dve.tensor_tensor(ol, og[:, :], oh, ALU.subtract).then_inc(o_lo.sem, 1)
                    out1 = use["out1"]
                    dve.wait_ge(*out1.filled(st))
                    dve.tensor_tensor(x2, out1[:, :].rearrange("p (t d) -> p t d", t=TILES), x1[:, :, :],
                                      ALU.add).then_inc(out1.free, 1)
                if 0 in st.layers:
                    out0 = use["out0"]
                    if 1 in st.layers:
                        dve.wait_ge(*out1.released(st))
                    dve.wait_ge(*x_plus_bm(i0))
                    dve.wait_ge(*out0.filled(st))
                    dve.tensor_tensor(x1[:, :, :], out0[:, :].rearrange("p (t d) -> p t d", t=TILES), xres[:, :, :],
                                      ALU.add).then_inc(out0.free, 1)
                    dve.wait_ge(*out0.released(st))
                    want = {"first": CH_FIRST, "both": CH_BOTH}[st.kind]
                    assert chain[0] == want, (st.kind, chain[0])

            def gate_done(st):
                return use["gate1"].released(st)

            run_steps(dve, step)

        @block.tensor
        def _(pe):
            pe.wait_ge(lo_made, len(pieces))
            pe.wait_ge(consts, 10)
            pe.wait_ge(consts_v, 7 + HD)
            pe.wait_ge(loaded, 16 * 9)

            def three(dst, left, right, start=True, stop=True):
                pe.matmul(dst, left[0], right[0], start=start, stop=False)
                pe.matmul(dst, left[1], right[0], start=False, stop=False)
                return pe.matmul(dst, left[0], right[1], start=False, stop=stop)

            def w(layer, col, width=P):
                hi, lo = ((w0h, w0l), (w1h, w1l))[layer]
                return hi[:, col:col + width], lo[:, col:col + width]

            def cols(pair, t):
                return pair[0][:, t * P:(t + 1) * P], pair[1][:, t * P:(t + 1) * P]

            X = ((xh0[:, :], xl0[:, :]), (xh1[:, :], xl1[:, :]))
            for bank in ring_banks.values():
                pe.sem_inc(bank.free, 1)

            def step(st):
                i0, i1 = st.i0, st.i1

                def bank_for(name):
                    pe.wait_ge(*use[name].empty(st))
                    return use[name]

                def turn(name, src):
                    bank = bank_for(name)
                    for t in range(TILES):
                        ins = pe.transpose(bank[:, t * P:(t + 1) * P], src(t), ident[:, :])
                    ins.then_inc(bank.full, 1)

                def project(name, layer, col):
                    bank = bank_for(name)
                    three(bank[:, :], w(layer, col), X[layer]).then_inc(bank.full, 1)

                def by_token(name, layer, col, width):
                    bank = bank_for(name)
                    for t in range(TILES):
                        ins = three(bank[:, t * width:(t + 1) * width], cols(X[layer], t), w(layer, col, width))
                    ins.then_inc(bank.full, 1)

                def turn_narrow(n, width):
                    pe.wait_ge(*cw_made[n]((i0, i1)[n]))
                    bank = bank_for(f"cwT{n}")
                    for t in range(TILES):
                        ins = pe.matmul(bank[0:width, t * P:(t + 1) * P], narrow[:, t, 0:width].bitcast(F32),
                                        ident[:, :], start=True, stop=True)
                    ins.then_inc(bank.full, 1)

                def spread(name, pick_rows, from_rows):
                    bank = bank_for(name)
                    pe.matmul(bank[:, :], pick_rows, from_rows, start=True, stop=True).then_inc(bank.full, 1)

                def down0(c):
                    if c < NF0 - 1:
                        pe.wait_ge(*use["cw0", c].released(st))
                    else:
                        pe.wait_ge(*use["u0", c].released(st))
                    y = use["y0"]
                    if c == 0:
                        pe.wait_ge(*y.empty(st))
                    pe.matmul(y[:, :], wd0[:, c, :], hid[:, c % 3, :], start=c == 0, stop=c == NF0 - 1)\
                      .then_inc(down_done[0].sem, 1)

                def layer1_projections(c):
                    if c == X1_AT:
                        pe.wait_ge(*normed[1](i1))
                        turn("xT1", lambda t: x1n[:, t, :])
                    if c == PROJ_AT:
                        pe.wait_ge(*use["xT1"].released(st))
                        by_token("r1", 1, W1_R, R1)
                        project("k1", 1, W1_K)
                        project("q1", 1, W1_Q)
                    if c == V1_AT:
                        project("v1", 1, W1_V)
                        project("gate1", 1, W1_G)
                    if c == SS_AT:
                        for a, name in enumerate(("k1", "q1")):
                            bank = bank_for(f"ss{a}")
                            pe.wait_ge(*use[name].released(st))
                            pe.matmul(bank[:, :], same_head[:, :], sq[:, a, :], start=True, stop=True)\
                              .then_inc(bank.full, 1)
                    if c == CWT1_AT:
                        turn_narrow(1, 2 * H + 2 * E1)
                    if c == BETA_AT:
                        pe.wait_ge(*use["cwT1"].released(st))
                        spread("beta", pick_h[:, :], rows1[0:2 * H, :])

                if 0 in st.layers:
                    pe.wait_ge(*normed[0](i0))
                    turn("xT0", lambda t: xin[:, t, :])
                    pe.wait_ge(*use["xT0"].released(st))
                    by_token("r0", 0, W0_R, E0)
                    project("q0", 0, W0_Q)
                    project("k0", 0, W0_K)
                    by_token("v0", 0, W0_V, P)

                for c in range(NF0 + LAG):
                    if 0 in st.layers:
                        if c < NF0:
                            g, u = (W0_G + c * P, W0_U + c * P) if c < NF0 - 1 else (W0_SG, W0_SU)
                            project(("g0", c), 0, g)
                            project(("u0", c), 0, u)
                        if c == 1:
                            turn_narrow(0, 2 * H)
                        if 1 <= c < NF0:
                            if c == 1:
                                pe.wait_ge(*use["cwT0"].released(st))
                            spread(("cw0", c - 1), pick_e0[:, c - 1, :], rows0[:, :])
                        if c >= LAG:
                            down0(c - LAG)
                    if 1 in st.layers:
                        layer1_projections(c)

                def down1(c):
                    pe.wait_ge(*use["u1", c].released(st))
                    for e, lo, hi in OWNERS[c]:
                        y = use["y1", e]
                        if c == FIRST_OF[e]:
                            pe.wait_ge(*y.empty(st))
                        ins = pe.matmul(y[:, :], wd1[lo:hi, c, :], hid[lo:hi, c % 3, :],
                                        start=c == FIRST_OF[e], stop=c == LAST_OF[e])
                    ins.then_inc(down_done[1].sem, 1)

                def spread_kq(name, a, j):
                    bank = bank_for((name, j))
                    pe.matmul(bank[:, :], pick[:, j, :], kqh[:, a, :], start=True, stop=False)
                    pe.matmul(bank[:, :], pick[:, j, :], kql[:, a, :], start=False, stop=True).then_inc(bank.full, 1)

                def score_rows(m):
                    b, h2 = divmod(m, H2)
                    q0 = b * S
                    for g in range(2):
                        q, k = Q[64 * g:64 * g + QK_ROWS, h2, :], K[64 * g:64 * g + QK_ROWS, h2, :]
                        bank = bank_for(("max", m, g))
                        pe.matmul(bank[:, 0:P], q[:, q0:q0 + P], k[:, q0:q0 + P], start=True, stop=False,
                                  skip_group_check=True)
                        pe.matmul(bank[:, P:3 * P], q[:, q0 + P:q0 + S], k[:, q0:q0 + S], start=False, stop=False,
                                  skip_group_check=True)
                        pe.matmul(bank[:, 0:3 * P].rearrange("p (c t) -> p c t", t=P)[:, 0:3:2, :], ident_b[:, :],
                                  causal[:, :, :], start=False, stop=True, skip_group_check=True)\
                          .then_inc(bank.full, 1)

                def score_cols(n, k):
                    b, h = k // 4, 4 * n + k % 4
                    g, h2, q0 = h % 2, h // 2, b * S
                    bank = bank_for(("st", n, k))
                    q, k = Q[64 * g:64 * g + ST_ROWS, h2, :], K[64 * g:64 * g + ST_ROWS, h2, :]
                    pe.matmul(bank[:, 0:3 * P].rearrange("p (c t) -> p c t", t=P)[:, 0:3:2, :], k[:, q0:q0 + P],
                              q[:, q0:q0 + S], start=True, stop=True)
                    pe.matmul(bank[:, P:2 * P], k[:, q0 + P:q0 + S], q[:, q0 + P:q0 + S], start=True, stop=True)\
                      .then_inc(bank.full, 1)

                def weigh_values(n):
                    bank = bank_for(("pv", n))
                    for b in range(2):
                        for c in range(4):
                            if c % 2 == 0:
                                pe.wait_ge(*probs_masked(i0, 4 * n + 2 * b + c // 2 + 1))
                            pe.matmul(bank[32 * c:32 * c + HD + 1, b * S:(b + 1) * S], V[:, 2 * b, 4 * n + c, :],
                                      probs[:, b, c, :].rearrange("p (c t) -> p c t", t=P)[:, 0:3:2, :],
                                      start=True, stop=False, skip_group_check=True)
                        for c in range(4):
                            ins = pe.matmul(bank[32 * c:32 * c + HD + 1, b * S + P:(b + 1) * S],
                                            V[:, 2 * b + 1, 4 * n + c, :], probs[:, b, c, P:2 * P],
                                            start=False, stop=True, skip_group_check=True)
                    ins.then_inc(bank.full, 1)

                def attention(c):
                    if c in PV_AT:
                        weigh_values(PV_AT[c])
                    if c in ON_AT:
                        n = ON_AT[c]
                        pe.wait_ge(*use["pv", n].released(st))
                        turn(("on", n), lambda t: heads_out[:, n % 2, t * P:(t + 1) * P])
                    if c in ST_AT:
                        if ST_AT[c] == 0:
                            pe.wait_ge(*max_packed(i0))
                        for k in range(8):
                            score_cols(ST_AT[c], k)

                for c in range(NF1 + LAG):
                    if 1 in st.layers and c < NF1:
                        project(("g1", c), 1, W1_1 + c * P)
                        project(("u1", c), 1, W1_3 + c * P)
                    if c == 0 and 0 in st.layers:
                        pe.wait_ge(*qk_packed(i0))
                    if 0 in st.layers:
                        for m in range(*MAX_AT.get(c, (0, 0))):
                            score_rows(m)
                    if 1 in st.layers:
                        if c in K_AT:
                            if K_AT[c] == 0:
                                pe.wait_ge(*kq_lo(i1))
                            spread_kq("kb", 0, K_AT[c])
                        if c in S_AT:
                            spread_kq("qb", 1, S_AT[c])
                        for e in range(E1):
                            if c == LAST_OF[e] + 1:
                                spread(("cw1", e), pick_e1[:, e, :], rows1[2 * H:, :])
                    if c == MT_AT and 0 in st.layers:
                        pe.wait_ge(*max_parts_made(i0))
                        bank = bank_for("mT")
                        for t in range(TILES):
                            ins = pe.matmul(bank[0:6 * H2, t * P:(t + 1) * P],
                                            max_parts[:, t, :, :, :].rearrange("p g c h -> p (g c h)"), ident_b[:, :],
                                            start=True, stop=True)
                        ins.then_inc(bank.full, 1)
                    if 0 in st.layers:
                        attention(c)
                    if 1 in st.layers:
                        if c == OT_AT:
                            pe.wait_ge(*read_added(i1))
                            turn("oT", lambda t: o_acc[:, t * P:(t + 1) * P])
                        if c == NT_AT:
                            pe.wait_ge(*use["oT"].released(st))
                            turn("nT", lambda t: on1[:, t, :])
                    if c == AT_AT and 0 in st.layers:
                        pe.wait_ge(*use["on", GROUPS - 1].released(st))
                        turn("aT", lambda t: attn[:, t, :])
                    if 1 in st.layers and c >= LAG:
                        down1(c - LAG)

                def add_up(name, y, parts, layer, col):
                    bank = bank_for(name)
                    for t in range(TILES):
                        dst = bank[:, t * P:(t + 1) * P]
                        pe.matmul(dst, y[:, t * P:(t + 1) * P], ident[:, :], start=True, stop=False)
                        ins = three(dst, cols(parts, t), w(layer, col), start=False)
                    ins.then_inc(bank.full, 1)

                if 1 in st.layers:
                    pe.wait_ge(*ye_added(i1))
                    pe.wait_ge(*o_lo(i1))
                    add_up("out1", y_acc, (oh, ol), 1, W1_O)
                if 0 in st.layers:
                    pe.wait_ge(*use["aT"].released(st))
                    pe.wait_ge(*use["y0"].released(st))
                    add_up("out0", y0, (ah, al), 0, W0_M)

            run_steps(pe, step)


_INS = ['L0_attn_x', 'L0_attn_Wq', 'L0_attn_bq', 'L0_attn_Wk', 'L0_attn_bk', 'L0_attn_Wv', 'L0_attn_bv',
        'L0_attn_Wm', 'L0_attn_bm', 'L0_ffn_Wr', 'L0_ffn_Wg', 'L0_ffn_Wu', 'L0_ffn_Wd', 'L0_ffn_Sg', 'L0_ffn_Su',
        'L0_ffn_Sd', 'L1_attn_Wq', 'L1_attn_Wk', 'L1_attn_Wv', 'L1_attn_Wbeta', 'L1_attn_Wg', 'L1_attn_Wout',
        'L1_attn_ln_g', 'L1_attn_ln_b', 'L1_ffn_gate_w', 'L1_ffn_w1', 'L1_ffn_w2', 'L1_ffn_w3']


def kernel(**inputs):
    import numpy as _np
    import concourse.bacc as _bacc
    from concourse import mybir as _mybir
    from concourse.bass_utils import run_bass_kernel_spmd as _run

    nc = _bacc.Bacc("TRN2", target_bir_lowering=False, num_devices=1)
    arrays, args = {}, []
    for name in _INS:
        a = _np.ascontiguousarray(inputs[name])
        arrays[f"in_{name}_dram"] = a
        args.append(nc.dram_tensor(f"in_{name}_dram", a.shape, _mybir.dt.from_np(a.dtype), kind="ExternalInput").ap())
    shape = inputs['L0_attn_x'].shape
    args.append(nc.dram_tensor("out_0_dram", shape, _mybir.dt.from_np(_np.dtype("float32")),
                               kind="ExternalOutput").ap())
    two_layer_kernel(nc, *args)
    r = _run(nc, [arrays], core_ids=[0])
    return r.results[0]["out_0_dram"]
```

```python
from contextlib import ExitStack

import concourse.bass as bass
from concourse import mybir

ALU = mybir.AluOpType
ACT = mybir.ActivationFunctionType
AX = mybir.AxisListType
F32 = mybir.dt.float32
F32R = mybir.dt.float32r
BF16 = mybir.dt.bfloat16

P = 128
C = 512
S = 256
TILES = C // P
H = 16
HD = 8
H2 = H // 2
E0, F0 = 16, 64
E1, F1 = 4, 704
LN_EPS = 1e-5
SCORE_SCALE = float(HD) ** -0.5
MASKED = -1e30

NF0 = E0 * F0 // P + 1
NF1 = E1 * F1 // P
NPAIR = 2 * H2

W0_Q, W0_K, W0_V, W0_M, W0_SG, W0_SU, W0_G = (P * n for n in range(7))
W0_U = W0_G + E0 * F0
W0_R = W0_U + E0 * F0
W0_COLS = W0_R + E0
W1_Q, W1_K, W1_V, W1_G, W1_O, W1_1 = (P * n for n in range(6))
W1_3 = W1_1 + E1 * F1
W1_R = W1_3 + E1 * F1
R1 = H + E1
W1_COLS = W1_R + R1
STAGE, STAGES = 768, 4

SLOTS = [(0, 2), (0, 1), (0, 0), (1, 0), (2, 0), (1, 1)]
NSLOTS = len(SLOTS)
PART_SLOTS = [[slice(0, 3), slice(3, 6, 2), slice(4, 5)], [slice(2, 5), slice(1, 6, 4), slice(0, 1)]]
QK_ROWS = HD * len(SLOTS)
ST_ROWS = QK_ROWS + 3

OWNERS = []
for _c in range(NF1):
    _lo, _hi = _c * P, (_c + 1) * P
    OWNERS.append([(e, max(_lo, e * F1) - _lo, min(_hi, (e + 1) * F1) - _lo)
                   for e in range(E1) if max(_lo, e * F1) < min(_hi, (e + 1) * F1)])
LAST_OF = [max(c for c in range(NF1) if any(o[0] == e for o in OWNERS[c])) for e in range(E1)]
FIRST_OF = [min(c for c in range(NF1) if any(o[0] == e for o in OWNERS[c])) for e in range(E1)]

CHUNK_AT = {**{c: (0, c) for c in range(NF0)}, **{NF0 + c: (1, c) for c in range(NF1)}}
LAG = 2
SLOT_COUNT = NF0 + NF1 + LAG
X1_AT, SS_AT, EXP_AT, TOP1_AT, CWT1_AT, BETA_AT = 2, 4, 5, 8, 10, 11
PROJ1_AT = {3: ('r1', 'k1'), 4: ('q1',), 5: ('v1',), 8: ('gate1',)}
Y0_AT = NF0 + LAG
MAX_AT = {1: (0, 1), 2: (2, 3), 3: (4, 5), 4: (6, 7), 5: (8, 9), 6: (10,), 9: (11,), 11: (12, 13), 13: (14,), 15: (15,)}
SPLIT_AT, MT_AT = 15, 16
GROUPS = 4
ST_AT = {18: 0, 19: 1, 20: 2, 21: 3, 22: 4, 23: 5, 24: 6, 25: 7}
PV_AT = {s + 1: n for s, n in ST_AT.items()}
ON_AT = {s + 2: n // 2 for s, n in ST_AT.items() if n % 2}
K_AT = {12 + 2 * j: j for j in range(HD)}
S_AT = {13 + 2 * j: j for j in range(HD)}
CW1_AT = [NF0 + c + 1 for c in LAST_OF[:-1]] + [29]
WEIGHTED1_AT = [NF0 + c + LAG + 1 for c in LAST_OF]
LN2_AT, NT_AT, OF_AT, AT_AT = 27, 29, 31, 30
LN0_AT, X0_AT, Q0_AT, K0_AT, TOP0_AT, V0_AT, CWT0_AT = 23, 25, 26, 27, 29, 28, 30
TANH_CHUNKS = [s - NF0 for s in range(min(ST_AT), min(Q0_AT + 2, NF0 + NF1))]



def spare_bank(s):
    def free(n):
        return all(s + 1 < NF0 + FIRST_OF[e] + LAG or s > WEIGHTED1_AT[e] for e in range(n, E1, 2))

    return "Y0" if free(0) else "Y1" if free(1) else "F"


def bank_uses():
    for s in range(SLOT_COUNT):
        if s in K_AT:
            yield "X", ("kb", K_AT[s]), 1, 1
        if s in S_AT:
            yield "X", ("qb", S_AT[s]), 1, 1
        for m in MAX_AT.get(s, ()):
            spare = "Y1" if Y0_AT < s < NF0 + FIRST_OF[1] + LAG else "X"
            yield from (((spare, "X")[g], ("max", m, g), 0, 1) for g in range(2))
        if s in CHUNK_AT:
            layer, c = CHUNK_AT[s]
            yield from (("F", (f"{n}{layer}", c), layer, 1) for n in "gu")
        if 1 <= s < NF0:
            yield "Y0", ("cw0", s - 1), 0, 1
        names = (s == X1_AT) * ("xT1",) + PROJ1_AT.get(s, ()) + (s == SS_AT) * ("ss0", "ss1")
        names += (s == CWT1_AT) * ("cwT1",) + (s == BETA_AT) * ("beta",)
        yield from (("F", n, 1, 1) for n in names)
        for e in range(E1):
            if s == CW1_AT[e]:
                yield "F", ("cw1", e), 1, 1
        if s == LAG:
            yield "Y1", "y0", 0, 0
        for e in range(E1):
            if s == NF0 + FIRST_OF[e] + LAG:
                yield f"Y{e % 2}", ("y1", e), 1, 0
        if s == MT_AT:
            yield "F", "mT", 0, 1
        if s in PV_AT and PV_AT[s] % 2 == 0:
            yield spare_bank(s), ("pv", PV_AT[s] // 2), 0, 0
        if s in ON_AT:
            yield "F", ("on", ON_AT[s]), 0, 1
        if s in ST_AT:
            yield from (("X", ("st", ST_AT[s], h), 0, 1) for h in range(4))
        if s == LN2_AT:
            yield "X", "oT", 1, 1
        if s == NT_AT:
            yield "F", "nT", 1, 1
        if s == AT_AT:
            yield "F", "aT", 0, 1
        names = (s == X0_AT) * ("xT0",) + (s == Q0_AT) * ("r0", "q0") + (s == K0_AT) * ("k0",)
        names += (s == V0_AT) * ("v0",) + (s == CWT0_AT) * ("cwT0",)
        yield from (("F", n, "start", 1) for n in names)
    yield "F", "out0", 0, 1
    yield "F", "out1", 1, 1


class Step:

    def __init__(self, kind, m, chunks):
        self.kind = kind
        self.parts = {"start": ("start",), "first": (0, "start"), "both": (0, 1, "start"), "both_end": (0, 1),
                      "last": (1,)}[kind]
        self.i0 = m + 1 if kind in ("both", "both_end") else 0
        self.i1 = m
        self.i2 = self.i0 + 1 if kind != "start" else 0
        self.m = m

    def before(self, counts):
        start = counts["start"]
        if self.kind == "start":
            return 0
        if self.kind == "first":
            return start
        n = self.m * sum(counts.values()) + 2 * start + counts[0]
        return n - start if self.kind == "last" else n


class Signal:

    def __init__(self, sem, per, unit=1, ahead=0):
        self.sem, self.per, self.unit, self.ahead = sem, per, unit, ahead

    def __call__(self, i, k=None):
        k = self.per if k is None else k
        return self.sem, i * (self.per * self.unit) + (k + self.ahead) * self.unit


class Bank:

    def __init__(self, tile, full, free):
        self.tile, self.full, self.free = tile, full, free
        self.uses = []

    def at(self, step, name):
        here = [u for u in self.uses if u[1] in step.parts]
        k = [u[0] for u in here].index(name)
        uses = {part: sum(u[1] == part for u in self.uses) for part in ("start", 0, 1)}
        fills = {part: sum(u[2] for u in self.uses if u[1] == part) for part in ("start", 0, 1)}
        return step.before(uses) + k, step.before(fills) + sum(u[2] for u in here[:k])


class Use:

    def __init__(self, bank, name):
        self.bank, self.name = bank, name
        self.full, self.free = bank.full, bank.free

    def __getitem__(self, key):
        return self.bank.tile[key]

    def empty(self, step):
        return self.free, self.bank.at(step, self.name)[0] + 1

    def filled(self, step):
        return self.full, self.bank.at(step, self.name)[1] + 1

    def released(self, step):
        return self.free, self.bank.at(step, self.name)[0] + 2


def two_layer_kernel(nc, x, Wq0, bq0, Wk0, bk0, Wv0, bv0, Wm0, bm0, Wr0, Wg0, Wu0, Wd0, Sg0, Su0, Sd0,
                     Wq1, Wk1, Wv1, Wbeta1, Wgate1, Wout1, ln_g1, ln_b1, gate_w1, w1, w2, w3, out):
    tokens = x.shape[0] * x.shape[1]
    NCH = tokens // C
    x_chunks = x.rearrange("b s d -> (b s) d").rearrange("(n t p) d -> n p t d", t=TILES, p=P)
    out_chunks = out.rearrange("b s d -> (b s) d").rearrange("(n t p) d -> n p t d", t=TILES, p=P)
    max_dram = nc.dram_tensor("max_dram", (6 * H2, C), BF16).ap()
    qk_dram = nc.dram_tensor("qk_dram", (2, NSLOTS, P, C), BF16).ap()

    ctx = ExitStack()
    with ctx:
        def sb(name, shape, dt=F32):
            return ctx.enter_context(nc.sbuf_tensor(name, shape, dt))

        def sem(name):
            return ctx.enter_context(nc.semaphore(name))

        def signal(name, per, unit=1, ahead=0):
            return Signal(sem(name), per, unit, ahead)

        w0h, w0l = sb("w0h", [P, W0_COLS], F32R), sb("w0l", [P, W0_COLS], F32R)
        w1h, w1l = sb("w1h", [P, W1_COLS], F32R), sb("w1l", [P, W1_COLS], F32R)
        wd0 = sb("wd0", [P, NF0, P])
        wd1 = sb("wd1", [P, NF1, P])
        bias0 = sb("bias0", [P, 3])
        bm_rows = sb("bm_rows", [P, P])
        ln1 = sb("ln1", [P, 2])
        ident = sb("ident", [P, P])
        ident_b = sb("ident_b", [P, P], BF16)
        causal = sb("causal", [P, 2, P], BF16)
        same_head = sb("same_head", [P, P])
        pick = sb("pick", [P, HD, P], F32R)
        head_of = sb("head_of", [P, H])
        part_row = sb("part_row", [2 * H, H])
        pick_e = sb("pick_e", [2 * H + 2 * E1, NF0 - 1, P], F32R)
        pick_e0, pick_e1 = pick_e[0:2 * H, :, :], pick_e[2 * H:, 0:E1, :]
        pick_h = sb("pick_h", [2 * H, P], F32R)
        mhalf = sb("mhalf", [P, TILES])

        xin = sb("xin", [P, TILES, P])
        xres = sb("xres", [P, TILES, P])
        xh0, xl0 = sb("xh0", [P, C], F32R), sb("xl0", [P, C], F32R)
        qk_parts = sb("qk_parts_sb", [P, 2, 3, C], BF16)
        rest = sb("rest", [P, 2, C])
        Q = sb("Q", [P, H2, C], BF16)
        K = sb("K", [P, H2, C], BF16)
        V = sb("V", [P, TILES, H, HD + 1])
        row_max = sb("row_max", [P, 2, H2, 2, 3])
        neg_max = sb("neg_max", [P, TILES, 2, H2])
        max_rest = sb("max_rest", [P, TILES, 2, H2])
        max_parts = sb("max_parts", [P, TILES, 2, 3, H2], BF16)
        probs = sb("probs", [P, 2, 4, 3 * P])
        stage = probs[:, :, :, :].rearrange("p b h t -> p (b h t)")[:, 0:STAGES * STAGE]\
            .rearrange("p (n c) -> p n c", n=STAGES)
        rden = sb("rden", [P, TILES, 4])
        attn = sb("attn", [P, TILES, P])
        max_rows = rest[0:6 * H2, 0, :].bitcast(BF16)[:, 0:C]
        rows = sb("rows", [2 * H + 2 * E1, C], F32R)
        rows0, rows1 = rows[0:2 * H, :], rows[:, :]
        ug = rest
        heads_out = rest[:, 0, :]
        qk_left = rest[:, 1, :]
        y0 = sb("y0", [P, C])

        stat = [sb(f"stat{n}", [P, TILES, 6]) for n in range(2)]
        mv = [sb(f"mv{n}", [P, TILES, 2]) for n in range(2)]
        veps = [sb(f"veps{n}", [P, TILES]) for n in range(2)]
        rstd = [sb(f"rstd{n}", [P, TILES]) for n in range(2)]
        top_max = sb("top_max", [P, TILES])
        shifted = sb("shifted", [P, TILES, E0])
        ex0 = sb("ex0", [P, TILES, E0 + 8])
        ex1 = sb("ex1", [P, TILES, E1 + 8])
        rest0 = sb("rest0", [P, TILES, E0 + 6])
        rest1 = sb("rest1", [P, TILES, E1 + 6])
        top8 = sb("top8", [P, TILES, 8])
        ex_sum = sb("ex_sum", [P, TILES])
        cw = sb("cw", [P, TILES, E0])
        narrow = sb("narrow", [P, TILES, 2 * H + 2 * E1], F32R)
        gated = sb("gated", [P, 2, C])
        hid = sb("hid", [P, 3, C])

        x1 = sb("x1", [P, TILES, P])
        x1_kept = sb("x1_kept", [P, TILES, P])
        x1n = sb("x1n", [P, TILES, P])
        xh1, xl1 = sb("xh1", [P, C], F32R), sb("xl1", [P, C], F32R)
        eb = sb("eb", [P, TILES, H])
        beta = sb("beta", [P, TILES, H])
        sq = sb("sq", [P, 2, C])
        kq = sb("kq", [P, 2, C])
        kqh, kql = sb("kqh", [P, 2, C], F32R), sb("kql", [P, 2, C], F32R)
        nbk = sb("nbk", [P, C])
        bv = sb("bv", [P, C])
        gate = sb("gate", [P, C])
        decay = sb("decay", [P, 2, 2, S])
        write_in = sb("write_in", [P, C])
        state = sb("state", [P, C])
        read, o_acc = kq[:, 0, :], kq[:, 1, :]
        x2 = state[:, :].rearrange("p (t d) -> p t d", t=TILES)
        on1 = x1n
        og = nbk
        oh, ol = kqh[:, 0, :], kql[:, 0, :]
        ah, al = kqh[:, 1, :], kql[:, 1, :]
        ye, y_acc = sq[:, 0, :], sq[:, 1, :]
        x1n_used = x1n[:, :, :].rearrange("p t d -> p (t d)")
        cw1 = [x1n_used] * (E1 - 1) + [write_in[:, :]]

        size = {"F": 4, "X": 2, "Y0": 1, "Y1": 1}
        ring_banks = {}
        for ring, n in size.items():
            for b in range(n):
                name = f"{ring}{b}"
                tile = ctx.enter_context(nc.psum_tensor(name, [P, C], F32))
                ring_banks[ring, b] = Bank(tile, sem(name + "_full"), sem(name + "_free"))
        use, seen = {}, dict.fromkeys(size, 0)
        for ring, name, layer, parts in bank_uses():
            bank = ring_banks[ring, seen[ring] % size[ring]]
            seen[ring] += 1
            bank.uses.append((name, layer, parts))
            use[name] = Use(bank, name)

        staged = [sem(f"staged{n}") for n in range(STAGES)]
        hi_made, lo_made = sem("hi_made"), sem("lo_made")
        loaded, consts, consts_v = sem("loaded"), sem("consts"), sem("consts_v")
        x_loaded = signal("x_loaded", 1, 16)
        res_loaded = signal("res_loaded", 1, 16)
        qk_saved = signal("qk_saved", 6, 16)
        qk_packed = signal("qk_packed", 4, 16)
        max_saved = signal("max_saved", 1, 16)
        max_packed = signal("max_packed", 2, 16)
        x_plus_bm = signal("x_plus_bm", 1)
        part1 = signal("part1", 2)
        part2 = signal("part2", 2)
        part3 = signal("part3", 2)
        max_parts_made = signal("max_parts_made", 1)
        probs_masked = signal("probs_masked", 4 * GROUPS)
        values_weighted = signal("values_weighted", 2 * GROUPS)
        a_hi = signal("a_hi", 1)
        var_made = [signal(f"var_made{n}", 1) for n in range(3)]
        rstd_made = [signal(f"rstd_made{n}", 1) for n in range(3)]
        normed = [signal(f"normed{n}", 1) for n in range(2)]
        x_hi = [signal(f"x_hi{n}", 1) for n in range(2)]
        exp_made = [signal(f"exp_made{n}", 1) for n in range(2)]
        cw_made = [signal(f"cw_made{n}", 1) for n in range(2)]
        down_done = [signal("down_done0", NF0), signal("down_done1", NF1)]
        x_stored = signal("x_stored", 1, 16, ahead=1)
        x1_copied = signal("x1_copied", 1)
        tanh_made = signal("tanh_made", len(TANH_CHUNKS))
        beta_in = signal("beta_in", 1)
        beta_exp = signal("beta_exp", 1)
        ln_made = signal("ln_made", 1)
        rs_made = signal("rs_made", 1)
        kq_made = signal("kq_made", 1)
        kq_hi = signal("kq_hi", 1)
        kq_lo = signal("kq_lo", 1)
        decay_in_made = signal("decay_in_made", HD)
        decay_made = signal("decay_made", HD)
        read_added = signal("read_added", HD - 1)
        ye_added = signal("ye_added", E1 - 2)
        of_made = signal("of_made", 1)
        o_hi = signal("o_hi", 1)
        o_lo = signal("o_lo", 1)
        CHAIN = {"start": 11, 0: 11, 1: 23}
        dve_chain = sem("dve_chain")
        dve_held, pool_held, sp_held = sem("dve_held"), sem("pool_held"), sem("sp_held")

        def run_steps(engine, step):
            step(Step("start", 0, NCH))
            step(Step("first", 0, NCH))
            if NCH > 2:
                with engine.Fori(0, NCH - 2) as m:
                    step(Step("both", m, NCH))
            step(Step("both_end", NCH - 2, NCH))
            step(Step("last", NCH - 1, NCH))

        LOADS = 7 + 2 * HD
        by_dgh = "p (h g d) -> p d g h"

        def split_views(layer, col, source, part):
            part = part[layer][:, col:col + source.shape[1]]
            if layer == 0 and col in (W0_Q, W0_K):
                source = source.rearrange(by_dgh, g=2, d=HD)
                part = part.rearrange("p (d g h) -> p d g h", d=HD, g=2)
            return source, part

        pieces = []
        for W, col in ((Wq0, W0_Q), (Wk0, W0_K), (Wv0, W0_V), (Wm0, W0_M), (Sg0, W0_SG), (Su0, W0_SU)):
            pieces.append((W, P, 0, col))
        pieces.append((Wr0, E0, 0, W0_R))
        for e in range(0, E0, E0 // 2):
            for W, col in ((Wg0, W0_G), (Wu0, W0_U)):
                pieces.append((W[e:e + E0 // 2].rearrange("e d f -> d e f"), E0 // 2 * F0, 0, col + e * F0))
        for W, col in ((Wq1, W1_Q), (Wk1, W1_K), (Wv1, W1_V), (Wgate1, W1_G), (Wout1, W1_O)):
            pieces.append((W, P, 1, col))
        pieces.append((Wbeta1, H, 1, W1_R))
        pieces.append((gate_w1[0:E1, :].rearrange("e d -> d e"), E1, 1, W1_R + H))
        for e in range(E1):
            pieces.append((w1[e], F1, 1, W1_1 + e * F1))
            pieces.append((w3[e], F1, 1, W1_3 + e * F1))

        block = ctx.enter_context(nc.Block())

        @block.sync
        def _(sp):
            sp.dma_start(xin[:, :, :], x_chunks[0]).then_inc(x_loaded.sem, 16)
            for n, (src, width, _, _) in enumerate(pieces):
                if n >= STAGES:
                    sp.wait_ge(lo_made, n - STAGES + 1)
                dst = stage[:, n % STAGES, 0:width]
                if len(src.shape) == 3:
                    dst = dst.rearrange("p (e f) -> p e f", f=F0)
                sp.dma_start(dst, src, allow_slow_non_contiguous=width == E1).then_inc(staged[n % STAGES], 16)

            sp.sem_inc(x_stored.sem, 16)

            def step(st):
                i0, i1, i2 = st.i0, st.i1, st.i2
                if "start" in st.parts and st.kind != "start":
                    sp.sem_inc(sp_held, 1)
                    sp.dma_start(xin[:, :, :], x_chunks[i2]).then_inc(x_loaded.sem, 16)
                if 0 in st.parts:
                    sp.wait_ge(*use["mT"].released(st))
                    sp.dma_start(max_dram, max_rows).then_inc(max_saved.sem, 16)
                    sp.wait_ge(*max_saved(i0))
                    for g in range(2):
                        sp.dma_start(Q[64 * g + QK_ROWS:64 * g + ST_ROWS, :, :],
                                     max_dram.rearrange("(g p h) t -> g p h t", g=2, h=H2)[g])\
                          .then_inc(max_packed.sem, 16)
                if "start" in st.parts:
                    for a in range(2):
                        sp.wait_ge(*part3(i2, a + 1))
                        for part, slots in enumerate(PART_SLOTS[a]):
                            n = len(range(NSLOTS)[slots])
                            sp.dma_start(qk_dram[a, slots].rearrange("n c t -> c n t"),
                                         qk_parts[:, a, part, :].unsqueeze(1).to_broadcast([P, n, C]))\
                              .then_inc(qk_saved.sem, 16)
                    sp.wait_ge(*qk_saved(i2))
                    if 0 in st.parts:
                        sp.wait_ge(*use["st", 2 * GROUPS - 1, 3].filled(st))
                    for g in range(2):
                        for a, dst in enumerate((Q, K)):
                            sp.dma_start(dst[64 * g:64 * g + QK_ROWS, :, :],
                                         qk_dram[a].rearrange("n (d g h) t -> (n d) g h t", d=HD, g=2)[:, g]).then_inc(qk_packed.sem, 16)
                    if 0 in st.parts:
                        sp.wait_ge(*use["out0"].released(st))
                        sp.sem_inc(sp_held, 1)
                    sp.dma_start(xres[:, :, :], x_chunks[i2]).then_inc(res_loaded.sem, 16)
                if 1 in st.parts:
                    sp.wait_ge(*use["out1"].released(st))
                    sp.sem_inc(sp_held, 1)
                    sp.dma_start(out_chunks[i1], x2).then_inc(x_stored.sem, 16)

            run_steps(sp, step)
            sp.wait_ge(*x_stored(NCH - 1))

        @block.gpsimd
        def _(pool):
            pool.memset(ident[:, :], 0.0).then_inc(consts, 1)
            pool.memset(causal[:, :, :], 0.0).then_inc(consts, 1)
            pool.memset(mhalf[:, :], -0.5).then_inc(consts, 1)
            pool.memset(decay[:, :, :, :], 0.0).then_inc(consts, 1)
            pool.memset(V[:, :, :, :], 1.0).then_inc(consts, 1)
            pool.memset(K[:, :, :], 1.0).then_inc(consts, 1)
            pool.memset(ex0[:, :, :], -1.0).then_inc(consts, 1)
            pool.memset(ex1[:, :, :], -1.0).then_inc(consts, 1)
            pool.wait_ge(consts, 8)
            pool.affine_select(out=ident[:, :], in_=ident[:, :], compare_op=ALU.not_equal, fill=1.0,
                               base=0, pattern=[[-1, P]], channel_multiplier=1).then_inc(consts, 1)
            pool.affine_select(out=causal[:, :, :], in_=causal[:, :, :], compare_op=ALU.is_ge, fill=MASKED,
                               base=0, pattern=[[0, 2], [-1, P]], channel_multiplier=1).then_inc(consts, 1)
            for dst, src in ((bias0[:, 2:3], bv0),
                             (ln1[:, 0:1], ln_g1), (ln1[:, 1:2], ln_b1)):
                pool.dma_start(dst, src.rearrange("(p a) -> p a", a=1)).then_inc(loaded, 16)
            pool.dma_start(bm_rows[:, :], bm0.partition_broadcast(P)).then_inc(loaded, 16)
            pool.dma_start(wd0[:, 0:NF0 - 1, :], Wd0.rearrange("e f d -> (e f) d")
                           .rearrange("(c p) d -> p c d", p=P)).then_inc(loaded, 16)
            pool.dma_start(wd0[:, NF0 - 1, :], Sd0).then_inc(loaded, 16)
            pool.dma_start(wd1[:, :, :], w2[0:E1].rearrange("e f d -> (e f) d")
                           .rearrange("(c p) d -> p c d", p=P)).then_inc(loaded, 16)
            for a, src in enumerate((bq0, bk0)):
                for d in range(HD):
                    pool.dma_start(bias0[H * d:H * (d + 1), a:a + 1],
                                   src.rearrange("(h g d a) -> d g h a", g=2, d=HD, a=1)[d],
                                   allow_slow_non_contiguous=True).then_inc(loaded, 16)

            pool.wait_ge(loaded, 16 * LOADS)

            def rsqrt(n, i):
                pool.wait_ge(*var_made[n](i))
                pool.tensor_tensor(rstd[min(n, 1)][:, :], veps[min(n, 1)][:, :], mhalf[:, :], ALU.pow)\
                    .then_inc(rstd_made[n].sem, 1)

            def step(st):
                i0, i1, i2 = st.i0, st.i1, st.i2

                def mask_probs(n):
                    for k in range(0, 4, 2):
                        pool.wait_ge(*use["st", n, k + 1].released(st))
                        pool.sem_inc(pool_held, 1)
                        diag = probs[:, n % 2, k:k + 2, 0:2 * P]
                        pool.affine_select(out=diag, in_=diag, compare_op=ALU.is_ge, fill=0.0, base=0,
                                           pattern=[[0, 2], [0, 2], [1, P]], channel_multiplier=-1)\
                            .then_inc(probs_masked.sem, 1)

                def add_read(j):
                    pool.wait_ge(*use["qb", j].released(st))
                    if j > 1:
                        pool.wait_ge(*read_added(i1, j - 1))
                    pool.tensor_tensor(o_acc, o_acc, read, ALU.add).then_inc(read_added.sem, 1)

                def add_expert(e):
                    pool.wait_ge(*use["y1", e].released(st))
                    if e > 1:
                        pool.wait_ge(*ye_added(i1, e - 1))
                    pool.tensor_tensor(y_acc, y_acc, ye, ALU.add).then_inc(ye_added.sem, 1)

                if "start" in st.parts and st.kind == "start":
                    rsqrt(0, i2)
                if 1 in st.parts:
                    pool.wait_ge(*use["xT1"].released(st))
                    pool.sem_inc(pool_held, 1)
                    pool.tensor_copy(x1_kept[:, :, :], x1[:, :, :]).then_inc(x1_copied.sem, 1)
                if 0 in st.parts:
                    pool.wait_ge(*res_loaded(i0))
                    pool.tensor_tensor(xres[:, :, :], xres[:, :, :],
                                       bm_rows[:, :].unsqueeze(1).to_broadcast([P, TILES, P]), ALU.add)\
                        .then_inc(x_plus_bm.sem, 1)
                for s in range(SLOT_COUNT):
                    if 1 in st.parts:
                        if S_AT.get(s, 0) > 0:
                            add_read(S_AT[s])
                        for e in range(1, E1 - 1):
                            if s == WEIGHTED1_AT[e]:
                                add_expert(e)
                    if s in ST_AT and 0 in st.parts:
                        mask_probs(ST_AT[s])
                    if s == LN0_AT and "start" in st.parts and st.kind != "start":
                        rsqrt(0, i2)
                    if s == LN2_AT and 1 in st.parts:
                        rsqrt(2, i1)
                if 0 in st.parts:
                    rsqrt(1, i0)

            run_steps(pool, step)

        @block.scalar
        def _(act):
            for n, (_, width, layer, col) in enumerate(pieces):
                act.wait_ge(staged[n % STAGES], 16 * (n // STAGES + 1))
                source, hi = split_views(layer, col, stage[:, n % STAGES, 0:width], (w0h, w1h))
                act.activation(hi, source, ACT.Copy).then_inc(hi_made, 1)
            act.wait_ge(loaded, 16 * LOADS)
            act.wait_ge(consts, 10)

            def step(st):
                i0, i1, i2 = st.i0, st.i1, st.i2

                def hi_of_x(n):
                    act.wait_ge(*use[f"xT{n}"].filled(st))
                    act.activation((xh0, xh1)[n][:, :], use[f"xT{n}"][:, :], ACT.Copy).then_inc(x_hi[n].sem, 1)

                def start_next(s):
                    if s == X0_AT:
                        hi_of_x(0)
                    for a, name in ((0, "q0"), (1, "k0")):
                        if s == (Q0_AT, K0_AT)[a] + 1:
                            act.wait_ge(*use[name].released(st))
                            act.activation(qk_parts[:, a, 1, :], qk_left, ACT.Copy).then_inc(part2.sem, 1)
                    for a, name in ((0, "q0"), (1, "k0")):
                        if s == (Q0_AT, K0_AT)[a]:
                            act.wait_ge(*use[name].filled(st))
                            act.activation(qk_parts[:, a, 0, :], use[name][:, :], ACT.Identity,
                                           bias=bias0[:, a:a + 1]).then_inc(part1.sem, 1)
                    if s == V0_AT:
                        act.wait_ge(*use["v0"].filled(st))
                        act.activation(V[:, :, :, 0:HD],
                                       use["v0"][:, :].rearrange("p (t h d) -> p t h d", t=TILES, d=HD),
                                       ACT.Copy).then_inc(use["v0"].free, 1)
                    if s == CWT0_AT:
                        act.wait_ge(*use["cwT0"].filled(st))
                        act.activation(rows0, use["cwT0"][0:2 * H, :], ACT.Copy).then_inc(use["cwT0"].free, 1)

                def silu(s):
                    layer, c = CHUNK_AT[s]
                    g = use[f"g{layer}", c]
                    act.wait_ge(*g.filled(st))
                    if s >= 2 and CHUNK_AT[s - 2][0] in st.parts:
                        l2, c2 = CHUNK_AT[s - 2]
                        act.wait_ge(*use[f"u{l2}", c2].released(st))
                    if layer == 1 and c in TANH_CHUNKS:
                        act.activation(gated[:, s % 2, :], g[:, :], ACT.Tanh, scale=0.5).then_inc(tanh_made.sem, 1)
                    else:
                        act.activation(gated[:, s % 2, :], g[:, :], ACT.Silu).then_inc(g.free, 1)

                def norms_and_exps():
                    act.wait_ge(*use["ss1"].released(st))
                    act.activation(sq[:, :, :], sq[:, :, :], ACT.Ln).then_inc(ln_made.sem, 1)
                    act.wait_ge(*beta_in(i1))
                    act.activation(eb[:, :, :], eb[:, :, :], ACT.Exp, scale=-1.0).then_inc(beta_exp.sem, 1)
                    act.wait_ge(*use["r1"].released(st))
                    act.activation(ex1[:, :, 0:E1], shifted[:, :, 0:E1], ACT.Exp).then_inc(exp_made[1].sem, 1)
                    act.wait_ge(*ln_made(i1))
                    act.activation(sq[:, :, :], sq[:, :, :], ACT.Exp, scale=-0.5).then_inc(rs_made.sem, 1)

                def layer1_projections(s):
                    if s == X1_AT:
                        hi_of_x(1)
                    if "r1" in PROJ1_AT.get(s, ()):
                        r = use["r1"]
                        act.wait_ge(*r.filled(st))
                        act.activation(eb[:, :, :], r[:, 0:TILES * R1].rearrange("p (t r) -> p t r", r=R1)[:, :, 0:H],
                                       ACT.Copy).then_inc(beta_in.sem, 1)
                    for a, name in enumerate(("k1", "q1")):
                        if name in PROJ1_AT.get(s, ()):
                            act.wait_ge(*use[name].filled(st))
                            act.activation(kq[:, a, :], use[name][:, :], ACT.Copy)
                            act.activation(sq[:, a, :], use[name][:, :], ACT.Square).then_inc(use[name].free, 1)
                    if "v1" in PROJ1_AT.get(s, ()):
                        act.wait_ge(*use["v1"].filled(st))
                        act.activation(bv[:, :], use["v1"][:, :], ACT.Copy).then_inc(use["v1"].free, 1)
                    if "gate1" in PROJ1_AT.get(s, ()):
                        act.wait_ge(*use["gate1"].filled(st))
                        act.activation(gate[:, :], use["gate1"][:, :], ACT.Silu).then_inc(use["gate1"].free, 1)
                    if s == TOP1_AT:
                        act.wait_ge(*kq_made(i1))
                        act.activation(kqh[:, :, :], kq[:, :, :], ACT.Copy).then_inc(kq_hi.sem, 1)
                    if s == CWT1_AT:
                        act.wait_ge(*use["cwT1"].filled(st))
                        act.activation(rows1, use["cwT1"][0:2 * H + 2 * E1, :], ACT.Copy)\
                           .then_inc(use["cwT1"].free, 1)

                def grow_decay(j):
                    act.wait_ge(*decay_in_made(i1, j + 1))
                    d = decay[:, j % 2, :, 1:S]
                    act.activation(d, d, ACT.Identity, bias=1.0).then_inc(decay_made.sem, 1)

                def exp_scores(n):
                    if n >= 2:
                        act.wait_ge(*values_weighted(i0, n - 1))
                    for k in range(4):
                        bank = use["st", n, k]
                        act.wait_ge(*bank.filled(st))
                        act.activation(probs[:, n % 2, k, :], bank[:, 0:3 * P], ACT.Exp,
                                       scale=SCORE_SCALE).then_inc(bank.free, 1)

                for s in range(SLOT_COUNT):
                    if s == EXP_AT and 1 in st.parts:
                        norms_and_exps()
                    if s in CHUNK_AT and CHUNK_AT[s][0] in st.parts:
                        silu(s)
                    if s == Q0_AT + 1 and "start" in st.parts:
                        act.wait_ge(*use["r0"].released(st))
                        act.activation(ex0[:, :, 0:E0], shifted[:, :, :], ACT.Exp).then_inc(exp_made[0].sem, 1)
                    if 0 in st.parts:
                        if s == Y0_AT:
                            act.wait_ge(*down_done[0](i0))
                            act.activation(y0[:, :], use["y0"][:, :], ACT.Copy).then_inc(use["y0"].free, 1)
                        if s == MT_AT:
                            act.wait_ge(*use["mT"].filled(st))
                            act.activation(max_rows, use["mT"][0:6 * H2, :], ACT.Copy).then_inc(use["mT"].free, 1)
                    if 1 in st.parts:
                        layer1_projections(s)
                        if s in K_AT:
                            grow_decay(K_AT[s])
                        for e in range(E1):
                            if s == CW1_AT[e]:
                                if e >= 1:
                                    act.wait_ge(*use["y1", e - 1].released(st))
                                act.wait_ge(*use["cw1", e].filled(st))
                                act.activation(cw1[e], use["cw1", e][:, :], ACT.Copy).then_inc(use["cw1", e].free, 1)
                        if s == NT_AT:
                            act.wait_ge(*use["nT"].filled(st))
                            act.activation(og[:, :], use["nT"][:, :], ACT.Identity, scale=ln1[:, 0:1],
                                           bias=ln1[:, 1:2]).then_inc(use["nT"].free, 1)
                    if s in ST_AT and 0 in st.parts:
                        exp_scores(ST_AT[s])
                    if PV_AT.get(s, 0) % 2 and 0 in st.parts:
                        n = PV_AT[s] // 2
                        act.wait_ge(*values_weighted(i0, 2 * n + 2))
                        if n >= 1:
                            act.wait_ge(*use["on", n - 1].filled(st))
                        act.activation(heads_out, use["pv", n][:, :], ACT.Copy)\
                           .then_inc(use["pv", n].free, 1)
                    if s == OF_AT and 1 in st.parts:
                        act.wait_ge(*of_made(i1))
                        act.activation(oh, og[:, :], ACT.Copy).then_inc(o_hi.sem, 1)
                    if s == AT_AT and 0 in st.parts:
                        act.wait_ge(*use["aT"].filled(st))
                        act.activation(ah, use["aT"][:, :], ACT.Identity, bias=bias0[:, 2:3]).then_inc(a_hi.sem, 1)
                    if "start" in st.parts:
                        start_next(s)

            run_steps(act, step)

        @block.vector
        def _(dve):
            for n, (_, width, layer, col) in enumerate(pieces):
                dve.wait_ge(hi_made, n + 1)
                source, lo = split_views(layer, col, stage[:, n % STAGES, 0:width], (w0l, w1l))
                _, hi = split_views(layer, col, stage[:, n % STAGES, 0:width], (w0h, w1h))
                dve.tensor_tensor(lo, source, hi, ALU.subtract).then_inc(lo_made, 1)
            dve.wait_ge(consts, 10)
            dve.tensor_copy(ident_b[:, :], ident[:, :]).then_inc(consts_v, 1)
            by_d = ident[:, :].rearrange("p (h d) -> p d h", d=HD)
            for j in range(HD):
                dve.tensor_copy(pick[:, j, :].rearrange("p (h i) -> p h i", i=HD),
                                by_d[:, j, :].unsqueeze(2).to_broadcast([P, H, HD])).then_inc(consts_v, 1)
            dve.reduce_sum(head_of[:, :], ident[:, :].rearrange("p (h d) -> p h d", d=HD), AX.X).then_inc(consts_v, 1)
            dve.wait_ge(consts_v, 2 + HD)
            dve.tensor_copy(same_head[:, :].rearrange("p (h i) -> p h i", i=HD),
                            head_of[:, :].unsqueeze(2).to_broadcast([P, H, HD])).then_inc(consts_v, 1)
            dve.tensor_tensor(part_row[:, :], ident[0:2 * H, 0:H], ident[0:2 * H, H:2 * H], ALU.add).then_inc(consts_v, 1)
            dve.wait_ge(consts_v, 4 + HD)
            dve.tensor_copy(pick_e0.rearrange("r c (k m) -> r c k m", k=2),
                            part_row[:, :].rearrange("r (c k) -> r c k", k=2).unsqueeze(3)
                            .to_broadcast([2 * H, NF0 - 1, 2, P // 2])).then_inc(consts_v, 1)
            dve.tensor_copy(pick_h[:, :].rearrange("r (h i) -> r h i", i=HD),
                            part_row[:, :].unsqueeze(2).to_broadcast([2 * H, H, HD])).then_inc(consts_v, 1)
            at = slice(2 * H, 2 * H + 2 * E1)
            dve.tensor_tensor(pick_e1,
                              ident[at, 2 * H:2 * H + E1].unsqueeze(2).to_broadcast([2 * E1, E1, P]),
                              ident[at, 2 * H + E1:2 * H + 2 * E1].unsqueeze(2).to_broadcast([2 * E1, E1, P]),
                              ALU.add).then_inc(consts_v, 1)
            dve.wait_ge(loaded, 16 * LOADS)

            def step(st):
                i0, i1, i2 = st.i0, st.i1, st.i2
                chain = [0]

                def link(ins):
                    chain[0] += 1
                    ins.then_inc(dve_chain, 1)
                    dve.wait_ge(dve_chain, st.before(CHAIN) + chain[0])

                def stand_alone():
                    dve.sem_inc(dve_held, 1)

                def variance(n, src):
                    w = min(n, 1)
                    for t in range(TILES):
                        ins = dve.bn_stats(stat[w][:, t, :], src[:, t, :])
                    link(ins)
                    stand_alone()
                    for t in range(TILES):
                        ins = dve.bn_aggr(mv[w][:, t, :], stat[w][:, t, :])
                    link(ins)
                    dve.tensor_scalar(veps[w][:, :], mv[w][:, :, 1], LN_EPS, None, ALU.add).then_inc(var_made[n].sem, 1)

                def normalise(n, i, dst, src):
                    w = min(n, 1)
                    dve.wait_ge(*rstd_made[n](i))
                    for t in range(TILES):
                        ins = dve.tensor_scalar(dst[:, t, :], src[:, t, :], mv[w][:, t, 0:1], rstd[w][:, t:t + 1],
                                                ALU.subtract, ALU.mult)
                    return ins

                def lo_of_x(n, i):
                    dve.wait_ge(*x_hi[n](i))
                    dve.tensor_tensor((xl0, xl1)[n][:, :], use[f"xT{n}"][:, :], (xh0, xh1)[n][:, :], ALU.subtract)\
                       .then_inc(use[f"xT{n}"].free, 1)

                def shift_logits(logits, experts):
                    link(dve.reduce_max(top_max[:, :], logits, AX.X))
                    return dve.tensor_tensor(shifted[:, :, 0:experts], logits,
                                             top_max[:, :].unsqueeze(2).to_broadcast([P, TILES, experts]),
                                             ALU.subtract)

                def top_two(ex, rest, experts):
                    stand_alone()
                    for t in range(TILES):
                        ins = dve.max(top8[:, t, :], ex[:, t, 0:experts + 6])
                    link(ins)
                    link(dve.memset(top8[:, :, 2:8], -1.0))
                    stand_alone()
                    for t in range(TILES):
                        ins = dve.match_replace(out=rest[:, t, :], in_to_replace=top8[:, t, :],
                                                in_values=ex[:, t, 0:experts + 6], imm_value=0.0)
                    link(ins)
                    link(dve.tensor_tensor(cw[:, :, 0:experts], ex[:, :, 0:experts], rest[:, :, 0:experts],
                                           ALU.subtract))

                def parts_of(values, at, width):
                    link(dve.tensor_copy(narrow[:, :, at:at + width], values))
                    return dve.tensor_tensor(narrow[:, :, at + width:at + 2 * width], values,
                                             narrow[:, :, at:at + width], ALU.subtract)

                def weigh(n, total_of, experts):
                    link(dve.reduce_sum(ex_sum[:, :], total_of, AX.X))
                    link(dve.reciprocal(ex_sum[:, :], ex_sum[:, :]))
                    link(dve.tensor_tensor(cw[:, :, 0:experts], cw[:, :, 0:experts],
                                           ex_sum[:, :].unsqueeze(2).to_broadcast([P, TILES, experts]), ALU.mult))
                    parts_of(cw[:, :, 0:experts], (0, 2 * H)[n], experts).then_inc(cw_made[n].sem, 1)

                def start_next(s):
                    if s == LN0_AT:
                        dve.wait_ge(*x_loaded(i2))
                        variance(0, xin)
                    if s == LN0_AT + 1:
                        normalise(0, i2, xin, xin).then_inc(normed[0].sem, 1)
                    if s == X0_AT:
                        lo_of_x(0, i2)
                    if s == Q0_AT:
                        dve.wait_ge(*use["r0"].filled(st))
                        shift_logits(use["r0"][:, 0:TILES * E0].rearrange("p (t e) -> p t e", e=E0), E0)\
                            .then_inc(use["r0"].free, 1)
                    for a in range(2):
                        if s == (Q0_AT, K0_AT)[a] + 1:
                            dve.wait_ge(*part2(i2, a + 1))
                            dve.tensor_tensor(qk_parts[:, a, 2, :], qk_left, qk_parts[:, a, 1, :], ALU.subtract)\
                               .then_inc(part3.sem, 1)
                    for a, name in enumerate(("q0", "k0")):
                        if s == (Q0_AT, K0_AT)[a]:
                            if a == 1:
                                dve.wait_ge(*part3(i2, 1))
                            dve.wait_ge(*part1(i2, a + 1))
                            dve.scalar_tensor_tensor(out=qk_left, in0=use[name][:, :],
                                                     scalar=bias0[:, a:a + 1], in1=qk_parts[:, a, 0, :],
                                                     op0=ALU.add, op1=ALU.subtract).then_inc(use[name].free, 1)
                    if s == TOP0_AT:
                        dve.wait_ge(*exp_made[0](i2))
                        top_two(ex0, rest0, E0)
                        weigh(0, ex0[:, :, 0:E0], E0)

                def hidden0(c):
                    g, u = use["g0", c], use["u0", c]
                    dve.wait_ge(*g.released(st))
                    dve.wait_ge(*u.filled(st))
                    if c == NF0 - 1:
                        dve.wait_ge(*down_done[0](i0, c - 2))
                    elif c >= 2:
                        dve.wait_ge(*use["cw0", c - 2].released(st))
                    else:
                        dve.wait_ge(*part3(i0))
                    dst = ug[:, c % 2, :] if c < NF0 - 1 else hid[:, c % 3, :]
                    dve.tensor_tensor(dst, u[:, :], gated[:, c % 2, :], ALU.mult).then_inc(u.free, 1)

                def weighted0(c):
                    dve.wait_ge(*use["u0", c].released(st))
                    dve.wait_ge(*use["cw0", c].filled(st))
                    if c >= 3:
                        dve.wait_ge(*down_done[0](i0, c - 2))
                    dve.tensor_tensor(hid[:, c % 3, :], use["cw0", c][:, :], ug[:, c % 2, :], ALU.mult)\
                       .then_inc(use["cw0", c].free, 1)

                def layer1_projections(s):
                    if s == X1_AT:
                        lo_of_x(1, i1)
                    if "r1" in PROJ1_AT.get(s, ()):
                        r = use["r1"]
                        dve.wait_ge(*r.filled(st))
                        dve.wait_ge(*beta_in(i1))
                        shift_logits(r[:, 0:TILES * R1].rearrange("p (t r) -> p t r", r=R1)[:, :, H:R1], E1)\
                            .then_inc(r.free, 1)
                    if s == SS_AT:
                        for a in range(2):
                            ss = use[f"ss{a}"]
                            dve.wait_ge(*ss.filled(st))
                            dve.tensor_scalar(sq[:, a, :], ss[:, :], 1e-24, None, ALU.max).then_inc(ss.free, 1)
                    if s == TOP1_AT - 1:
                        dve.wait_ge(*rs_made(i1))
                        dve.tensor_tensor(kq[:, :, :], kq[:, :, :], sq[:, :, :], ALU.mult).then_inc(kq_made.sem, 1)
                        dve.wait_ge(*beta_exp(i1))
                        link(dve.tensor_scalar(eb[:, :, :], eb[:, :, :], 1.0, None, ALU.add))
                        link(dve.reciprocal(beta[:, :, :], eb[:, :, :]))
                        link(parts_of(beta[:, :, :], 0, H))
                    if s == TOP1_AT:
                        dve.wait_ge(*exp_made[1](i1))
                        top_two(ex1, rest1, E1)
                        weigh(1, cw[:, :, 0:E1], E1)
                    if s == TOP1_AT + 1:
                        dve.wait_ge(*kq_hi(i1))
                        dve.tensor_tensor(kql[:, :, :], kq[:, :, :], kqh[:, :, :], ALU.subtract).then_inc(kq_lo.sem, 1)
                    if s == BETA_AT:
                        b = use["beta"]
                        dve.wait_ge(*b.filled(st))
                        dve.wait_ge(*kq_made(i1))
                        dve.scalar_tensor_tensor(out=nbk[:, :], in0=kq[:, 0, :], scalar=-1.0, in1=b[:, :],
                                                 op0=ALU.mult, op1=ALU.mult)
                        dve.wait_ge(*use["v1"].released(st))
                        dve.tensor_tensor(bv[:, :], bv[:, :], b[:, :], ALU.mult).then_inc(b.free, 1)

                def hidden1(c):
                    g, u = use["g1", c], use["u1", c]
                    s = NF0 + c
                    if c in TANH_CHUNKS:
                        dve.wait_ge(*tanh_made(i1, TANH_CHUNKS.index(c) + 1))
                        dve.scalar_tensor_tensor(out=gated[:, s % 2, :], in0=gated[:, s % 2, :], scalar=1.0,
                                                 in1=g[:, :], op0=ALU.add, op1=ALU.mult).then_inc(g.free, 1)
                    dve.wait_ge(*g.released(st))
                    dve.wait_ge(*u.filled(st))
                    if c >= 3:
                        dve.wait_ge(*down_done[1](i1, c - 2))
                    elif 0 in st.parts:
                        dve.wait_ge(*down_done[0](i0, NF0 + c - 2))
                    if c in TANH_CHUNKS:
                        dve.scalar_tensor_tensor(out=hid[:, s % 3, :], in0=gated[:, s % 2, :], scalar=0.5,
                                                 in1=u[:, :], op0=ALU.mult, op1=ALU.mult).then_inc(u.free, 1)
                    else:
                        dve.tensor_tensor(hid[:, s % 3, :], u[:, :], gated[:, s % 2, :], ALU.mult).then_inc(u.free, 1)

                def row_maxima(m):
                    b, h2 = divmod(m, H2)
                    for g in range(2):
                        bank = use["max", m, g]
                        dve.wait_ge(*bank.filled(st))
                        dve.tensor_reduce(row_max[:, b, h2, g, :], bank[:, 0:3 * P].rearrange("p (c t) -> p c t", t=P),
                                          AX.X, ALU.max).then_inc(bank.free, 1)

                def split_maxima():
                    dve.wait_ge(*use["max", NPAIR - 1, 1].released(st))
                    tiles = neg_max[:, :, :, :].rearrange("p (b q) g h -> p b q g h", q=2)
                    by_head = row_max[:, :, :, :, :].rearrange("p b h g c -> p b g h c")
                    link(dve.tensor_tensor(max_rest[:, 0:2, :, :], by_head[:, :, :, :, 1], by_head[:, :, :, :, 2],
                                           ALU.max))
                    for b in range(2):
                        dve.tensor_scalar(tiles[:, b, 0, :, :], by_head[:, b, :, :, 0], -1.0, None, ALU.mult)
                        ins = dve.tensor_scalar(tiles[:, b, 1, :, :], max_rest[:, b, :, :], -1.0, None, ALU.mult)
                    link(ins)
                    link(dve.tensor_copy(max_parts[:, :, :, 0, :], neg_max[:, :, :, :]))
                    link(dve.tensor_tensor(max_rest[:, :, :, :], neg_max[:, :, :, :], max_parts[:, :, :, 0, :],
                                           ALU.subtract))
                    link(dve.tensor_copy(max_parts[:, :, :, 1, :], max_rest[:, :, :, :]))
                    dve.tensor_tensor(max_parts[:, :, :, 2, :], max_rest[:, :, :, :], max_parts[:, :, :, 1, :],
                                      ALU.subtract).then_inc(max_parts_made.sem, 1)

                def delta_in(j):
                    kb = use["kb", j]
                    dve.wait_ge(*kb.filled(st))
                    if j == 0:
                        dve.wait_ge(*use["beta"].released(st))
                    halves = kb[:, :].rearrange("p (b s) -> p b s", s=S)
                    dve.tensor_tensor(decay[:, j % 2, :, 1:S], halves[:, :, 1:S],
                                      nbk[:, :].rearrange("p (b s) -> p b s", s=S)[:, :, 1:S], ALU.mult)\
                       .then_inc(decay_in_made.sem, 1)
                    dve.tensor_tensor(write_in[:, :], kb[:, :], bv[:, :], ALU.mult).then_inc(kb.free, 1)

                def delta_scan(j):
                    dve.wait_ge(*decay_made(i1, j + 1))
                    dve.wait_ge(*use["kb", j].released(st))
                    if j == 0:
                        dve.wait_ge(*x_stored(i1, 0))
                    link(dve.tensor_tensor_scan(state[:, :], decay[:, j % 2, :, :].rearrange("p b s -> p (b s)"),
                                                write_in[:, :], 0.0, ALU.mult, ALU.add))

                def delta_read(j):
                    qb = use["qb", j]
                    dve.wait_ge(*qb.filled(st))
                    if j >= 2:
                        dve.wait_ge(*read_added(i1, j - 1))
                    dve.tensor_tensor(o_acc if j == 0 else read, qb[:, :], state[:, :], ALU.mult)\
                       .then_inc(qb.free, 1)

                def weighted1(e):
                    dve.wait_ge(*down_done[1](i1, LAST_OF[e] + 1))
                    dve.wait_ge(*use["cw1", e].released(st))
                    if e >= 2:
                        dve.wait_ge(*ye_added(i1, e - 1))
                    dve.tensor_tensor(y_acc if e == 0 else ye, use["y1", e][:, :], cw1[e], ALU.mult)\
                       .then_inc(use["y1", e].free, 1)

                def normalise_heads(n):
                    on = use["on", n]
                    dve.wait_ge(*on.filled(st))
                    if n >= 1:
                        dve.wait_ge(*use["on", n - 1].released(st))
                    got = on[:, :].rearrange("p (t h c) -> p t h c", t=TILES, h=4)
                    link(dve.reciprocal(rden[:, :, :], got[:, :, :, HD]))
                    dve.tensor_tensor(attn[:, :, :].rearrange("p t (h d) -> p t h d", d=HD)[:, :, 4 * n:4 * n + 4, :],
                                      got[:, :, :, 0:HD], rden[:, :, :].unsqueeze(3).to_broadcast([P, TILES, 4, HD]),
                                      ALU.mult).then_inc(on.free, 1)

                for s in range(SLOT_COUNT):
                    if s in K_AT and 1 in st.parts:
                        delta_in(K_AT[s])
                    if s in S_AT and 1 in st.parts:
                        delta_scan(S_AT[s])
                        delta_read(S_AT[s])
                    if 1 <= s < NF0 and 0 in st.parts:
                        weighted0(s - 1)
                    if 0 in st.parts:
                        for m in MAX_AT.get(s, ()):
                            row_maxima(m)
                    if s in CHUNK_AT and CHUNK_AT[s][0] in st.parts:
                        (hidden0, hidden1)[CHUNK_AT[s][0]](CHUNK_AT[s][1])
                    if 0 in st.parts:
                        if s == SPLIT_AT:
                            split_maxima()
                        if s in ON_AT:
                            normalise_heads(ON_AT[s])
                    if 1 in st.parts:
                        layer1_projections(s)
                        for e in range(E1 - 1):
                            if s == WEIGHTED1_AT[e]:
                                weighted1(e)
                        oT = use["oT"]
                        turned = oT[:, :].rearrange("p (t d) -> p t d", t=TILES)
                        if s == LN2_AT:
                            dve.wait_ge(*oT.filled(st))
                            variance(2, turned)
                        if s == LN2_AT + 1:
                            dve.wait_ge(*use["y1", E1 - 2].released(st))
                            normalise(2, i1, on1, turned).then_inc(oT.free, 1)
                        if s == OF_AT:
                            dve.wait_ge(*use["gate1"].released(st))
                            dve.wait_ge(*use["nT"].released(st))
                            dve.tensor_tensor(og[:, :], og[:, :], gate[:, :], ALU.mult).then_inc(of_made.sem, 1)
                    if s == AT_AT + 1 and 0 in st.parts:
                        dve.wait_ge(*a_hi(i0))
                        dve.scalar_tensor_tensor(out=al, in0=use["aT"][:, :], scalar=bias0[:, 2:3], in1=ah,
                                                 op0=ALU.add, op1=ALU.subtract).then_inc(use["aT"].free, 1)
                    if s == OF_AT + 1 and 1 in st.parts:
                        dve.wait_ge(*o_hi(i1))
                        dve.tensor_tensor(ol, og[:, :], oh, ALU.subtract).then_inc(o_lo.sem, 1)
                    if "start" in st.parts:
                        start_next(s)
                if 1 in st.parts:
                    weighted1(E1 - 1)
                    dve.wait_ge(*x1_copied(i1))
                if 0 in st.parts:
                    out0 = use["out0"]
                    dve.wait_ge(*x_plus_bm(i0))
                    dve.wait_ge(*out0.filled(st))
                    dve.tensor_tensor(x1[:, :, :], out0[:, :].rearrange("p (t d) -> p t d", t=TILES), xres[:, :, :],
                                      ALU.add).then_inc(out0.free, 1)
                    dve.wait_ge(*out0.released(st))
                    variance(1, x1)
                    normalise(1, i0, x1n, x1).then_inc(normed[1].sem, 1)
                if 1 in st.parts:
                    out1 = use["out1"]
                    dve.wait_ge(*out1.filled(st))
                    dve.tensor_tensor(x2, out1[:, :].rearrange("p (t d) -> p t d", t=TILES), x1_kept[:, :, :],
                                      ALU.add).then_inc(out1.free, 1)
                assert chain[0] == sum(CHAIN[part] for part in st.parts), (st.kind, chain[0])

            run_steps(dve, step)

        @block.tensor
        def _(pe):
            pe.wait_ge(lo_made, len(pieces))
            pe.wait_ge(consts, 10)
            pe.wait_ge(consts_v, 7 + HD)
            pe.wait_ge(loaded, 16 * LOADS)

            def three(dst, left, right, start=True, stop=True):
                pe.matmul(dst, left[0], right[0], start=start, stop=False, skip_group_check=not start)
                pe.matmul(dst, left[1], right[0], start=False, stop=False, skip_group_check=not start)
                return pe.matmul(dst, left[0], right[1], start=False, stop=stop, skip_group_check=not start)

            def w(layer, col, width=P):
                hi, lo = ((w0h, w0l), (w1h, w1l))[layer]
                return hi[:, col:col + width], lo[:, col:col + width]

            def cols(pair, t):
                return pair[0][:, t * P:(t + 1) * P], pair[1][:, t * P:(t + 1) * P]

            X = ((xh0[:, :], xl0[:, :]), (xh1[:, :], xl1[:, :]))
            for bank in ring_banks.values():
                pe.sem_inc(bank.free, 1)

            def step(st):
                i0, i1, i2 = st.i0, st.i1, st.i2

                def bank_for(name):
                    pe.wait_ge(*use[name].empty(st))
                    return use[name]

                def turn(name, src):
                    bank = bank_for(name)
                    for t in range(TILES):
                        ins = pe.transpose(bank[:, t * P:(t + 1) * P], src(t), ident[:, :])
                    ins.then_inc(bank.full, 1)

                def project(name, layer, col):
                    bank = bank_for(name)
                    three(bank[:, :], w(layer, col), X[layer]).then_inc(bank.full, 1)

                def by_token(name, layer, col, width):
                    bank = bank_for(name)
                    for t in range(TILES):
                        ins = three(bank[:, t * width:(t + 1) * width], cols(X[layer], t), w(layer, col, width))
                    ins.then_inc(bank.full, 1)

                def turn_narrow(n, width):
                    pe.wait_ge(*cw_made[n]((i2, i1)[n]))
                    bank = bank_for(f"cwT{n}")
                    for t in range(TILES):
                        ins = pe.matmul(bank[0:width, t * P:(t + 1) * P], narrow[:, t, 0:width].bitcast(F32),
                                        ident[:, :], start=True, stop=True)
                    ins.then_inc(bank.full, 1)

                def spread(name, pick_rows, from_rows):
                    bank = bank_for(name)
                    pe.matmul(bank[:, :], pick_rows, from_rows, start=True, stop=True).then_inc(bank.full, 1)

                def down0(c):
                    if c < NF0 - 1:
                        pe.wait_ge(*use["cw0", c].released(st))
                    else:
                        pe.wait_ge(*use["u0", c].released(st))
                    y = use["y0"]
                    if c == 0:
                        pe.wait_ge(*y.empty(st))
                    pe.matmul(y[:, :], wd0[:, c, :], hid[:, c % 3, :], start=c == 0, stop=c == NF0 - 1)\
                      .then_inc(down_done[0].sem, 1)

                def layer1_projections(s):
                    if s == X1_AT:
                        pe.wait_ge(*normed[1](i1))
                        turn("xT1", lambda t: x1n[:, t, :])
                    if "r1" in PROJ1_AT.get(s, ()):
                        pe.wait_ge(*use["xT1"].released(st))
                        by_token("r1", 1, W1_R, R1)
                    for name, col in (("k1", W1_K), ("q1", W1_Q), ("v1", W1_V), ("gate1", W1_G)):
                        if name in PROJ1_AT.get(s, ()):
                            project(name, 1, col)
                    if s == SS_AT:
                        for a, name in enumerate(("k1", "q1")):
                            bank = bank_for(f"ss{a}")
                            pe.wait_ge(*use[name].released(st))
                            pe.matmul(bank[:, :], same_head[:, :], sq[:, a, :], start=True, stop=True)\
                              .then_inc(bank.full, 1)
                    if s == CWT1_AT:
                        turn_narrow(1, 2 * H + 2 * E1)
                    if s == BETA_AT:
                        pe.wait_ge(*use["cwT1"].released(st))
                        spread("beta", pick_h[:, :], rows1[0:2 * H, :])

                def start_next(s):
                    if s == X0_AT:
                        pe.wait_ge(*normed[0](i2))
                        turn("xT0", lambda t: xin[:, t, :])
                    if s == Q0_AT:
                        pe.wait_ge(*use["xT0"].released(st))
                        by_token("r0", 0, W0_R, E0)
                        project("q0", 0, W0_Q)
                    if s == K0_AT:
                        project("k0", 0, W0_K)
                    if s == V0_AT:
                        by_token("v0", 0, W0_V, P)
                    if s == CWT0_AT:
                        turn_narrow(0, 2 * H)

                def down1(c):
                    pe.wait_ge(*use["u1", c].released(st))
                    for e, lo, hi in OWNERS[c]:
                        y = use["y1", e]
                        if c == FIRST_OF[e]:
                            pe.wait_ge(*y.empty(st))
                        ins = pe.matmul(y[:, :], wd1[lo:hi, c, :], hid[lo:hi, (NF0 + c) % 3, :],
                                        start=c == FIRST_OF[e], stop=c == LAST_OF[e])
                    ins.then_inc(down_done[1].sem, 1)

                def spread_kq(name, a, j):
                    bank = bank_for((name, j))
                    pe.matmul(bank[:, :], pick[:, j, :], kqh[:, a, :], start=True, stop=False)
                    pe.matmul(bank[:, :], pick[:, j, :], kql[:, a, :], start=False, stop=True).then_inc(bank.full, 1)

                def score_rows(m, g):
                    b, h2 = divmod(m, H2)
                    q0 = b * S
                    q, k = Q[64 * g:64 * g + QK_ROWS, h2, :], K[64 * g:64 * g + QK_ROWS, h2, :]
                    bank = bank_for(("max", m, g))
                    pe.matmul(bank[:, 0:P], q[:, q0:q0 + P], k[:, q0:q0 + P], start=True, stop=False,
                              skip_group_check=True)
                    pe.matmul(bank[:, P:3 * P], q[:, q0 + P:q0 + S], k[:, q0:q0 + S], start=False, stop=False,
                              skip_group_check=True)
                    pe.matmul(bank[:, 0:3 * P].rearrange("p (c t) -> p c t", t=P)[:, 0:3:2, :], ident_b[:, :],
                              causal[:, :, :], start=False, stop=True, skip_group_check=True)\
                      .then_inc(bank.full, 1)

                def score_cols(n, c):
                    b, h = n % 2, 4 * (n // 2) + c
                    g, h2, q0 = h % 2, h // 2, b * S
                    bank = bank_for(("st", n, c))
                    q, k = Q[64 * g:64 * g + ST_ROWS, h2, :], K[64 * g:64 * g + ST_ROWS, h2, :]
                    pe.matmul(bank[:, 0:3 * P].rearrange("p (c t) -> p c t", t=P)[:, 0:3:2, :], k[:, q0:q0 + P],
                              q[:, q0:q0 + S], start=True, stop=True)
                    pe.matmul(bank[:, P:2 * P], k[:, q0 + P:q0 + S], q[:, q0 + P:q0 + S], start=True, stop=True)\
                      .then_inc(bank.full, 1)

                def score_pair(n, k):
                    score_cols(n, 2 * k)
                    score_cols(n, 2 * k + 1)

                def weigh_values(n):
                    b = n % 2
                    bank = bank_for(("pv", n // 2)) if b == 0 else use["pv", n // 2]
                    h = 4 * (n // 2)
                    for c in range(4):
                        if c % 2 == 0:
                            pe.wait_ge(*probs_masked(i0, 2 * n + c // 2 + 1))
                        pe.matmul(bank[32 * c:32 * c + HD + 1, b * S:(b + 1) * S], V[:, 2 * b, h + c, :],
                                  probs[:, b, c, :].rearrange("p (c t) -> p c t", t=P)[:, 0:3:2, :],
                                  start=True, stop=False, skip_group_check=True)
                    for c in range(4):
                        ins = pe.matmul(bank[32 * c:32 * c + HD + 1, b * S + P:(b + 1) * S],
                                        V[:, 2 * b + 1, h + c, :], probs[:, b, c, P:2 * P],
                                        start=False, stop=True, skip_group_check=True)
                    ins.then_inc(values_weighted.sem, 1)

                def up(s, name):
                    layer, c = CHUNK_AT[s]
                    if layer == 1:
                        col = {"g": W1_1, "u": W1_3}[name] + c * P
                    elif c < NF0 - 1:
                        col = {"g": W0_G, "u": W0_U}[name] + c * P
                    else:
                        col = {"g": W0_SG, "u": W0_SU}[name]
                    project((f"{name}{layer}", c), layer, col)

                def down(s):
                    layer, c = CHUNK_AT[s - LAG]
                    if layer in st.parts:
                        (down0, down1)[layer](c)

                def delta(s):
                    if s in K_AT:
                        if K_AT[s] == 0:
                            pe.wait_ge(*kq_lo(i1))
                        spread_kq("kb", 0, K_AT[s])
                    if s in S_AT:
                        spread_kq("qb", 1, S_AT[s])

                def turn_maxima():
                    pe.wait_ge(*max_parts_made(i0))
                    bank = bank_for("mT")
                    for t in range(TILES):
                        ins = pe.matmul(bank[0:6 * H2, t * P:(t + 1) * P],
                                        max_parts[:, t, :, :, :].rearrange("p g c h -> p (g c h)"), ident_b[:, :],
                                        start=True, stop=True)
                    ins.then_inc(bank.full, 1)

                for s in range(SLOT_COUNT):
                    chunk = s in CHUNK_AT and CHUNK_AT[s][0] in st.parts
                    scores = s in ST_AT and 0 in st.parts
                    if 1 in st.parts:
                        delta(s)
                    if 1 <= s < NF0 and 0 in st.parts:
                        spread(("cw0", s - 1), pick_e0[:, s - 1, :], rows0)
                    maxima = [(m, g) for m in MAX_AT.get(s, ()) for g in range(2)] if 0 in st.parts else []
                    if s == min(MAX_AT) and 0 in st.parts:
                        pe.wait_ge(*qk_packed(i0))
                    if maxima:
                        score_rows(*maxima[0])
                    if chunk:
                        up(s, "g")
                    if maxima:
                        score_rows(*maxima[1])
                    if chunk:
                        up(s, "u")
                    if scores:
                        if ST_AT[s] == 0:
                            pe.wait_ge(*max_packed(i0))
                        score_pair(ST_AT[s], 0)
                    for m, g in maxima[2:]:
                        score_rows(m, g)
                    if 1 in st.parts:
                        layer1_projections(s)
                        for e in range(E1):
                            if s == CW1_AT[e]:
                                spread(("cw1", e), pick_e1[:, e, :], rows1[2 * H:, :])
                    if s >= LAG:
                        down(s)
                    if scores:
                        score_pair(ST_AT[s], 1)
                    if 0 in st.parts:
                        if s == MT_AT:
                            turn_maxima()
                        if s in PV_AT:
                            weigh_values(PV_AT[s])
                        if s in ON_AT:
                            n = ON_AT[s]
                            pe.wait_ge(*use["pv", n].released(st))
                            turn(("on", n), lambda t: heads_out[:, t * P:(t + 1) * P])
                    if 1 in st.parts:
                        if s == LN2_AT:
                            pe.wait_ge(*read_added(i1))
                            turn("oT", lambda t: o_acc[:, t * P:(t + 1) * P])
                        if s == NT_AT:
                            pe.wait_ge(*use["oT"].released(st))
                            turn("nT", lambda t: on1[:, t, :])
                    if s == AT_AT and 0 in st.parts:
                        pe.wait_ge(*use["on", GROUPS - 1].released(st))
                        turn("aT", lambda t: attn[:, t, :])
                    if "start" in st.parts:
                        start_next(s)

                def add_up(name, y, parts, layer, col, last=None):
                    bank = bank_for(name)
                    for t in range(TILES):
                        dst = bank[:, t * P:(t + 1) * P]
                        pe.matmul(dst, y[:, t * P:(t + 1) * P], ident[:, :], start=t == 0, stop=False,
                                  skip_group_check=True)
                        ins = three(dst, cols(parts, t), w(layer, col), start=False,
                                    stop=last is None and t == TILES - 1)
                    if last is not None:
                        pe.wait_ge(*use["y1", E1 - 1].released(st))
                        for t in range(TILES):
                            ins = pe.matmul(bank[:, t * P:(t + 1) * P], last[:, t * P:(t + 1) * P], ident[:, :],
                                            start=False, stop=t == TILES - 1, skip_group_check=True)
                    ins.then_inc(bank.full, 1)

                if 0 in st.parts:
                    pe.wait_ge(*use["aT"].released(st))
                    pe.wait_ge(*use["y0"].released(st))
                    add_up("out0", y0, (ah, al), 0, W0_M)
                if 1 in st.parts:
                    pe.wait_ge(*ye_added(i1))
                    pe.wait_ge(*o_lo(i1))
                    add_up("out1", y_acc, (oh, ol), 1, W1_O, last=ye)
                if "start" in st.parts:
                    pe.wait_ge(*use["cwT0"].released(st))

            run_steps(pe, step)


_INS = ['L0_attn_x', 'L0_attn_Wq', 'L0_attn_bq', 'L0_attn_Wk', 'L0_attn_bk', 'L0_attn_Wv', 'L0_attn_bv',
        'L0_attn_Wm', 'L0_attn_bm', 'L0_ffn_Wr', 'L0_ffn_Wg', 'L0_ffn_Wu', 'L0_ffn_Wd', 'L0_ffn_Sg', 'L0_ffn_Su',
        'L0_ffn_Sd', 'L1_attn_Wq', 'L1_attn_Wk', 'L1_attn_Wv', 'L1_attn_Wbeta', 'L1_attn_Wg', 'L1_attn_Wout',
        'L1_attn_ln_g', 'L1_attn_ln_b', 'L1_ffn_gate_w', 'L1_ffn_w1', 'L1_ffn_w2', 'L1_ffn_w3']


def kernel(**inputs):
    import numpy as _np
    import concourse.bacc as _bacc
    from concourse import mybir as _mybir
    from concourse.bass_utils import run_bass_kernel_spmd as _run

    nc = _bacc.Bacc("TRN2", target_bir_lowering=False, num_devices=1)
    arrays, args = {}, []
    for name in _INS:
        a = _np.ascontiguousarray(inputs[name])
        arrays[f"in_{name}_dram"] = a
        args.append(nc.dram_tensor(f"in_{name}_dram", a.shape, _mybir.dt.from_np(a.dtype), kind="ExternalInput").ap())
    shape = inputs['L0_attn_x'].shape
    args.append(nc.dram_tensor("out_0_dram", shape, _mybir.dt.from_np(_np.dtype("float32")),
                               kind="ExternalOutput").ap())
    two_layer_kernel(nc, *args)
    r = _run(nc, [arrays], core_ids=[0])
    return r.results[0]["out_0_dram"]
```
